# Optimizing a Trainium2 kernel written in Bass

```python
import numpy as np
import jax
import jax.numpy as jnp

def _softmax(x, axis=-1):
    return jax.nn.softmax(x, axis=axis)

def _gelu(x):
    return jax.nn.gelu(x, approximate=True)

def _silu(x):
    return jax.nn.silu(x)

def _sigmoid(x):
    return jax.nn.sigmoid(x)

def _layernorm(x, axis=-1, eps=1e-05):
    m = jnp.mean(x, axis=axis, keepdims=True)
    v = jnp.var(x, axis=axis, keepdims=True)
    return (x - m) / jnp.sqrt(v + eps)

def _scatter_add(tgt, idx, src, axis=0):
    return tgt.at[idx].add(src)

def _segment_sum(src, seg, n):
    return jax.ops.segment_sum(src, seg, n)
kernel_name = 'mk_perceiver_d1_seqx_r4_4d3fb5'

def setup_inputs(seed: int=0):
    np.random.seed(seed)
    _w = jnp.asarray

    def _rec_inputs():
        import jax
        import jax.numpy as jnp
        _rk = jax.random.key(seed)
        x = 7.22e-05 + 1 * jax.random.normal(jax.random.fold_in(_rk, 1), (128, 32, 256), jnp.float32)
        _lenS = 32 - jax.random.randint(jax.random.fold_in(_rk, 7), (128,), 0, max(1, 32 // 4) + 1, jnp.int32)
        _lenS2 = 257 - jax.random.randint(jax.random.fold_in(_rk, 8), (128,), 0, max(1, 257 // 4) + 1, jnp.int32)
        _ctx_1024P = jax.random.normal(jax.random.fold_in(_rk, 11), (128, 16, 256), jnp.float32)
        _ctx_1024c = jax.random.dirichlet(jax.random.fold_in(_rk, 511), 0.3 * jnp.ones((16,), jnp.float32), (128, 257))
        _ctx_1024t = jnp.einsum('bsk,bkd->bsd', _ctx_1024c, _ctx_1024P)
        _ctx_1024t = _ctx_1024t * jax.lax.rsqrt(jnp.mean(jnp.square(_ctx_1024t)) + 1e-12) * 0.953939
        ctx_1024 = 4.13588e-05 + 0.999923 * (_ctx_1024t + 0.3 * jax.random.normal(jax.random.fold_in(_rk, 611), (128, 257, 256), jnp.float32))
        return (x, ctx_1024)
    x, ctx_1024 = _rec_inputs()

    def _L0_xattn_setup():
        import jax, jax.numpy as jnp
        import numpy as np
        H, D_MODEL, D_K, D_V = (16, 256, 64, 64)
        B, S = (4, 512)

        def _xavier(key, shape):
            fan_in, fan_out = (shape[-2], shape[-1])
            limit = jnp.sqrt(6.0 / (fan_in + fan_out))
            return jax.random.uniform(key, shape, jnp.float32, -limit, limit)
        key = jax.random.key(seed)
        kq, kk, kv, kwq, kwk, kwv, kwo = jax.random.split(key, 7)
        return {'Q': jax.random.normal(kq, (B, S, D_MODEL), jnp.float32), 'K': jax.random.normal(kk, (B, S, D_MODEL), jnp.float32), 'V': jax.random.normal(kv, (B, S, D_MODEL), jnp.float32), 'W_Q': _xavier(kwq, (H, D_MODEL, D_K)), 'W_K': _xavier(kwk, (H, D_MODEL, D_K)), 'W_V': _xavier(kwv, (H, D_MODEL, D_V)), 'W_O': _xavier(kwo, (H * D_V, D_MODEL))}
    _L0_xattn_all = _L0_xattn_setup()
    _L0_xattn_in = {k: v for k, v in _L0_xattn_all.items() if k in ('W_Q', 'W_K', 'W_V', 'W_O')}
    del _L0_xattn_all

    def _L0_attn_setup():
        import jax, jax.numpy as jnp
        import numpy as np
        NUM_HEADS = 16
        D_MODEL = 256
        HEAD_DIM = D_MODEL // NUM_HEADS
        NEG_INF = -1000000000.0

        def alibi_bidirectional_bias(num_heads, seq_len, dtype=jnp.float32):
            half = num_heads // 2
            base = 24.0 ** (1.0 / half)
            slopes = (1.0 / base ** jnp.arange(1, half + 1, dtype=dtype))[:, None, None]
            pos = jnp.arange(seq_len)
            rel = (pos[None, :] - pos[:, None]).astype(dtype)
            neg = jnp.full((seq_len, seq_len), NEG_INF, dtype=dtype)
            fwd = slopes * jnp.tril(rel) + jnp.triu(neg, 1)
            bwd = slopes * jnp.triu(-rel) + jnp.tril(neg, -1)
            return jnp.concatenate([fwd, bwd], axis=0)
        key = jax.random.key(seed)
        ks = jax.random.split(key, 9)
        B, S, D = (2, 512, D_MODEL)
        sc = 1.0 / np.sqrt(D)
        inp = {'x': jax.random.normal(ks[0], (B, S, D), dtype=jnp.float32)}
        inp['Wq'] = jax.random.normal(ks[1], (D, D), dtype=jnp.float32) * sc
        inp['bq'] = jnp.zeros((D,), dtype=jnp.float32)
        inp['Wk'] = jax.random.normal(ks[2], (D, D), dtype=jnp.float32) * sc
        inp['bk'] = jnp.zeros((D,), dtype=jnp.float32)
        inp['Wv'] = jax.random.normal(ks[3], (D, D), dtype=jnp.float32) * sc
        inp['bv'] = jnp.zeros((D,), dtype=jnp.float32)
        inp['Wf'] = jax.random.normal(ks[4], (D, D), dtype=jnp.float32) * sc
        inp['bf'] = jnp.zeros((D,), dtype=jnp.float32)
        return inp
    _L0_attn_all = _L0_attn_setup()
    _L0_attn_in = {k: v for k, v in _L0_attn_all.items() if k in ('Wq', 'bq', 'Wk', 'bk', 'Wv', 'bv', 'Wf', 'bf')}
    del _L0_attn_all

    def _L0_ffn_setup():
        import math
        import jax, jax.numpy as jnp
        import numpy as np
        CAPACITY_FACTOR = 1.25
        key = jax.random.key(seed)
        ks = jax.random.split(key, 5)
        B, S, H, F, E = (4, 1024, 256, 256, 32)
        scale_in = 1.0 / math.sqrt(H)
        scale_mid = 1.0 / math.sqrt(F)
        return {'x': jax.random.normal(ks[0], (B, S, H), dtype=jnp.float32), 'w_router': jax.random.normal(ks[1], (H, E), dtype=jnp.float32) * scale_in, 'w_gate': jax.random.normal(ks[2], (E, H, F), dtype=jnp.float32) * scale_in, 'w_up': jax.random.normal(ks[3], (E, H, F), dtype=jnp.float32) * scale_in, 'w_down': jax.random.normal(ks[4], (E, F, H), dtype=jnp.float32) * scale_mid}
    _L0_ffn_all = _L0_ffn_setup()
    _L0_ffn_in = {k: v for k, v in _L0_ffn_all.items() if k in ('w_router', 'w_gate', 'w_up', 'w_down')}
    del _L0_ffn_all
    return {'x': x, 'ctx_1024': ctx_1024, 'L0_xattn_W_Q': _L0_xattn_in['W_Q'], 'L0_xattn_W_K': _L0_xattn_in['W_K'], 'L0_xattn_W_V': _L0_xattn_in['W_V'], 'L0_xattn_W_O': _L0_xattn_in['W_O'], 'L0_attn_Wq': _L0_attn_in['Wq'], 'L0_attn_bq': _L0_attn_in['bq'], 'L0_attn_Wk': _L0_attn_in['Wk'], 'L0_attn_bk': _L0_attn_in['bk'], 'L0_attn_Wv': _L0_attn_in['Wv'], 'L0_attn_bv': _L0_attn_in['bv'], 'L0_attn_Wf': _L0_attn_in['Wf'], 'L0_attn_bf': _L0_attn_in['bf'], 'L0_ffn_w_router': _L0_ffn_in['w_router'], 'L0_ffn_w_gate': _L0_ffn_in['w_gate'], 'L0_ffn_w_up': _L0_ffn_in['w_up'], 'L0_ffn_w_down': _L0_ffn_in['w_down']}

def reference(x, ctx_1024, L0_xattn_W_Q, L0_xattn_W_K, L0_xattn_W_V, L0_xattn_W_O, L0_attn_Wq, L0_attn_bq, L0_attn_Wk, L0_attn_bk, L0_attn_Wv, L0_attn_bv, L0_attn_Wf, L0_attn_bf, L0_ffn_w_router, L0_ffn_w_gate, L0_ffn_w_up, L0_ffn_w_down):
    import jax
    import jax.numpy as jnp

    def _L0_xattn_ref(Q, K, V, W_Q, W_K, W_V, W_O):
        import jax, jax.numpy as jnp
        import numpy as np
        H, D_MODEL, D_K, D_V = (16, 256, 64, 64)
        B, S = (4, 512)

        def _xavier(key, shape):
            fan_in, fan_out = (shape[-2], shape[-1])
            limit = jnp.sqrt(6.0 / (fan_in + fan_out))
            return jax.random.uniform(key, shape, jnp.float32, -limit, limit)
        q = jnp.einsum('bsm,hmk->bhsk', Q, W_Q)
        k = jnp.einsum('bsm,hmk->bhsk', K, W_K)
        v = jnp.einsum('bsm,hmv->bhsv', V, W_V)
        scale = 1.0 / jnp.sqrt(jnp.asarray(q.shape[-1], q.dtype))
        scores = jnp.einsum('bhqk,bhsk->bhqs', q, k) * scale
        attn = jax.nn.softmax(scores, axis=-1)
        heads = jnp.einsum('bhqs,bhsv->bhqv', attn, v)
        concat = jnp.transpose(heads, (0, 2, 1, 3)).reshape(Q.shape[0], Q.shape[1], -1)
        return concat @ W_O

    def _L0_attn_ref(x, Wq, bq, Wk, bk, Wv, bv, Wf, bf):
        import jax, jax.numpy as jnp
        import numpy as np
        NUM_HEADS = 16
        D_MODEL = 256
        HEAD_DIM = D_MODEL // NUM_HEADS
        NEG_INF = -1000000000.0

        def alibi_bidirectional_bias(num_heads, seq_len, dtype=jnp.float32):
            half = num_heads // 2
            base = 24.0 ** (1.0 / half)
            slopes = (1.0 / base ** jnp.arange(1, half + 1, dtype=dtype))[:, None, None]
            pos = jnp.arange(seq_len)
            rel = (pos[None, :] - pos[:, None]).astype(dtype)
            neg = jnp.full((seq_len, seq_len), NEG_INF, dtype=dtype)
            fwd = slopes * jnp.tril(rel) + jnp.triu(neg, 1)
            bwd = slopes * jnp.triu(-rel) + jnp.tril(neg, -1)
            return jnp.concatenate([fwd, bwd], axis=0)
        B, S, D = x.shape
        H, hd = (NUM_HEADS, HEAD_DIM)

        def heads(y):
            return y.reshape(B, S, H, hd).transpose(0, 2, 1, 3)
        q = heads(x @ Wq + bq)
        k = heads(x @ Wk + bk)
        v = heads(x @ Wv + bv)
        bias = alibi_bidirectional_bias(H, S, x.dtype)
        scores = jnp.einsum('bhqd,bhkd->bhqk', q, k) * (1.0 / np.sqrt(hd)) + bias[None]
        attn = jax.nn.softmax(scores, axis=-1)
        out = jnp.einsum('bhqk,bhkd->bhqd', attn, v)
        out = out.transpose(0, 2, 1, 3).reshape(B, S, D)
        return out @ Wf + bf

    def _L0_ffn_ref(x, w_router, w_gate, w_up, w_down):
        import math
        import jax, jax.numpy as jnp
        import numpy as np
        CAPACITY_FACTOR = 1.25
        B, S, H = x.shape
        E = w_gate.shape[0]
        T = B * S
        C = int(math.ceil(CAPACITY_FACTOR * T / E))
        xt = x.reshape(T, H)
        logits = xt @ w_router
        probs = jax.nn.softmax(logits, axis=-1)
        top1 = jnp.argmax(probs, axis=-1)
        gate = jnp.take_along_axis(probs, top1[:, None], axis=1)[:, 0]
        onehot = jax.nn.one_hot(top1, E, dtype=jnp.int32)
        pos = jnp.cumsum(onehot, axis=0)[jnp.arange(T), top1] - 1
        accepted = pos < C
        slot = jnp.where(accepted, top1 * C + pos, E * C)
        buf = jnp.zeros((E * C + 1, H), dtype=x.dtype).at[slot].set(xt)
        buf = buf[:E * C].reshape(E, C, H)
        g = jnp.einsum('ech,ehf->ecf', buf, w_gate)
        u = jnp.einsum('ech,ehf->ecf', buf, w_up)
        y = jnp.einsum('ecf,efh->ech', jax.nn.silu(g) * u, w_down)
        out_tok = y.reshape(E * C, H)[jnp.clip(slot, 0, E * C - 1)]
        out_tok = jnp.where(accepted[:, None], out_tok * gate[:, None], 0.0)
        return (xt + out_tok).reshape(B, S, H)
    x = x + _L0_xattn_ref(_layernorm(x, axis=-1), ctx_1024, ctx_1024, L0_xattn_W_Q, L0_xattn_W_K, L0_xattn_W_V, L0_xattn_W_O)
    x = x + _L0_attn_ref(_layernorm(x, axis=-1), L0_attn_Wq, L0_attn_bq, L0_attn_Wk, L0_attn_bk, L0_attn_Wv, L0_attn_bv, L0_attn_Wf, L0_attn_bf)
    x = x + _L0_ffn_ref(_layernorm(x, axis=-1), L0_ffn_w_router, L0_ffn_w_gate, L0_ffn_w_up, L0_ffn_w_down)
    return x

_drawn_inputs = setup_inputs


def setup_inputs(seed=0):
    import zlib

    import numpy as np

    out = dict(_drawn_inputs(seed))
    spreads = {'L0_attn_bq': (0.0, 0.564),
     'L0_attn_bk': (0.0, 0.8),
     'L0_attn_bv': (0.0, 0.1),
     'L0_attn_bf': (0.0, 0.1)}
    factors = {}
    for name, (base, spread) in spreads.items():
        noise = np.random.default_rng([zlib.crc32(name.encode()), seed]).standard_normal(out[name].shape)
        drawn = base * np.exp(spread * noise) if base else spread * noise
        out[name] = jnp.asarray(drawn.astype(out[name].dtype))
    for name, factor in factors.items():
        out[name] = (out[name] * factor).astype(out[name].dtype)
    return out
```

```python
from contextlib import ExitStack

import numpy as np

import concourse.bass as bass
from concourse import mybir

F32 = mybir.dt.float32
F32R = mybir.dt.float32r
I32 = mybir.dt.int32
U32 = mybir.dt.uint32
ALU = mybir.AluOpType
ACT = mybir.ActivationFunctionType
AX = mybir.AxisListType

P = 128
NB, SQ, D = 128, 32, 256
KC = D // P
T = NB * SQ
LK = 257
LM = LK - 1
H, DK = 16, 64
NP = H // 2
GB = 8
GT = GB * SQ
G = NB // GB
RT = H * SQ // P
HR = P // SQ
NX = 3 * RT
EPS = 1e-5
PASSES = ((0, 0), (0, 1), (1, 0))


def fp(ap):
    return ap.bitcast(F32)


def prepare(nc, ins, wq, wkt, wv, wo, cxt, ident, scratch):
    with ExitStack() as ctx:
        def sb(name, shape, dt=F32):
            return ctx.enter_context(nc.sbuf_tensor(name, shape, dt))

        def sem(name):
            return ctx.enter_context(nc.semaphore(name))

        stage = sb("stage", [P, 4, KC * H * DK])
        x_in = sb("x_in", [P, 2, KC, D])
        stats = sb("stats", [P, 2, KC, 6])
        mean_var = sb("mean_var", [P, 2, KC, 2])
        rstd = sb("rstd", [P, 2, KC, 1])
        half = sb("half", [P, KC, 1])
        xn = sb("xn", [P, 2, KC, D])
        xnt = sb("xnt", [P, 2, 2, KC, GT], F32R)
        cx = sb("c_last", [P, D])
        cxs = sb("cxs", [P, 2, D], F32R)
        turn = [ctx.enter_context(nc.psum_tensor(f"turn{i}", [P, 512], F32)) for i in range(4)]
        wk_ps, x_ps, c_ps = turn[0:2], turn[2], turn[3]

        const_in, cx_in = sem("const_in"), sem("cx_in")
        w_in = [sem(f"w_in{i}") for i in range(4)]
        xld = [sem(f"xld{i}") for i in range(2)]
        xst = [sem(f"xst{i}") for i in range(2)]
        cx_out = sem("cx_out")
        w_hi = sem("w_hi")
        wk_turned, wk_hi, wk_lo = sem("wk_turned"), sem("wk_hi"), sem("wk_lo")
        cx_hi, cx_lo, cx_turned, cxt_hi = sem("cx_hi"), sem("cx_lo"), sem("cx_turned"), sem("cxt_hi")
        half_set, aggregated, passed = sem("half_set"), sem("aggregated"), sem("passed0")
        moments, rstd_done = sem("moments"), sem("rstd_done")
        xn_done, x_turned, xnt_hi, xnt_lo = sem("xn_done"), sem("x_turned"), sem("xnt_hi"), sem("xnt_lo")
        block = ctx.enter_context(nc.Block())
        wview = [stage[:, i, :].rearrange("p (c h k) -> p c h k", c=KC, h=H) for i in range(3)]
        x_rows = ins["x"].rearrange("(g b) s d -> g (b s) d", g=G).rearrange("g (c p) d -> g p c d", p=P)

        started = (*xst, xnt_lo, xn_done)

        @block.sync
        def _(sp):
            for counter in started:
                sp.sem_inc(counter, 1)
            sp.dma_start(ident[:, :], ins["ident"]).then_inc(const_in, 16)
            sp.dma_start(cx[:, :], ins["ctx"][:, LM, :]).then_inc(cx_in, 16)
            for i, name in ((1, "wk"), (0, "wq"), (2, "wv")):
                for c in range(KC):
                    sp.dma_start(wview[i][:, c],
                                 ins[name][:, c * P:(c + 1) * P, :].rearrange("h p k -> p h k")).then_inc(w_in[i], 16)
            sp.dma_start(stage[:, 3, :].rearrange("p (j n) -> p j n", n=D),
                         ins["wo"].rearrange("(j p) n -> p j n", p=P)).then_inc(w_in[3], 16)
            for half_no in range(2):
                sp.wait_ge(cx_hi if half_no == 0 else cx_lo, 1)
                sp.dma_start(scratch["cx"][half_no], fp(cxs[:, half_no, :])).then_inc(cx_out, 16)
            with sp.Fori(0, G // 2) as gg:
                for s in range(2):
                    sp.wait_ge(xnt_lo, 1 + gg * 2 + s + 1)
                    sp.dma_start(scratch["xnt"][bass.ds(gg * 2 + s, 1)].rearrange("g p n -> p (g n)"),
                                 fp(xnt[:, s].rearrange("p a c t -> p (a c t)"))).then_inc(xst[s], 16)
            sp.wait_ge(cx_out, 32)
            for s in range(2):
                sp.wait_ge(xst[s], 1 + 16 * (G // 2))

        @block.gpsimd
        def _(pool):
            pool.memset(half[:, :, :], -0.5).then_inc(half_set, 1)
            pool.wait_ge(half_set, 1)
            with pool.Fori(0, G // 2) as gg:
                for s in range(2):
                    pool.wait_ge(xn_done, 1 + gg * 2)
                    pool.sem_inc(passed, 1)
                    pool.dma_start(x_in[:, s, :, :], x_rows[bass.ds(gg * 2 + s, 1)].rearrange("g p c d -> p (g c) d")).then_inc(xld[s], 16)
                for s in range(2):
                    pool.wait_ge(moments, gg * 2 + s + 1)
                    pool.tensor_tensor(rstd[:, s], mean_var[:, s, :, 1:2], half[:, :, :], ALU.pow).then_inc(rstd_done, 1)

        @block.scalar
        def _(act):
            act.wait_ge(cx_in, 16)
            nc.scalar.activation(cxs[:, 0, :], cx[:, :], ACT.Copy).then_inc(cx_hi, 1)
            act.wait_ge(cx_turned, 1)
            nc.scalar.activation(cxt[:, 0, :, :], c_ps[:, 0:KC * NB], ACT.Copy).then_inc(cxt_hi, 1)
            for p in range(NP):
                act.wait_ge(wk_turned, p + 1)
                nc.scalar.activation(wkt[:, 0, p, :], wk_ps[p % 2][:, 0:D], ACT.Copy).then_inc(wk_hi, 1)
            act.wait_ge(w_in[0], 32)
            nc.scalar.activation(wq[:, 0, :], stage[:, 0, :], ACT.Copy, scale=DK ** -0.5).then_inc(w_hi, 1)
            act.wait_ge(w_in[2], 32)
            nc.scalar.activation(wv[:, 0, :], stage[:, 2, :], ACT.Copy).then_inc(w_hi, 1)
            act.wait_ge(w_in[3], 16)
            nc.scalar.activation(wo[:, 0, :], stage[:, 3, :], ACT.Copy).then_inc(w_hi, 1)
            with act.Fori(0, G // 2) as gg:
                for s in range(2):
                    act.wait_ge(x_turned, gg * 2 + s + 1)
                    act.wait_ge(xst[s], 1 + gg * 16)
                    nc.scalar.activation(xnt[:, s, 0], x_ps[:, :], ACT.Copy).then_inc(xnt_hi, 1)

        @block.vector
        def _(dve):
            dve.wait_ge(cx_hi, 1)
            dve.tensor_tensor(cxs[:, 1, :], cx[:, :], fp(cxs[:, 0, :]), ALU.subtract).then_inc(cx_lo, 1)
            dve.wait_ge(cxt_hi, 1)
            dve.tensor_tensor(cxt[:, 1, :, :].rearrange("p c b -> p (c b)"), c_ps[:, 0:KC * NB],
                              fp(cxt[:, 0, :, :]).rearrange("p c b -> p (c b)"), ALU.subtract).then_inc(cx_lo, 1)
            for p in range(NP):
                dve.wait_ge(wk_hi, p + 1)
                dve.tensor_tensor(wkt[:, 1, p, :], wk_ps[p % 2][:, 0:D], fp(wkt[:, 0, p, :]), ALU.subtract).then_inc(wk_lo, 1)
            for n, (w, i, k) in enumerate(((wq, 0, DK ** -0.5), (wv, 2, 1.0), (wo, 3, 1.0))):
                dve.wait_ge(w_hi, n + 1)
                dve.scalar_tensor_tensor(out=w[:, 1, :], in0=stage[:, i, :], scalar=k, in1=fp(w[:, 0, :]),
                                         op0=ALU.mult, op1=ALU.subtract)
            with dve.Fori(0, G // 2) as gg:
                for s in range(2):
                    dve.wait_ge(xld[s], (gg + 1) * 16)
                    for c in range(KC):
                        ins_ = dve.bn_stats(stats[:, s, c, :], x_in[:, s, c, :])
                    dve.drain()
                    for c in range(KC):
                        ins_ = dve.bn_aggr(mean_var[:, s, c, :], stats[:, s, c, :])
                    ins_.then_inc(aggregated, 1)
                    dve.wait_ge(aggregated, gg * 2 + s + 1)
                    dve.tensor_scalar(mean_var[:, s, :, 1], mean_var[:, s, :, 1], EPS, None, ALU.add).then_inc(moments, 1)
                for s in range(2):
                    dve.wait_ge(rstd_done, gg * 2 + s + 1)
                    for c in range(KC):
                        ins_ = dve.tensor_scalar(xn[:, s, c, :], x_in[:, s, c, :], mean_var[:, s, c, 0:1],
                                                 rstd[:, s, c, :], ALU.subtract, ALU.mult)
                    ins_.then_inc(xn_done, 1)
                for s in range(2):
                    dve.wait_ge(xnt_hi, gg * 2 + s + 1)
                    dve.tensor_tensor(xnt[:, s, 1].rearrange("p c t -> p (c t)"), x_ps[:, :],
                                      fp(xnt[:, s, 0]).rearrange("p c t -> p (c t)"), ALU.subtract).then_inc(xnt_lo, 1)

        @block.tensor
        def _(pe):
            pe.wait_ge(const_in, 16)
            pe.wait_ge(cx_in, 16)
            for c in range(KC):
                mm = pe.transpose(c_ps[:, c * NB:(c + 1) * NB], cx[:, c * P:(c + 1) * P], ident[:, :])
            mm.then_inc(cx_turned, 1)
            pe.wait_ge(w_in[1], 32)
            for p in range(NP):
                if p >= 2:
                    pe.wait_ge(wk_lo, p - 1)
                for c in range(KC):
                    mm = pe.transpose(wk_ps[p % 2][:, c * P:(c + 1) * P], wview[1][:, c, 2 * p:2 * p + 2, :], ident[:, :])
                mm.then_inc(wk_turned, 1)
            with pe.Fori(0, G // 2) as gg:
                for s in range(2):
                    pe.wait_ge(xn_done, 1 + gg * 2 + s + 1)
                    pe.wait_ge(xnt_lo, 1 + gg * 2 + s)
                    for c in range(KC):
                        for t in range(KC):
                            mm = pe.transpose(x_ps[:, c * GT + t * P:c * GT + (t + 1) * P],
                                              xn[:, s, t, c * P:(c + 1) * P], ident[:, :])
                    mm.then_inc(x_turned, 1)


def cross_attention(nc, ins, wq, wkt, wv, wo, cxt, ident, scratch):
    with ExitStack() as ctx:
        def sb(name, shape, dt=F32):
            return ctx.enter_context(nc.sbuf_tensor(name, shape, dt))

        def sem(name):
            return ctx.enter_context(nc.semaphore(name))

        def psum(name):
            return [ctx.enter_context(nc.psum_tensor(f"{name}{i}", [P, 512], F32)) for i in range(2)]

        xnt = sb("g_xnt", [P, 2, KC, GT], F32R)
        qt = sb("qt", [P, 2, 2, GT], F32R)
        qu = sb("qu", [P, 2, KC, GB, H, SQ], F32R)
        craw = sb("craw", [P, 2, KC, D])
        cs = sb("cs", [P, 2, 2, KC, D], F32R)
        ct = sb("ct", [P, 2, KC, LM + 2], F32R)
        prob = sb("prob", [P, 2, RT, LK])
        negmax = sb("negmax", [P, 2, RT])
        rowsum = sb("rowsum", [P, 2, RT])
        rinv = sb("rinv", [P, 2, RT])
        pxh = sb("pxh", [P, RT], F32R)
        px = sb("px", [P, NX])
        pt = sb("pt", [P, 2, KC, 512], F32R)
        xp = sb("xp", [NX, RT, P], F32R)
        cxg = sb("cxg", [NX, GB, D], F32R)
        mask = sb("row_mask", [NX, RT])
        heads = sb("heads", [P, 2, NP, GT], F32R)
        xg = sb("xg", [P, KC, D])

        s_bank, pt_bank, u_bank, m_bank = psum("s_bank"), psum("pt_bank"), psum("u_bank"), psum("m_bank")
        S_N, PT_N, U_N = GB * RT, GB * KC + NP, GB * KC + H
        m_order = [("ct", 0)] + [("q", p) for p in range(NP)]
        for b in range(GB):
            if b >= 1:
                m_order.append(("px", b - 1))
            if b + 1 < GB:
                m_order.append(("ct", b + 1))
        m_order += [("px", GB - 1), ("out", 0), ("out", 1)]
        M_N = len(m_order)
        assert M_N % 2 == PT_N % 2 == U_N % 2 == S_N % 2 == 0
        m_at = {what: n for n, what in enumerate(m_order)}

        def full(g, per, n):
            return (g + 1) * per + n + 1

        def free(g, per, n):
            return g * per + n + 1

        def held(bank, n, like):
            v = bank[n % 2][:, 0:like.free_size()]
            if len(like.shape) == 3:
                v = v.rearrange("p (a b) -> p a b", a=like.shape[1])
            elif len(like.shape) == 4:
                v = v.rearrange("p (a b c) -> p a b c", a=like.shape[1], b=like.shape[2])
            return v

        mask_in, cx_in, x_in, x_out, xnt_in = sem("mask_in"), sem("g_cx_in"), sem("g_x_in"), sem("g_x_out"), sem("g_xnt_in")
        c_in = [sem(f"c_in{i}") for i in range(2)]
        pad_set, passed, passed_sp = sem("pad_set"), sem("passed1"), sem("passed_sp")
        s_full, s_free = sem("s_full"), sem("s_free")
        pt_full, pt_free = sem("pt_full"), sem("pt_free")
        u_full, u_free = sem("u_full"), sem("u_free")
        m_full, m_free = sem("m_full"), sem("m_free")
        s_max, p_scaled, p_inv = sem("s_max"), sem("p_scaled"), sem("p_inv")
        pt_hi, u_hi, m_hi = sem("pt_hi"), sem("u_hi"), sem("m_hi")
        c_hi, c_split, ct_last = sem("c_hi"), sem("c_split"), sem("ct_last")
        px_hi, px_done = sem("px_hi"), sem("px_done")
        block = ctx.enter_context(nc.Block())

        x_rows = ins["x"].rearrange("(g b) s d -> g (b s) d", g=G).rearrange("g (c p) d -> g p c d", p=P)
        x1_rows = scratch["x1"].rearrange("(g c p) d -> g p c d", c=KC, p=P)
        ctx_rows = ins["ctx"].rearrange("b k d -> b (k d)")
        pass

        started = (x_out,)

        @block.sync
        def _(sp):
            for counter in started:
                sp.sem_inc(counter, 1)
            sp.dma_start(mask[:, :], ins["mask"]).then_inc(mask_in, 16)
            with sp.Fori(0, G) as g:
                for b in range(GB):
                    sp.wait_ge(c_split, full(g, GB, b - 2))
                    sp.sem_inc(passed_sp, 1)
                    sp.wait_ge(m_full, full(g, M_N, m_at[("ct", (b - 2) % GB)] - (M_N if b < 2 else 0)))
                    sp.sem_inc(passed_sp, 1)
                    sp.dma_start(craw[:, b % 2, :, :].rearrange("p c d -> p (c d)"),
                                 ctx_rows[bass.ds(g * GB + b, 1), 0:LM * D].rearrange("b (p n) -> (b p) n", p=P)
                                 ).then_inc(c_in[b % 2], 16)
                    if b == 1:
                        sp.wait_ge(m_full, full(g, M_N, m_at[("q", NP - 1)] - M_N))
                        sp.dma_start(fp(xnt[:, :, :, :]).rearrange("p a c t -> p (a c t)"),
                                     scratch["xnt"][bass.ds(g, 1)].rearrange("g p n -> (g p) n")).then_inc(xnt_in, 16)
                        sp.wait_ge(u_full, full(g, U_N, -1))
                        for t, part in enumerate((0, 0, 1)):
                            sp.dma_start(fp(cxg[t * RT:(t + 1) * RT, :, :]),
                                         scratch["cx"][part, bass.ds(g * GB, GB), :].partition_broadcast(RT)
                                         ).then_inc(cx_in, 16)
                        sp.wait_ge(x_out, 1 + g * 16)
                        sp.dma_start(xg[:, :, :], x_rows[bass.ds(g, 1)].rearrange("g p c d -> p (g c) d")).then_inc(x_in, 16)
            sp.wait_ge(x_out, 1 + G * 16)

        @block.gpsimd
        def _(pool):
            pool.memset(fp(ct[:, :, :, LM + 1:LM + 2]), 0.0).then_inc(pad_set, 1)
            pool.sem_inc(c_split, GB)
            with pool.Fori(0, G) as g:
                def split_c(b):
                    s = b % 2
                    pool.wait_ge(c_in[s], (g * (GB // 2) + b // 2 + 1) * 16)
                    pool.wait_ge(u_full, full(g, U_N, H + KC * (b - 2) + 1 if b >= 2 else KC * (b - 2) + 1))
                    pool.sem_inc(passed, 1)
                    pool.tensor_copy(cs[:, s, 0, :, :], craw[:, s, :, :]).then_inc(c_hi, 1)
                    pool.wait_ge(c_hi, g * GB + b + 1)
                    pool.tensor_tensor(cs[:, s, 1, :, :], craw[:, s, :, :], fp(cs[:, s, 0, :, :]), ALU.subtract).then_inc(c_split, 1)

                def last_row(b):
                    pool.wait_ge(s_full, full(g, S_N, RT * b - 1))
                    pool.sem_inc(passed, 1)
                    pool.tensor_copy(ct[:, :, :, LM], fp(cxt[:, :, :, bass.ds(g * GB + b, 1)]).rearrange("p a c b -> p a (c b)")).then_inc(ct_last, 1)

                def last_prob(b):
                    pool.wait_ge(p_scaled, g * GB + b + 1)
                    pool.wait_ge(m_full, full(g, M_N, m_at[("px", (b - 1) % GB)] - (0 if b else M_N)))
                    pool.sem_inc(passed, 1)
                    pool.tensor_copy(pxh[:, :], prob[:, b % 2, :, LM]).then_inc(px_hi, 1)
                    pool.wait_ge(px_hi, g * GB + b + 1)
                    pool.sem_inc(passed, 1)
                    pool.tensor_copy(px[:, 0:RT], fp(pxh[:, :]))
                    pool.tensor_copy(px[:, 2 * RT:3 * RT], fp(pxh[:, :]))
                    pool.tensor_tensor(px[:, RT:2 * RT], prob[:, b % 2, :, LM], fp(pxh[:, :]), ALU.subtract).then_inc(px_done, 1)

                split_c(0)
                last_row(0)
                for b in range(GB):
                    if b + 1 < GB:
                        split_c(b + 1)
                        last_row(b + 1)
                    last_prob(b)

        @block.scalar
        def _(act):
            act.sem_inc(m_free, 2)
            with act.Fori(0, G) as g:
                def high(out, bank, full_sem, per, n, done):
                    act.wait_ge(full_sem, full(g, per, n))
                    nc.scalar.activation(out, held(bank, n, out), ACT.Copy).then_inc(done, 1)

                def ct_high(b):
                    high(ct[:, 0, :, 0:LM], m_bank, m_full, M_N, m_at[("ct", b)], m_hi)

                def exps(b, r):
                    n = RT * b + r
                    act.wait_ge(s_max, g * S_N + n + 1)
                    act.wait_ge(m_full, full(g, M_N, m_at[("px", (b - 2) % GB)] - (0 if b >= 2 else M_N)))
                    nc.scalar.activation(prob[:, b % 2, r, :], s_bank[n % 2][:, 0:LK], ACT.Exp, bias=negmax[:, b % 2, r:r + 1],
                                         accum_out=rowsum[:, b % 2, r:r + 1]).then_inc(s_free, 1)

                ct_high(0)
                for p in range(NP):
                    high(qt[:, p % 2, 0, :], m_bank, m_full, M_N, m_at[("q", p)], m_hi)
                    if p:
                        for s in range(2):
                            high(qu[:, 0, :, :, 2 * p - 2 + s, :], u_bank, u_full, U_N, 2 * p - 2 + s, u_hi)
                for s in range(2):
                    high(qu[:, 0, :, :, H - 2 + s, :], u_bank, u_full, U_N, H - 2 + s, u_hi)

                def p_high(b, c):
                    high(pt[:, 0, c, :], pt_bank, pt_full, PT_N, KC * b + c, pt_hi)

                def u_high(b, c):
                    high(qu[:, 0, c, b, :, :].rearrange("p h q -> p (h q)"), u_bank, u_full, U_N, H + KC * b + c, u_hi)

                for b in range(GB + 1):
                    if b < GB:
                        exps(b, 0)
                        exps(b, 1)
                    if b:
                        p_high(b - 1, 0)
                        p_high(b - 1, 1)
                    if b < GB:
                        exps(b, 2)
                        exps(b, 3)
                    if b + 1 < GB:
                        ct_high(b + 1)
                    if b:
                        u_high(b - 1, 0)
                        u_high(b - 1, 1)
                for p in range(NP):
                    n = GB * KC + p
                    act.wait_ge(pt_full, full(g, PT_N, n))
                    for s in range(2):
                        r = slice(s * DK, (s + 1) * DK)
                        mm = nc.scalar.activation(heads[r, 0, p, :], pt_bank[n % 2][r, s * GT:(s + 1) * GT], ACT.Copy)
                    mm.then_inc(pt_hi, 1)
                act.wait_ge(m_free, free(g, M_N, m_at[("out", 1)]) + 2)
                nc.scalar.dma_start(x1_rows[bass.ds(g, 1)].rearrange("g p c d -> p (g c) d"), xg[:, :, :]).then_inc(x_out, 16)

        @block.vector
        def _(dve):
            dve.sem_inc(s_free, 2)
            dve.sem_inc(pt_free, 2)
            dve.sem_inc(u_free, 2)
            dve.wait_ge(mask_in, 16)
            with dve.Fori(0, G) as g:
                def low(out, hi, bank, n, hi_sem, hi_count, emptied):
                    dve.wait_ge(hi_sem, hi_count)
                    dve.tensor_tensor(out, held(bank, n, out), fp(hi), ALU.subtract).then_inc(emptied, 1)

                def ct_low(b):
                    n = m_at[("ct", b)]
                    low(ct[:, 1, :, 0:LM], ct[:, 0, :, 0:LM], m_bank, n, m_hi, g * (GB + NP) + (NP if b else 0) + b + 1, m_free)

                def maxs(b, r):
                    n = RT * b + r
                    dve.wait_ge(s_full, full(g, S_N, n))
                    dve.tensor_reduce(negmax[:, b % 2, r:r + 1], s_bank[n % 2][:, 0:LK], AX.X, ALU.max, negate=True).then_inc(s_max, 1)

                def scale(b):
                    dve.wait_ge(s_free, free(g, S_N, RT * b + 3) + 2)
                    dve.reciprocal(rinv[:, b % 2, :], rowsum[:, b % 2, :]).then_inc(p_inv, 1)
                    dve.wait_ge(p_inv, g * GB + b + 1)
                    for r in range(RT):
                        op = dve.tensor_scalar(prob[:, b % 2, r, :], prob[:, b % 2, r, :], rinv[:, b % 2, r:r + 1], None, ALU.mult)
                    op.then_inc(p_scaled, 1)

                ct_low(0)
                for p in range(NP):
                    low(qt[:, p % 2, 1, :], qt[:, p % 2, 0, :], m_bank, m_at[("q", p)], m_hi, g * (GB + NP) + p + 2, m_free)
                    if p:
                        for h in (2 * p - 2, 2 * p - 1):
                            low(qu[:, 1, :, :, h, :], qu[:, 0, :, :, h, :], u_bank, h, u_hi, free(g, U_N, h), u_free)
                for h in (H - 2, H - 1):
                    low(qu[:, 1, :, :, h, :], qu[:, 0, :, :, h, :], u_bank, h, u_hi, free(g, U_N, h), u_free)

                def p_low(b, c):
                    n = KC * b + c
                    low(pt[:, 1, c, :], pt[:, 0, c, :], pt_bank, n, pt_hi, free(g, PT_N, n), pt_free)

                def u_low(b, c):
                    n = H + KC * b + c
                    hi, lo = (qu[:, i, c, b, :, :].rearrange("p h q -> p (h q)") for i in range(2))
                    low(lo, hi, u_bank, n, u_hi, free(g, U_N, n), u_free)

                def spread_px(b):
                    n = m_at[("px", b)]
                    dve.wait_ge(m_full, full(g, M_N, n))
                    dve.tensor_tensor(xp[:, :, :], m_bank[n % 2][0:NX, 0:P].unsqueeze(1).broadcast_to([NX, RT, P]),
                                      mask[:, :].unsqueeze(2).broadcast_to([NX, RT, P]), ALU.mult).then_inc(m_free, 1)

                for b in range(GB + 1):
                    if b < GB:
                        maxs(b, 0)
                        maxs(b, 1)
                    if b:
                        p_low(b - 1, 0)
                        p_low(b - 1, 1)
                        spread_px(b - 1)
                    if b < GB:
                        maxs(b, 2)
                        maxs(b, 3)
                    if b + 1 < GB:
                        ct_low(b + 1)
                    if b < GB:
                        scale(b)
                    if b:
                        u_low(b - 1, 0)
                        u_low(b - 1, 1)
                for p in range(NP):
                    n = GB * KC + p
                    dve.wait_ge(pt_hi, free(g, PT_N, n))
                    for s in range(2):
                        r = slice(s * DK, (s + 1) * DK)
                        op = dve.tensor_tensor(heads[r, 1, p, :], pt_bank[n % 2][r, s * GT:(s + 1) * GT],
                                               fp(heads[r, 0, p, :]), ALU.subtract)
                    op.then_inc(pt_free, 1)
                dve.wait_ge(x_in, (g + 1) * 16)
                for t in range(KC):
                    n = m_at[("out", t)]
                    dve.wait_ge(m_full, full(g, M_N, n))
                    dve.tensor_tensor(xg[:, t, :], m_bank[n % 2][:, 0:D], xg[:, t, :], ALU.add).then_inc(m_free, 1)

        @block.tensor
        def _(pe):
            pe.wait_ge(pad_set, 1)
            pe.sem_inc(s_full, S_N)
            pe.sem_inc(pt_full, PT_N)
            pe.sem_inc(u_full, U_N)
            pe.sem_inc(m_full, M_N)
            with pe.Fori(0, G) as g:
                def product(out, terms):
                    for i, (w, m) in enumerate(terms):
                        mm = pe.matmul(out, w, m, start=(i == 0), stop=(i == len(terms) - 1))
                    return mm

                def turn_c(b):
                    n = m_at[("ct", b)]
                    pe.wait_ge(c_in[b % 2], (g * (GB // 2) + b // 2 + 1) * 16)
                    pe.wait_ge(m_free, free(g, M_N, n))
                    for d in range(KC):
                        for c in range(KC):
                            mm = pe.transpose(m_bank[n % 2][:, d * LM + c * P:d * LM + (c + 1) * P],
                                              craw[:, b % 2, c, d * P:(d + 1) * P], ident[:, :])
                    mm.then_inc(m_full, 1)

                def project_q(p):
                    n = m_at[("q", p)]
                    pe.wait_ge(m_free, free(g, M_N, n))
                    if p == 0:
                        pe.wait_ge(xnt_in, (g + 1) * 16)
                    product(m_bank[n % 2][:, 0:GT],
                            [(wq[:, i, c * H * DK + p * P:c * H * DK + (p + 1) * P], xnt[:, j, c, :])
                             for i, j in PASSES for c in range(KC)]).then_inc(m_full, 1)

                def q_to_context(p):
                    pe.wait_ge(m_free, free(g, M_N, m_at[("q", p)]) + 2)
                    for s in range(2):
                        h, r = 2 * p + s, slice(s * DK, (s + 1) * DK)
                        pe.wait_ge(u_free, free(g, U_N, h))
                        for c in range(KC):
                            mm = product(u_bank[h % 2][:, c * GT:(c + 1) * GT],
                                         [(wkt[r, i, p, c * P:(c + 1) * P], qt[r, p % 2, j, :]) for i, j in PASSES])
                        mm.then_inc(u_full, 1)

                def scores(b, r):
                    n = RT * b + r
                    if r == 0:
                        pe.wait_ge(m_free, free(g, M_N, m_at[("ct", b)]) + 2)
                        pe.wait_ge(ct_last, g * GB + b + 1)
                        if b == 0:
                            pe.wait_ge(u_free, free(g, U_N, H - 1) + 2)
                    pe.wait_ge(s_free, free(g, S_N, n))
                    product(s_bank[n % 2][:, 0:LM + 2],
                            [(qu[:, i, c, b, HR * r:HR * (r + 1), :].rearrange("p h q -> p (h q)"), ct[:, j, c, :])
                             for i, j in PASSES for c in range(KC)]).then_inc(s_full, 1)

                def turn_p(b, c):
                    n = KC * b + c
                    pe.wait_ge(p_scaled, g * GB + b + 1)
                    pe.wait_ge(pt_free, free(g, PT_N, n))
                    for r in range(RT):
                        mm = pe.transpose(pt_bank[n % 2][:, r * P:(r + 1) * P], prob[:, b % 2, r, c * P:(c + 1) * P], ident[:, :])
                    mm.then_inc(pt_full, 1)

                def turn_px(b):
                    n = m_at[("px", b)]
                    pe.wait_ge(px_done, g * GB + b + 1)
                    pe.wait_ge(m_free, free(g, M_N, n))
                    pe.transpose(m_bank[n % 2][0:NX, 0:P], px[:, :], ident[:, :]).then_inc(m_full, 1)

                def attend(b, d):
                    n = H + KC * b + d
                    if d == 0:
                        pe.wait_ge(c_split, full(g, GB, b))
                        pe.wait_ge(pt_free, free(g, PT_N, KC * b + 1) + 2)
                        pe.wait_ge(m_free, free(g, M_N, m_at[("px", b)]) + 2)
                        if b == 0:
                            pe.wait_ge(cx_in, (g + 1) * 48)
                    pe.wait_ge(u_free, free(g, U_N, n))
                    dd = slice(d * P, (d + 1) * P)
                    terms = [(cs[:, b % 2, i, c, dd], pt[:, j, c, :]) for i, j in PASSES for c in range(KC)]
                    terms.append((cxg[:, b, dd], xp[:, :, :].rearrange("t r n -> t (r n)")))
                    product(u_bank[n % 2][:, :], terms).then_inc(u_full, 1)

                turn_c(0)
                project_q(0)
                for p in range(NP):
                    if p + 1 < NP:
                        project_q(p + 1)
                    q_to_context(p)
                for b in range(GB + 1):
                    if b < GB:
                        scores(b, 0)
                        scores(b, 1)
                    if b:
                        turn_p(b - 1, 0)
                        turn_p(b - 1, 1)
                        turn_px(b - 1)
                    if b < GB:
                        scores(b, 2)
                        scores(b, 3)
                    if b + 1 < GB:
                        turn_c(b + 1)
                    if b:
                        attend(b - 1, 0)
                        attend(b - 1, 1)
                for p in range(NP):
                    n = GB * KC + p
                    if p == 0:
                        pe.wait_ge(u_free, free(g, U_N, U_N - 1) + 2)
                    pe.wait_ge(pt_free, free(g, PT_N, n))
                    product(pt_bank[n % 2][:, :],
                            [(wv[:, i, c * H * DK + p * P:c * H * DK + (p + 1) * P],
                              qu[:, j, c, :, 2 * p:2 * p + 2, :].rearrange("p b h q -> p h b q"))
                             for i, j in PASSES for c in range(KC)]).then_inc(pt_full, 1)
                pe.wait_ge(pt_free, free(g, PT_N, PT_N - 1) + 2)
                for t in range(KC):
                    n = m_at[("out", t)]
                    pe.wait_ge(m_free, free(g, M_N, n))
                    product(m_bank[n % 2][:, 0:D],
                            [(heads[:, i, p, t * P:(t + 1) * P], wo[:, j, p * D:(p + 1) * D])
                             for i, j in PASSES for p in range(NP)]).then_inc(m_full, 1)


EXPERTS, CAP = 32, 160
HS, HD = 16, D // 16
HC = P // HD
SKIP = float(4 * EXPERTS * CAP)


def self_attention(nc, ins, scratch, gate, slot, ident):
    with ExitStack() as ctx:
        def sb(name, shape, dt=F32):
            return ctx.enter_context(nc.sbuf_tensor(name, shape, dt))

        def sem(name):
            return ctx.enter_context(nc.semaphore(name))

        w_self = sb("w_self", [P, 3, KC, D])
        w_f = sb("w_f", [P, KC, D])
        w_r = sb("w_r", [P, KC, EXPERTS])
        bq = sb("bq_col", [P, KC])
        bk = sb("bk_col", [P, KC])
        bv = sb("bv_col", [P, KC])
        bf = sb("bf_rows", [P, D])
        alibi = sb("alibi_tile", [P, RT, SQ])
        head_mask = sb("head_mask", [P, HC])
        upto = sb("upto", [P, P])
        ones = sb("ones", [P, P])
        rank = sb("rank", [P, EXPERTS])
        zero = sb("zero", [P, 2 * D])
        x1 = sb("x1_tile", [P, KC, D])
        x2 = sb("x2_tile", [P, KC, D])
        z = sb("z_tile", [P, KC, D])
        xn = sb("xn1", [P, KC, D])
        xn2 = sb("xn2", [P, KC, D])
        half = sb("minus_half", [P, KC, 1])
        stats = sb("stats1", [P, KC, 6])
        mv = sb("mean_var1", [P, KC, 2])
        rstd = sb("rstd1", [P, KC, 1])
        stats2 = sb("stats2", [P, KC, 6])
        mv2 = sb("mean_var2", [P, KC, 2])
        rstd2 = sb("rstd2", [P, KC, 1])
        xt = sb("xt", [P, KC, GT])
        xt2 = sb("xt2", [P, KC, GT])
        q_t = sb("q_t", [P, KC, GT])
        k_t = sb("k_t", [P, KC, GT])
        q_bd = sb("q_bd", [P, KC, GB, HC, SQ])
        v_bd = sb("v_bd", [P, KC, HR, KC, P])
        prob = sb("prob_self", [P, KC, HR * RT, SQ])
        negmax = sb("rowmax", [P, KC, HR * RT])
        rsum = sb("rsum", [P, KC, HR * RT])
        rinv = sb("rinv_self", [P, KC, HR * RT])
        p_t = sb("p_t", [P, KC, HR, P])
        o_t = sb("o_t", [P, KC, KC, HR, SQ])
        lmax = sb("lmax", [P, KC])
        nlmax = sb("nlmax", [P, KC])
        expl = sb("expl", [P, KC, EXPERTS])
        esum = sb("esum", [P, KC])
        cand = sb("cand", [P, KC, EXPERTS])
        best = sb("best", [P, KC])
        onehot = sb("onehot", [P, KC, EXPERTS])
        taken = sb("taken", [P, EXPERTS])
        place = sb("place", [P, KC, EXPERTS])
        pos = sb("pos", [P, KC])
        refused = sb("refused", [P, KC])
        slot_f = sb("slot_f", [P, KC])
        slot_s = sb("slot_s", [P, KC], I32)
        gate_r = sb("gate_r", [P, KC])
        kept = sb("kept", [P, KC])
        slot_g = sb("slot_g", [P, KC])

        bank = [ctx.enter_context(nc.psum_tensor(f"bank{i}", [P, 512], F32)) for i in range(8)]
        xt_b, q_b, k_b, v_b = bank[0:4]
        s_b, pt_b = bank[4:6], bank[6:8]
        o_b = ((bank[1], bank[2]), (bank[3], bank[0]))
        f_b, xt2_b, l_b, n_b = bank[4], bank[5], bank[6], bank[7]

        w_in, x_in = sem("w2_in"), sem("x1_in")
        z_out = sem("z_out")
        set_up, wq_scaled, zeroed = sem("set_up"), sem("wq_scaled"), sem("zeroed")
        aggr_ok, var_ok, rstd_ok, xn_ok = (sem(f"ln1_{n}") for n in ("aggr", "var", "rstd", "xn"))
        aggr2_ok, var2_ok, rstd2_ok, xn2_ok = (sem(f"ln2_{n}") for n in ("aggr", "var", "rstd", "xn"))
        xt_full, xt_ok = sem("xt_full"), sem("xt_ok")
        q_full, k_full, v_full = sem("q_full"), sem("k_full"), sem("v_full")
        q_ok, k_ok = sem("q_ok"), sem("k_ok")
        qbd_dve, qbd_pool, vbd_act, vbd_dve = sem("qbd_dve"), sem("qbd_pool"), sem("vbd_act"), sem("vbd_dve")
        sc_full, biased, max_ok, sub_ok, exp_ok, sum_ok, inv_ok, prob_ok = (
            sem(n) for n in ("sc_full", "biased", "max_ok", "sub_ok", "exp_ok", "sum_ok", "inv_ok", "prob_ok"))
        pt_full, pt_ok, o_full = sem("pt2_full"), sem("pt2_ok"), sem("o_full")
        ot_act, ot_dve = sem("ot_act"), sem("ot_dve")
        f_full, xb_ok, x2_ok, z_ok = sem("f_full"), sem("xb_ok"), sem("x2_ok"), sem("z_ok")
        xt2_full, xt2_ok, l_full = sem("xt2_full"), sem("xt2_ok"), sem("l_full")
        step, late, passed = sem("step"), sem("late"), sem("passed2")
        route = sem("route")
        lexp_ok, onehot_ok, n_full, slot_ok, sent, sent_ok = sem("lexp_ok"), sem("onehot_ok"), sem("n_full"), sem("slot_ok"), sem("sent"), sem("sent_ok")
        block = ctx.enter_context(nc.Block())

        def v_block(b, r):
            to = v_bd[r * SQ:(r + 1) * SQ, :, b, r // 2, :].rearrange("p t (h n) -> p t h n", h=HR)
            src = v_b[b * SQ:(b + 1) * SQ, :].rearrange("p (t r h n) -> p t r h n", t=KC, r=RT, h=HR)
            return to[:, :, :, (r % 2) * HD:(r % 2 + 1) * HD], src[:, :, r]

        x1_rows = scratch["x1"].rearrange("(g c p) d -> g p c d", c=KC, p=P)
        z_rows = scratch["z"].rearrange("(g c p) d -> g p c d", c=KC, p=P)
        N_W = 11 + 2 * 2 * KC * HR

        started = (x2_ok, z_ok, xn2_ok, sc_full, o_full, z_out, v_full, qbd_pool, qbd_dve, f_full, l_full, xt_full,
                   pt_full, sent_ok, xt2_full, lexp_ok, ot_dve, ot_act, xt2_ok, slot_ok)

        @block.sync
        def _(sp):
            for counter in started:
                sp.sem_inc(counter, 1)
            for i, name in enumerate(("s_wq", "s_wk", "s_wv")):
                sp.dma_start(w_self[:, i], ins[name].rearrange("(c p) n -> p c n", p=P)).then_inc(w_in, 16)
            sp.dma_start(w_r[:, :, :], ins["w_router"].rearrange("(c p) n -> p c n", p=P)).then_inc(w_in, 16)
            sp.dma_start(bq[:, :], ins["s_bq"].rearrange("(c p) -> p c", p=P), allow_slow_non_contiguous=True).then_inc(w_in, 16)
            sp.dma_start(bk[:, :], ins["s_bk"].rearrange("(c p) -> p c", p=P), allow_slow_non_contiguous=True).then_inc(w_in, 16)
            sp.dma_start(bf[:, :], ins["s_bf"].partition_broadcast(P)).then_inc(w_in, 16)
            for u in range(KC):
                for r in range(2):
                    for h4 in range(HR):
                        h = HR * (2 * u + r) + h4
                        at = h4 * 2 * HD + r * HD
                        sp.dma_start(w_f[at:at + HD, u, :], ins["s_wf"][h * HD:(h + 1) * HD, :]).then_inc(w_in, 16)
                        sp.dma_start(bv[at:at + HD, u:u + 1], ins["s_bv"][h * HD:(h + 1) * HD].unsqueeze(1),
                                     allow_slow_non_contiguous=True).then_inc(w_in, 16)
            sp.dma_start(alibi[:, :, :], ins["alibi"]).then_inc(w_in, 16)
            sp.dma_start(head_mask[:, :], ins["head_mask"]).then_inc(w_in, 16)
            sp.dma_start(upto[:, :], ins["upto"]).then_inc(w_in, 16)
            sp.dma_start(rank[:, :], ins["rank"]).then_inc(w_in, 16)
            sp.wait_ge(set_up, 1)
            rows = scratch["buf"].rearrange("(a p j) d -> a p (j d)", p=P, j=2)
            for a in range(EXPERTS * CAP // (2 * P)):
                sp.dma_start(rows[a], zero[:, :]).then_inc(zeroed, 16)
            with sp.Fori(0, G) as i:
                sp.wait_ge(x2_ok, 1 + i * KC)
                sp.dma_start(x1[:, :, :], x1_rows[bass.ds(i, 1)].rearrange("g p c d -> p (g c) d")).then_inc(x_in, 16)
                sp.wait_ge(z_ok, 1 + i + 1)
                sp.dma_start(z_rows[bass.ds(i, 1)].rearrange("g p c d -> p (g c) d"), z[:, :, :]).then_inc(z_out, 16)
            sp.wait_ge(z_out, 1 + 16 * G)

        @block.gpsimd
        def _(pool):
            pool.memset(zero[:, :], 0.0).then_inc(set_up, 1)
            pool.memset(half[:, :, :], -0.5).then_inc(set_up, 1)
            pool.memset(ones[:, :], 1.0).then_inc(set_up, 1)
            pool.memset(taken[:, :], 0.0).then_inc(set_up, 1)
            pool.memset(v_bd[:, :, :, :, :], 0.0).then_inc(set_up, 1)
            pool.wait_ge(w_in, 16 * N_W)
            pool.wait_ge(set_up, 5)
            with pool.Fori(0, G) as i:
                pool.wait_ge(var_ok, i + 1)
                pool.tensor_tensor(rstd[:, :, :], mv[:, :, 1:2], half[:, :, :], ALU.pow).then_inc(rstd_ok, 1)
                pool.wait_ge(x_in, (i + 1) * 16)
                pool.wait_ge(z_ok, 1 + i)
                pool.wait_ge(xn2_ok, 1 + i)
                pool.tensor_tensor(x2[:, :, :], x1[:, :, :], bf[:, :].unsqueeze(1).broadcast_to([P, KC, D]), ALU.add).then_inc(xb_ok, 1)
                pool.wait_ge(q_ok, (i + 1) * KC)
                pool.wait_ge(sc_full, 1 + i * KC)
                pool.tensor_tensor(q_bd[:, 1], q_t[:, 1, :].rearrange("p (b q) -> p b q", b=GB).unsqueeze(2).broadcast_to([P, GB, HC, SQ]),
                                   head_mask[:, :].unsqueeze(1).unsqueeze(3).broadcast_to([P, GB, HC, SQ]), ALU.mult).then_inc(qbd_pool, 1)
                for t in range(KC):
                    pool.wait_ge(inv_ok, i * KC + t + 1)
                    pool.tensor_tensor(prob[:, t], prob[:, t], rinv[:, t, :].unsqueeze(2).broadcast_to([P, HR * RT, SQ]), ALU.mult).then_inc(prob_ok, 1)
                pool.wait_ge(var2_ok, i + 1)
                pool.tensor_tensor(rstd2[:, :, :], mv2[:, :, 1:2], half[:, :, :], ALU.pow).then_inc(rstd2_ok, 1)
                pool.wait_ge(xn2_ok, 1 + i + 1)
                pool.wait_ge(z_out, 1 + i * 16)
                pool.tensor_tensor(z[:, :, :], x2[:, :, :], xn2[:, :, :], ALU.add).then_inc(z_ok, 1)
                pool.wait_ge(zeroed, 16 * (EXPERTS * CAP // (2 * P)))
                pool.wait_ge(slot_ok, 1 + i + 1)
                pool.sem_inc(passed, 1)
                for t in range(KC):
                    pool.indirect_dma_start(out=scratch["buf"], out_offset=bass.IndirectOffsetOnAxis(ap=slot_s[:, t:t + 1], axis=0),
                                            in_=xn2[:, t, :], in_offset=None, bounds_check=EXPERTS * CAP - 1, oob_is_err=False).then_inc(sent, 16)
                pool.wait_ge(sent, (i + 1) * 16 * KC)
                pool.sem_inc(sent_ok, 1)

        @block.scalar
        def _(act):
            act.wait_ge(w_in, 16 * N_W)
            nc.scalar.activation(w_self[:, 0], w_self[:, 0], ACT.Copy, scale=HD ** -0.5).then_inc(wq_scaled, 1)
            nc.scalar.activation(bq[:, :], bq[:, :], ACT.Copy, scale=HD ** -0.5).then_inc(wq_scaled, 1)
            act.wait_ge(wq_scaled, 2)
            with act.Fori(0, G) as i:
                act.wait_ge(xt_full, 1 + i + 1)
                act.wait_ge(v_full, 1 + i)
                nc.scalar.activation(xt[:, :, :].rearrange("p c t -> p (c t)"), xt_b[:, :], ACT.Copy).then_inc(xt_ok, 1)
                act.wait_ge(q_full, i + 1)
                act.wait_ge(qbd_pool, 1 + i)
                act.wait_ge(qbd_dve, 1 + i)
                for c in range(KC):
                    nc.scalar.activation(q_t[:, c, :], q_b[:, c * GT:(c + 1) * GT], ACT.Identity, bias=bq[:, c:c + 1]).then_inc(q_ok, 1)
                act.wait_ge(k_full, i + 1)
                act.wait_ge(sc_full, 1 + i * KC)
                for c in range(KC):
                    nc.scalar.activation(k_t[:, c, :], k_b[:, c * GT:(c + 1) * GT], ACT.Identity, bias=bk[:, c:c + 1]).then_inc(k_ok, 1)
                act.wait_ge(v_full, 1 + i + 1)
                act.wait_ge(o_full, 1 + i * KC)
                for b in (0, 1):
                    for r in range(RT):
                        op = nc.scalar.activation(*v_block(b, r), ACT.Copy)
                op.then_inc(vbd_act, 1)
                for t in range(KC):
                    act.wait_ge(sub_ok, i * KC + t + 1)
                    nc.scalar.activation(prob[:, t], prob[:, t], ACT.Exp).then_inc(exp_ok, 1)
                for t in range(KC):
                    act.wait_ge(pt_full, 1 + i * KC + t + 1)
                    act.wait_ge(o_full, 1 + i * KC)
                    nc.scalar.activation(p_t[:, t].rearrange("p b n -> p (b n)"), pt_b[t][:, :], ACT.Copy).then_inc(pt_ok, 1)
                for t in range(KC):
                    act.wait_ge(o_full, 1 + i * KC + t + 1)
                    act.wait_ge(f_full, 1 + i)
                    for h in range(HR):
                        r = slice(h * SQ, (h + 1) * SQ)
                        op = nc.scalar.activation(o_t[r, 0, t], o_b[t][0][r, :].rearrange("p (b h q) -> p b h q", b=HR, h=HR)[:, :, h, :],
                                                  ACT.Identity, bias=bv[r, 0:1])
                    op.then_inc(ot_act, 1)
                act.wait_ge(xt2_full, 1 + i + 1)
                act.wait_ge(l_full, 1 + i)
                nc.scalar.activation(xt2[:, :, :].rearrange("p c t -> p (c t)"), xt2_b[:, :], ACT.Copy).then_inc(xt2_ok, 1)
                act.wait_ge(route, i * 6 + 3)
                for t in range(KC):
                    op = nc.scalar.activation(expl[:, t, :], l_b[:, t * EXPERTS:(t + 1) * EXPERTS], ACT.Exp, bias=nlmax[:, t:t + 1], accum_out=esum[:, t:t + 1])
                op.then_inc(lexp_ok, 1)

        @block.vector
        def _(dve):
            dve.wait_ge(w_in, 16 * N_W)
            dve.wait_ge(set_up, 5)
            with dve.Fori(0, G) as i:
                dve.wait_ge(x_in, (i + 1) * 16)
                for c in range(KC):
                    op = dve.bn_stats(stats[:, c, :], x1[:, c, :])
                dve.drain()
                for c in range(KC):
                    op = dve.bn_aggr(mv[:, c, :], stats[:, c, :])
                op.then_inc(aggr_ok, 1)
                dve.wait_ge(aggr_ok, i + 1)
                dve.tensor_scalar(mv[:, :, 1], mv[:, :, 1], EPS, None, ALU.add).then_inc(var_ok, 1)
                dve.wait_ge(rstd_ok, i + 1)
                dve.wait_ge(xt_full, 1 + i)
                for c in range(KC):
                    op = dve.tensor_scalar(xn[:, c, :], x1[:, c, :], mv[:, c, 0:1], rstd[:, c, :], ALU.subtract, ALU.mult)
                op.then_inc(xn_ok, 1)
                dve.wait_ge(q_ok, (i + 1) * KC)
                dve.wait_ge(sc_full, 1 + i * KC)
                dve.tensor_tensor(q_bd[:, 0], q_t[:, 0, :].rearrange("p (b q) -> p b q", b=GB).unsqueeze(2).broadcast_to([P, GB, HC, SQ]),
                                  head_mask[:, :].unsqueeze(1).unsqueeze(3).broadcast_to([P, GB, HC, SQ]), ALU.mult).then_inc(qbd_dve, 1)
                dve.wait_ge(v_full, 1 + i + 1)
                dve.wait_ge(o_full, 1 + i * KC)
                for b in (2, 3):
                    for r in range(RT):
                        op = dve.tensor_copy(*v_block(b, r))
                op.then_inc(vbd_dve, 1)
                for t in range(KC):
                    dve.wait_ge(sc_full, 1 + i * KC + t + 1)
                    dve.wait_ge(pt_full, 1 + i * KC)
                    dve.tensor_tensor(prob[:, t].rearrange("p (b r) k -> p b (r k)", b=HR), s_b[t][:, :].rearrange("p (b n) -> p b n", b=HR),
                                      alibi[:, :, :].rearrange("p r k -> p (r k)").unsqueeze(1).broadcast_to([P, HR, RT * SQ]), ALU.add).then_inc(biased, 1)
                    dve.wait_ge(biased, i * KC + t + 1)
                    dve.tensor_reduce(negmax[:, t, :], prob[:, t], AX.X, ALU.max).then_inc(max_ok, 1)
                    dve.wait_ge(max_ok, i * KC + t + 1)
                    dve.tensor_tensor(prob[:, t], prob[:, t], negmax[:, t, :].unsqueeze(2).broadcast_to([P, HR * RT, SQ]), ALU.subtract).then_inc(sub_ok, 1)
                for t in range(KC):
                    dve.wait_ge(exp_ok, i * KC + t + 1)
                    dve.tensor_reduce(rsum[:, t, :], prob[:, t], AX.X, ALU.add).then_inc(sum_ok, 1)
                    dve.wait_ge(sum_ok, i * KC + t + 1)
                    dve.reciprocal(rinv[:, t, :], rsum[:, t, :]).then_inc(inv_ok, 1)
                for t in range(KC):
                    dve.wait_ge(o_full, 1 + i * KC + t + 1)
                    dve.wait_ge(f_full, 1 + i)
                    for h in range(HR):
                        r = slice(h * SQ, (h + 1) * SQ)
                        op = dve.tensor_scalar(o_t[r, 1, t], o_b[t][1][r, :].rearrange("p (b h q) -> p b h q", b=HR, h=HR)[:, :, h, :],
                                               bv[r, 1:2], None, ALU.add)
                    op.then_inc(ot_dve, 1)
                dve.wait_ge(f_full, 1 + i + 1)
                dve.wait_ge(xb_ok, i + 1)
                for t in range(KC):
                    dve.tensor_tensor(x2[:, t, :], f_b[:, t * D:(t + 1) * D], x2[:, t, :], ALU.add).then_inc(x2_ok, 1)
                dve.wait_ge(x2_ok, 1 + (i + 1) * KC)
                for c in range(KC):
                    op = dve.bn_stats(stats2[:, c, :], x2[:, c, :])
                dve.drain()
                for c in range(KC):
                    op = dve.bn_aggr(mv2[:, c, :], stats2[:, c, :])
                op.then_inc(aggr2_ok, 1)
                dve.wait_ge(aggr2_ok, i + 1)
                dve.tensor_scalar(mv2[:, :, 1], mv2[:, :, 1], EPS, None, ALU.add).then_inc(var2_ok, 1)
                dve.wait_ge(rstd2_ok, i + 1)
                dve.wait_ge(z_ok, 1 + i)
                dve.wait_ge(xt2_full, 1 + i)
                dve.wait_ge(sent_ok, 1 + i)
                for c in range(KC):
                    op = dve.tensor_scalar(xn2[:, c, :], x2[:, c, :], mv2[:, c, 0:1], rstd2[:, c, :], ALU.subtract, ALU.mult)
                op.then_inc(xn2_ok, 1)
                logits = l_b[:, 0:KC * EXPERTS].rearrange("p (t e) -> p t e", t=KC)
                dve.wait_ge(l_full, 1 + i + 1)
                dve.wait_ge(lexp_ok, 1 + i)
                dve.tensor_reduce(lmax[:, :], logits, AX.X, ALU.max).then_inc(route, 1)
                dve.tensor_reduce(nlmax[:, :], logits, AX.X, ALU.max, negate=True).then_inc(route, 1)
                dve.wait_ge(route, i * 6 + 2)
                for t in range(KC):
                    op = dve.scalar_tensor_tensor(out=cand[:, t, :], in0=logits[:, t, :], scalar=lmax[:, t:t + 1], in1=rank[:, :], op0=ALU.is_ge, op1=ALU.mult)
                op.then_inc(route, 1)
                dve.wait_ge(route, i * 6 + 3)
                dve.tensor_reduce(best[:, :], cand[:, :, :], AX.X, ALU.max).then_inc(route, 1)
                dve.wait_ge(route, i * 6 + 4)
                for t in range(KC):
                    op = dve.tensor_scalar(onehot[:, t, :], rank[:, :], best[:, t:t + 1], None, ALU.is_equal)
                op.then_inc(onehot_ok, 1)
                dve.wait_ge(n_full, i + 1)
                for t in range(KC):
                    dve.tensor_tensor(place[:, t, :], n_b[:, t * EXPERTS:(t + 1) * EXPERTS], taken[:, :], ALU.add).then_inc(step, 1)
                    dve.wait_ge(step, i * 4 + 2 * t + 1)
                    dve.tensor_tensor(taken[:, :], n_b[:, (KC + t) * EXPERTS:(KC + t + 1) * EXPERTS], taken[:, :], ALU.add).then_inc(step, 1)
                    dve.wait_ge(step, i * 4 + 2 * t + 2)
                dve.tensor_tensor(place[:, :, :], place[:, :, :], onehot[:, :, :], ALU.mult).then_inc(route, 1)
                dve.wait_ge(route, i * 6 + 5)
                dve.tensor_reduce(pos[:, :], place[:, :, :], AX.X, ALU.add).then_inc(route, 1)
                dve.wait_ge(route, i * 6 + 6)
                dve.tensor_scalar(refused[:, :], pos[:, :], float(CAP), SKIP, ALU.is_gt, ALU.mult).then_inc(late, 1)
                dve.tensor_scalar(kept[:, :], pos[:, :], float(CAP), None, ALU.is_le).then_inc(late, 1)
                dve.tensor_scalar(slot_f[:, :], best[:, :], -float(CAP), float(EXPERTS * CAP - 1), ALU.mult, ALU.add).then_inc(late, 1)
                dve.wait_ge(late, i * 8 + 3)
                dve.tensor_tensor(slot_f[:, :], slot_f[:, :], pos[:, :], ALU.add).then_inc(late, 1)
                dve.wait_ge(late, i * 8 + 4)
                dve.tensor_tensor(slot_f[:, :], slot_f[:, :], refused[:, :], ALU.add).then_inc(late, 1)
                dve.wait_ge(late, i * 8 + 5)
                dve.wait_ge(sent_ok, 1 + i)
                dve.tensor_copy(slot_s[:, :], slot_f[:, :]).then_inc(slot_ok, 1)
                dve.tensor_scalar(slot_g[:, :], slot_f[:, :], float(EXPERTS * CAP - 1), None, ALU.min).then_inc(late, 1)
                dve.wait_ge(lexp_ok, 1 + i + 1)
                dve.reciprocal(gate_r[:, :], esum[:, :]).then_inc(late, 1)
                dve.wait_ge(late, i * 8 + 7)
                dve.tensor_copy(slot[:, bass.ds(i * KC, KC)], slot_g[:, :])
                dve.tensor_tensor(gate[:, bass.ds(i * KC, KC)], gate_r[:, :], kept[:, :], ALU.mult).then_inc(late, 1)

        @block.tensor
        def _(pe):
            pe.wait_ge(w_in, 16 * N_W)
            pe.wait_ge(set_up, 5)
            pe.wait_ge(wq_scaled, 2)
            with pe.Fori(0, G) as i:
                def turn(out, x):
                    for c in range(KC):
                        for t in range(KC):
                            mm = pe.transpose(out[:, c * GT + t * P:c * GT + (t + 1) * P], x[:, t, c * P:(c + 1) * P], ident[:, :])
                    return mm
                pe.wait_ge(xn_ok, i + 1)
                pe.wait_ge(ot_dve, 1 + i * KC)
                turn(xt_b, xn).then_inc(xt_full, 1)
                pe.wait_ge(xt_ok, i + 1)
                pe.wait_ge(ot_act, 1 + i * KC)
                for w, out, done in ((0, q_b, q_full), (1, k_b, k_full)):
                    for c in range(KC):
                        for kc in range(KC):
                            mm = pe.matmul(out[:, c * GT:(c + 1) * GT], w_self[:, w, kc, c * P:(c + 1) * P], xt[:, kc, :], start=(kc == 0), stop=(kc == KC - 1))
                    mm.then_inc(done, 1)
                for t in range(KC):
                    for kc in range(KC):
                        mm = pe.matmul(v_b[:, t * D:(t + 1) * D], xt[:, kc, t * P:(t + 1) * P], w_self[:, 2, kc, :], start=(kc == 0), stop=(kc == KC - 1))
                mm.then_inc(v_full, 1)
                pe.wait_ge(k_ok, (i + 1) * KC)
                pe.wait_ge(qbd_dve, 1 + i + 1)
                pe.wait_ge(qbd_pool, 1 + i + 1)
                pe.wait_ge(x2_ok, 1 + i * KC)
                pe.wait_ge(xt2_ok, 1 + i)
                for t in range(KC):
                    for b in range(HR):
                        for r in range(RT):
                            at = (b * RT + r) * SQ
                            g = t * HR + b
                            mm = pe.matmul(s_b[t][:, at:at + SQ], q_bd[:, r // 2, g, HR * (r % 2):HR * (r % 2 + 1), :].rearrange("p h q -> p (h q)"),
                                           k_t[:, r // 2, g * SQ:(g + 1) * SQ], start=True, stop=True)
                    mm.then_inc(sc_full, 1)
                pe.wait_ge(slot_ok, 1 + i)
                pe.wait_ge(lexp_ok, 1 + i)
                for t in range(KC):
                    pe.wait_ge(prob_ok, i * KC + t + 1)
                    for b in range(HR):
                        mm = pe.transpose(pt_b[t][:, b * P:(b + 1) * P], prob[:, t, b * RT:(b + 1) * RT, :].rearrange("p r k -> p (r k)"), ident[:, :])
                    mm.then_inc(pt_full, 1)
                pe.wait_ge(vbd_act, i + 1)
                pe.wait_ge(vbd_dve, i + 1)
                for t in range(KC):
                    pe.wait_ge(pt_ok, i * KC + t + 1)
                    for u in range(KC):
                        for b in range(HR):
                            mm = pe.matmul(o_b[t][u][:, b * P:(b + 1) * P], v_bd[:, t, b, u, :], p_t[:, t, b, :], start=True, stop=True)
                    mm.then_inc(o_full, 1)
                for t in range(KC):
                    pe.wait_ge(ot_act, 1 + i * KC + t + 1)
                    pe.wait_ge(ot_dve, 1 + i * KC + t + 1)
                    pe.wait_ge(biased, (i + 1) * KC)
                    for u in range(KC):
                        mm = pe.matmul(f_b[:, t * D:(t + 1) * D], o_t[:, u, t].rearrange("p b q -> p (b q)"), w_f[:, u, :], start=(u == 0), stop=(u == KC - 1))
                mm.then_inc(f_full, 1)
                pe.wait_ge(xn2_ok, 1 + i + 1)
                turn(xt2_b, xn2).then_inc(xt2_full, 1)
                pe.wait_ge(xt2_ok, 1 + i + 1)
                for t in range(KC):
                    for kc in range(KC):
                        mm = pe.matmul(l_b[:, t * EXPERTS:(t + 1) * EXPERTS], xt2[:, kc, t * P:(t + 1) * P], w_r[:, kc, :], start=(kc == 0), stop=(kc == KC - 1))
                mm.then_inc(l_full, 1)
                pe.wait_ge(onehot_ok, i + 1)
                for j, w in enumerate((upto, ones)):
                    for t in range(KC):
                        at = (j * KC + t) * EXPERTS
                        mm = pe.matmul(n_b[:, at:at + EXPERTS], w[:, :], onehot[:, t, :], start=True, stop=True)
                mm.then_inc(n_full, 1)


def experts(nc, ins, scratch, gate, slot, ident, out):
    with ExitStack() as ctx:
        def sb(name, shape, dt=F32):
            return ctx.enter_context(nc.sbuf_tensor(name, shape, dt))

        def sem(name):
            return ctx.enter_context(nc.semaphore(name))

        NS = 2
        C2 = CAP - P
        w = [sb(f"w_expert{n}", [P, NS, KC, D]) for n in range(3)]
        rows = sb("rows", [P, NS, 2, D])
        bt = sb("bt", [P, NS, KC, CAP])
        ex = sb("ex", [P, NS, KC, CAP])
        act_t = sb("act_t", [P, NS, KC, CAP])
        y = sb("y", [P, NS, 2, D])
        z = sb("z_in", [P, NS, KC, D])
        yt = sb("y_rows", [P, NS, KC, D])
        o = sb("o_rows", [P, NS, KC, D])
        idx = sb("idx", [P, NS, KC], I32)
        gcol = sb("gcol", [P, NS, KC])
        idx_ok, gc_ok, passed = sem("idx_ok"), sem("gc_ok"), sem("passed3")
        bank = [ctx.enter_context(nc.psum_tensor(f"ebank{i}", [P, 512], F32)) for i in range(8)]
        bt_b, g_b, u_b, y_b = bank[0:2], bank[2:4], bank[4:6], bank[6:8]
        w_in = [sem(f"we_in{s}") for s in range(NS)]
        r_in = [sem(f"rows_in{s}") for s in range(NS)]
        y_out = [sem(f"y_out{s}") for s in range(NS)]
        z_in = [sem(f"z_in{s}") for s in range(NS)]
        y_in = [sem(f"yr_in{s}") for s in range(NS)]
        o_out = [sem(f"o_out{s}") for s in range(NS)]
        bt_full, bt_ok, gu_full, ex_ok, plus, inv, gate_ok, act_ok, y_full, y_ok, o_ok = (
            sem(n) for n in ("bt_full", "bt_ok", "gu_full", "ex_ok", "plus", "inv", "gated", "act_ok", "y_full", "y_ok", "o_ok"))
        block = ctx.enter_context(nc.Block())
        NE = EXPERTS // NS
        z_rows = scratch["z"].rearrange("(g c p) d -> g p c d", c=KC, p=P)
        o_rows = out.rearrange("(g b) s d -> g (b s) d", g=G).rearrange("g (c p) d -> g p c d", p=P)
        buf = scratch["buf"].rearrange("(e c) d -> e c d", c=CAP)
        yd = scratch["y"].rearrange("(e c) d -> e c d", c=CAP)

        started = (y_full, o_ok, *y_out, *o_out, y_ok)

        @block.sync
        def _(sp):
            for counter in started:
                sp.sem_inc(counter, 1)
            with sp.Fori(0, NE) as i:
                for s in range(NS):
                    e = i * NS + s
                    sp.wait_ge(y_full, 1 + i * NS)
                    for n, name in enumerate(("w_gate", "w_up", "w_down")):
                        sp.dma_start(w[n][:, s].rearrange("p c n -> p (c n)"),
                                     ins[name][bass.ds(e, 1)].rearrange("e (p c) n -> (e p) (c n)", c=KC)).then_inc(w_in[s], 16)
                    sp.dma_start(rows[:, s, 0, :], buf[bass.ds(e, 1), 0:P, :].rearrange("e c d -> (e c) d")).then_inc(r_in[s], 16)
                    sp.dma_start(rows[0:C2, s, 1, :], buf[bass.ds(e, 1), P:CAP, :].rearrange("e c d -> (e c) d")).then_inc(r_in[s], 16)
            for s in range(NS):
                sp.wait_ge(y_out[s], 1 + 32 * NE)
            with sp.Fori(0, G // NS) as i:
                for s in range(NS):
                    g = i * NS + s
                    sp.wait_ge(o_ok, 1 + i * NS)
                    sp.dma_start(z[:, s], z_rows[bass.ds(g, 1)].rearrange("g p c d -> p (g c) d")).then_inc(z_in[s], 16)
                for s in range(NS):
                    g = i * NS + s
                    sp.wait_ge(o_ok, 1 + g + 1)
                    sp.dma_start(o_rows[bass.ds(g, 1)].rearrange("g p c d -> p (g c) d"), o[:, s]).then_inc(o_out[s], 16)
            for s in range(NS):
                sp.wait_ge(o_out[s], 1 + 16 * (G // NS))

        @block.gpsimd
        def _(pool):
            for s in range(NS):
                pool.wait_ge(y_out[s], 1 + 32 * NE)
            with pool.Fori(0, G // NS) as i:
                for s in range(NS):
                    g = i * NS + s
                    pool.wait_ge(o_ok, 1 + i * NS)
                    for t in range(KC):
                        pool.tensor_copy(idx[:, s, t:t + 1], slot[:, bass.ds(g * KC + t, 1)]).then_inc(idx_ok, 1)
                        pool.wait_ge(idx_ok, g * KC + t + 1)
                        pool.sem_inc(passed, 1)
                        pool.indirect_dma_start(out=yt[:, s, t, :], out_offset=None, in_=scratch["y"],
                                                in_offset=bass.IndirectOffsetOnAxis(ap=idx[:, s, t:t + 1], axis=0),
                                                bounds_check=EXPERTS * CAP - 1, oob_is_err=False).then_inc(y_in[s], 16)

        @block.scalar
        def _(act):
            with act.Fori(0, NE) as i:
                for s in range(NS):
                    e = i * NS + s
                    act.wait_ge(bt_full, e + 1)
                    nc.scalar.activation(bt[:, s].rearrange("p c n -> p (c n)"), bt_b[s][:, 0:KC * CAP], ACT.Copy).then_inc(bt_ok, 1)
                for s in range(NS):
                    e = i * NS + s
                    act.wait_ge(gu_full, e + 1)
                    nc.scalar.activation(ex[:, s].rearrange("p c n -> p (c n)"), g_b[s][:, 0:KC * CAP], ACT.Exp, scale=-1.0).then_inc(ex_ok, 1)
                for s in range(NS):
                    e = i * NS + s
                    act.wait_ge(y_full, 1 + e + 1)
                    act.wait_ge(y_out[s], 1 + i * 32)
                    nc.scalar.activation(y[:, s, 0, :], y_b[s][:, 0:D], ACT.Copy)
                    nc.scalar.activation(y[0:C2, s, 1, :], y_b[s][0:C2, D:2 * D], ACT.Copy).then_inc(y_ok, 1)
                    act.wait_ge(y_ok, 1 + e + 1)
                    nc.scalar.dma_start(yd[bass.ds(e, 1), 0:P, :].rearrange("e c d -> (e c) d"), y[:, s, 0, :]).then_inc(y_out[s], 16)
                    nc.scalar.dma_start(yd[bass.ds(e, 1), P:CAP, :].rearrange("e c d -> (e c) d"), y[0:C2, s, 1, :]).then_inc(y_out[s], 16)

        @block.vector
        def _(dve):
            with dve.Fori(0, NE) as i:
                for s in range(NS):
                    e = i * NS + s
                    dve.wait_ge(ex_ok, e + 1)
                    dve.tensor_scalar(ex[:, s], ex[:, s], 1.0, None, ALU.add).then_inc(plus, 1)
                    dve.wait_ge(plus, e + 1)
                    dve.reciprocal(ex[:, s], ex[:, s]).then_inc(inv, 1)
                    dve.wait_ge(inv, e + 1)
                    dve.tensor_tensor(ex[:, s], g_b[s][:, 0:KC * CAP].rearrange("p (c n) -> p c n", c=KC), ex[:, s], ALU.mult).then_inc(gate_ok, 1)
                    dve.wait_ge(gate_ok, e + 1)
                    dve.tensor_tensor(act_t[:, s], u_b[s][:, 0:KC * CAP].rearrange("p (c n) -> p c n", c=KC), ex[:, s], ALU.mult).then_inc(act_ok, 1)
            with dve.Fori(0, G // NS) as i:
                for s in range(NS):
                    g = i * NS + s
                    dve.wait_ge(z_in[s], (i + 1) * 16)
                    dve.wait_ge(y_in[s], (i + 1) * 32)
                    dve.wait_ge(o_out[s], 1 + i * 16)
                    for t in range(KC):
                        dve.tensor_copy(gcol[:, s, t:t + 1], gate[:, bass.ds(g * KC + t, 1)]).then_inc(gc_ok, 1)
                    dve.wait_ge(gc_ok, (g + 1) * KC)
                    for t in range(KC):
                        op = dve.scalar_tensor_tensor(out=o[:, s, t, :], in0=yt[:, s, t, :], scalar=gcol[:, s, t:t + 1],
                                                      in1=z[:, s, t, :], op0=ALU.mult, op1=ALU.add)
                    op.then_inc(o_ok, 1)

        @block.tensor
        def _(pe):
            with pe.Fori(0, NE) as i:
                for s in range(NS):
                    e = i * NS + s
                    pe.wait_ge(r_in[s], (i + 1) * 32)
                    for c in range(KC):
                        pe.transpose(bt_b[s][:, c * CAP:c * CAP + P], rows[:, s, 0, c:D:KC], ident[:, :])
                        mm = pe.transpose(bt_b[s][:, c * CAP + P:(c + 1) * CAP], rows[0:C2, s, 1, c:D:KC], ident[0:C2, 0:C2])
                    mm.then_inc(bt_full, 1)
                for s in range(NS):
                    e = i * NS + s
                    pe.wait_ge(w_in[s], (i + 1) * 48)
                    pe.wait_ge(bt_ok, e + 1)
                    for n, b in ((0, g_b), (1, u_b)):
                        for f in range(KC):
                            for c in range(KC):
                                mm = pe.matmul(b[s][:, f * CAP:(f + 1) * CAP], w[n][:, s, c, f:D:KC], bt[:, s, c, :], start=(c == 0), stop=(c == KC - 1))
                    mm.then_inc(gu_full, 1)
                for s in range(NS):
                    e = i * NS + s
                    pe.wait_ge(act_ok, e + 1)
                    pe.wait_ge(y_ok, 1 + i * NS)
                    for f in range(KC):
                        pe.matmul(y_b[s][:, 0:D], act_t[:, s, f, 0:P], w[2][:, s, f, :], start=(f == 0), stop=(f == KC - 1))
                    for f in range(KC):
                        mm = pe.matmul(y_b[s][0:C2, D:2 * D], act_t[:, s, f, P:CAP], w[2][:, s, f, :], start=(f == 0), stop=(f == KC - 1))
                    mm.then_inc(y_full, 1)


def cross_weights(nc, ctx):
    def sb(name, shape, dt=F32R):
        return ctx.enter_context(nc.sbuf_tensor(name, shape, dt))

    return dict(wq=sb("w_q", [P, 2, KC * H * DK]), wkt=sb("w_kt", [P, 2, NP, D]), wv=sb("w_v", [P, 2, KC * H * DK]),
                wo=sb("w_o", [P, 2, NP * D]), cxt=sb("c_last_t", [P, 2, KC, NB]))


def constants():
    row = np.arange(NX)
    h4, q = np.divmod(np.arange(P), SQ)
    head = HR * np.arange(RT)[None, :] + h4[:, None]
    half = HS // 2
    base = np.float32(24.0 ** (1.0 / half))
    slopes = (np.float32(1.0) / base ** np.arange(1, half + 1, dtype=np.float32)).astype(np.float32)
    rel = (np.arange(SQ)[None, :] - q[:, None]).astype(np.float32)[:, None, :]
    slope = slopes[head % half][:, :, None]
    far = np.float32(-1e9)
    alibi = np.where((head < half)[:, :, None], np.where(rel <= 0, slope * rel, far), np.where(rel >= 0, -slope * rel, far))
    return {"ident": np.eye(P, dtype=np.float32),
            "mask": (row[:, None] % RT == np.arange(RT)[None, :]).astype(np.float32),
            "alibi": alibi.astype(np.float32),
            "head_mask": (np.arange(P)[:, None] // HD == np.arange(HC)[None, :]).astype(np.float32),
            "upto": np.triu(np.ones((P, P), np.float32)),
            "rank": np.tile(EXPERTS - np.arange(EXPERTS, dtype=np.float32), (P, 1))}


def perceiver(nc, ins, out):
    scratch = {"xnt": nc.dram_tensor("xnt_d", (G, P, 2 * KC * GT), F32, kind="Internal").ap(),
               "cx": nc.dram_tensor("cx_d", (2, NB, D), F32, kind="Internal").ap(),
               "x1": nc.dram_tensor("x1_d", (T, D), F32, kind="Internal").ap(),
               "z": nc.dram_tensor("z_d", (T, D), F32, kind="Internal").ap(),
               "buf": nc.dram_tensor("buf_d", (EXPERTS * CAP, D), F32, kind="Internal").ap(),
               "y": nc.dram_tensor("y_d", (EXPERTS * CAP, D), F32, kind="Internal").ap()}
    with ExitStack() as ctx:
        ident = ctx.enter_context(nc.sbuf_tensor("identity", [P, P], F32))
        gate = ctx.enter_context(nc.sbuf_tensor("gate", [P, T // P], F32))
        slot = ctx.enter_context(nc.sbuf_tensor("slot", [P, T // P], I32))
        with ExitStack() as first:
            weights = cross_weights(nc, first)
            prepare(nc, ins, scratch=scratch, ident=ident, **weights)
            cross_attention(nc, ins, scratch=scratch, ident=ident, **weights)
        self_attention(nc, ins, scratch, gate, slot, ident)
        experts(nc, ins, scratch, gate, slot, ident, out)


NAMES = {"x": "x", "ctx_1024": "ctx", "L0_xattn_W_Q": "wq", "L0_xattn_W_K": "wk", "L0_xattn_W_V": "wv", "L0_xattn_W_O": "wo",
         "L0_attn_Wq": "s_wq", "L0_attn_bq": "s_bq", "L0_attn_Wk": "s_wk", "L0_attn_bk": "s_bk", "L0_attn_Wv": "s_wv",
         "L0_attn_bv": "s_bv", "L0_attn_Wf": "s_wf", "L0_attn_bf": "s_bf", "L0_ffn_w_router": "w_router",
         "L0_ffn_w_gate": "w_gate", "L0_ffn_w_up": "w_up", "L0_ffn_w_down": "w_down"}


def kernel(**inputs):
    import concourse.bacc as bacc
    from concourse.bass_utils import run_bass_kernel_spmd

    nc = bacc.Bacc("TRN2", target_bir_lowering=False, num_devices=1)
    arrays = {NAMES[name]: np.ascontiguousarray(inputs[name]) for name in NAMES}
    arrays.update(constants())
    ins = {name: nc.dram_tensor(f"in_{name}", a.shape, mybir.dt.from_np(a.dtype), kind="ExternalInput").ap()
           for name, a in arrays.items()}
    out = nc.dram_tensor("out", (NB, SQ, D), F32, kind="ExternalOutput").ap()
    perceiver(nc, ins, out)
    r = run_bass_kernel_spmd(nc, [{f"in_{name}": a for name, a in arrays.items()}], core_ids=[0])
    return r.results[0]["out"]
```

```python
from contextlib import ExitStack

import numpy as np

import concourse.bass as bass
from concourse import mybir

F32 = mybir.dt.float32
F32R = mybir.dt.float32r
I32 = mybir.dt.int32
U32 = mybir.dt.uint32
ALU = mybir.AluOpType
ACT = mybir.ActivationFunctionType
AX = mybir.AxisListType

P = 128
NB, SQ, D = 128, 32, 256
KC = D // P
T = NB * SQ
LK = 257
LM = LK - 1
H, DK = 16, 64
NP = H // 2
GB = 8
GT = GB * SQ
G = NB // GB
RT = H * SQ // P
HR = P // SQ
NX = 3 * RT
ZR = 8
EPS = 1e-5
PASSES = ((0, 0), (0, 1), (1, 0))


def fp(ap):
    return ap.bitcast(F32)


def prepare(nc, ins, wq, wkt, wv, wo, cxt, ident, scratch):
    with ExitStack() as ctx:
        def sb(name, shape, dt=F32):
            return ctx.enter_context(nc.sbuf_tensor(name, shape, dt))

        def sem(name):
            return ctx.enter_context(nc.semaphore(name))

        stage = sb("stage", [P, 4, KC * H * DK])
        x_in = sb("x_in", [P, 2, KC, D])
        stats = sb("stats", [P, 2, KC, 6])
        mean_var = sb("mean_var", [P, 2, KC, 2])
        rstd = sb("rstd", [P, 2, KC, 1])
        half = sb("half", [P, KC, 1])
        xn = sb("xn", [P, 2, KC, D])
        xnt = sb("xnt", [P, 2, 2, KC, GT], F32R)
        cx = sb("c_last", [P, D])
        cxs = sb("cxs", [P, 2, D], F32R)
        turn = [ctx.enter_context(nc.psum_tensor(f"turn{i}", [P, 512], F32)) for i in range(4)]
        wk_ps, x_ps, c_ps = turn[0:2], turn[2], turn[3]

        const_in, cx_in = sem("const_in"), sem("cx_in")
        w_in = [sem(f"w_in{i}") for i in range(4)]
        xld = [sem(f"xld{i}") for i in range(2)]
        xst = [sem(f"xst{i}") for i in range(2)]
        cx_out = sem("cx_out")
        w_hi = sem("w_hi")
        wk_turned, wk_hi, wk_lo = sem("wk_turned"), sem("wk_hi"), sem("wk_lo")
        cx_hi, cx_lo, cx_turned, cxt_hi = sem("cx_hi"), sem("cx_lo"), sem("cx_turned"), sem("cxt_hi")
        half_set, aggregated, passed = sem("half_set"), sem("aggregated"), sem("passed0")
        moments, rstd_done = sem("moments"), sem("rstd_done")
        xn_done, x_turned, xnt_hi, xnt_lo = sem("xn_done"), sem("x_turned"), sem("xnt_hi"), sem("xnt_lo")
        block = ctx.enter_context(nc.Block())
        wview = [stage[:, i, :].rearrange("p (c h k) -> p c h k", c=KC, h=H) for i in range(3)]
        x_rows = ins["x"].rearrange("(g b) s d -> g (b s) d", g=G).rearrange("g (c p) d -> g p c d", p=P)

        started = (*xst, xnt_lo, xn_done)

        @block.sync
        def _(sp):
            for counter in started:
                sp.sem_inc(counter, 1)
            sp.dma_start(ident[:, :], ins["ident"]).then_inc(const_in, 16)
            sp.dma_start(cx[:, :], ins["ctx"][:, LM, :]).then_inc(cx_in, 16)
            for i, name in ((1, "wk"), (0, "wq"), (2, "wv")):
                for c in range(KC):
                    sp.dma_start(wview[i][:, c],
                                 ins[name][:, c * P:(c + 1) * P, :].rearrange("h p k -> p h k")).then_inc(w_in[i], 16)
            sp.dma_start(stage[:, 3, :].rearrange("p (j n) -> p j n", n=D),
                         ins["wo"].rearrange("(j p) n -> p j n", p=P)).then_inc(w_in[3], 16)
            for half_no in range(2):
                sp.wait_ge(cx_hi if half_no == 0 else cx_lo, 1)
                sp.dma_start(scratch["cx"][half_no], fp(cxs[:, half_no, :])).then_inc(cx_out, 16)
            with sp.Fori(0, G // 2) as gg:
                for s in range(2):
                    sp.wait_ge(xnt_lo, 1 + gg * 2 + s + 1)
                    sp.dma_start(scratch["xnt"][bass.ds(gg * 2 + s, 1)].rearrange("g p n -> p (g n)"),
                                 fp(xnt[:, s].rearrange("p a c t -> p (a c t)"))).then_inc(xst[s], 16)
            sp.wait_ge(cx_out, 32)
            for s in range(2):
                sp.wait_ge(xst[s], 1 + 16 * (G // 2))

        @block.gpsimd
        def _(pool):
            pool.memset(half[:, :, :], -0.5).then_inc(half_set, 1)
            pool.wait_ge(half_set, 1)
            with pool.Fori(0, G // 2) as gg:
                for s in range(2):
                    pool.wait_ge(xn_done, 1 + gg * 2)
                    pool.sem_inc(passed, 1)
                    pool.dma_start(x_in[:, s, :, :], x_rows[bass.ds(gg * 2 + s, 1)].rearrange("g p c d -> p (g c) d")).then_inc(xld[s], 16)
                for s in range(2):
                    pool.wait_ge(moments, gg * 2 + s + 1)
                    pool.tensor_tensor(rstd[:, s], mean_var[:, s, :, 1:2], half[:, :, :], ALU.pow).then_inc(rstd_done, 1)

        @block.scalar
        def _(act):
            act.wait_ge(cx_in, 16)
            nc.scalar.activation(cxs[:, 0, :], cx[:, :], ACT.Copy).then_inc(cx_hi, 1)
            act.wait_ge(cx_turned, 1)
            nc.scalar.activation(cxt[:, 0, :, :], c_ps[:, 0:KC * NB], ACT.Copy).then_inc(cxt_hi, 1)
            for p in range(NP):
                act.wait_ge(wk_turned, p + 1)
                nc.scalar.activation(wkt[:, 0, p, :], wk_ps[p % 2][:, 0:D], ACT.Copy).then_inc(wk_hi, 1)
            act.wait_ge(w_in[0], 32)
            nc.scalar.activation(wq[:, 0, :], stage[:, 0, :], ACT.Copy, scale=DK ** -0.5).then_inc(w_hi, 1)
            act.wait_ge(w_in[2], 32)
            nc.scalar.activation(wv[:, 0, :], stage[:, 2, :], ACT.Copy).then_inc(w_hi, 1)
            act.wait_ge(w_in[3], 16)
            nc.scalar.activation(wo[:, 0, :], stage[:, 3, :], ACT.Copy).then_inc(w_hi, 1)
            with act.Fori(0, G // 2) as gg:
                for s in range(2):
                    act.wait_ge(x_turned, gg * 2 + s + 1)
                    act.wait_ge(xst[s], 1 + gg * 16)
                    nc.scalar.activation(xnt[:, s, 0], x_ps[:, :], ACT.Copy).then_inc(xnt_hi, 1)

        @block.vector
        def _(dve):
            dve.wait_ge(cx_hi, 1)
            dve.tensor_tensor(cxs[:, 1, :], cx[:, :], fp(cxs[:, 0, :]), ALU.subtract).then_inc(cx_lo, 1)
            dve.wait_ge(cxt_hi, 1)
            dve.tensor_tensor(cxt[:, 1, :, :].rearrange("p c b -> p (c b)"), c_ps[:, 0:KC * NB],
                              fp(cxt[:, 0, :, :]).rearrange("p c b -> p (c b)"), ALU.subtract).then_inc(cx_lo, 1)
            for p in range(NP):
                dve.wait_ge(wk_hi, p + 1)
                dve.tensor_tensor(wkt[:, 1, p, :], wk_ps[p % 2][:, 0:D], fp(wkt[:, 0, p, :]), ALU.subtract).then_inc(wk_lo, 1)
            for n, (w, i, k) in enumerate(((wq, 0, DK ** -0.5), (wv, 2, 1.0), (wo, 3, 1.0))):
                dve.wait_ge(w_hi, n + 1)
                dve.scalar_tensor_tensor(out=w[:, 1, :], in0=stage[:, i, :], scalar=k, in1=fp(w[:, 0, :]),
                                         op0=ALU.mult, op1=ALU.subtract)
            with dve.Fori(0, G // 2) as gg:
                for s in range(2):
                    dve.wait_ge(xld[s], (gg + 1) * 16)
                    for c in range(KC):
                        ins_ = dve.bn_stats(stats[:, s, c, :], x_in[:, s, c, :])
                    dve.drain()
                    for c in range(KC):
                        ins_ = dve.bn_aggr(mean_var[:, s, c, :], stats[:, s, c, :])
                    ins_.then_inc(aggregated, 1)
                    dve.wait_ge(aggregated, gg * 2 + s + 1)
                    dve.tensor_scalar(mean_var[:, s, :, 1], mean_var[:, s, :, 1], EPS, None, ALU.add).then_inc(moments, 1)
                for s in range(2):
                    dve.wait_ge(rstd_done, gg * 2 + s + 1)
                    for c in range(KC):
                        ins_ = dve.tensor_scalar(xn[:, s, c, :], x_in[:, s, c, :], mean_var[:, s, c, 0:1],
                                                 rstd[:, s, c, :], ALU.subtract, ALU.mult)
                    ins_.then_inc(xn_done, 1)
                for s in range(2):
                    dve.wait_ge(xnt_hi, gg * 2 + s + 1)
                    dve.tensor_tensor(xnt[:, s, 1].rearrange("p c t -> p (c t)"), x_ps[:, :],
                                      fp(xnt[:, s, 0]).rearrange("p c t -> p (c t)"), ALU.subtract).then_inc(xnt_lo, 1)

        @block.tensor
        def _(pe):
            pe.wait_ge(const_in, 16)
            pe.wait_ge(cx_in, 16)
            for c in range(KC):
                mm = pe.transpose(c_ps[:, c * NB:(c + 1) * NB], cx[:, c * P:(c + 1) * P], ident[:, :])
            mm.then_inc(cx_turned, 1)
            pe.wait_ge(w_in[1], 32)
            for p in range(NP):
                if p >= 2:
                    pe.wait_ge(wk_lo, p - 1)
                for c in range(KC):
                    mm = pe.transpose(wk_ps[p % 2][:, c * P:(c + 1) * P], wview[1][:, c, 2 * p:2 * p + 2, :], ident[:, :])
                mm.then_inc(wk_turned, 1)
            with pe.Fori(0, G // 2) as gg:
                for s in range(2):
                    pe.wait_ge(xn_done, 1 + gg * 2 + s + 1)
                    pe.wait_ge(xnt_lo, 1 + gg * 2 + s)
                    for c in range(KC):
                        for t in range(KC):
                            mm = pe.transpose(x_ps[:, c * GT + t * P:c * GT + (t + 1) * P],
                                              xn[:, s, t, c * P:(c + 1) * P], ident[:, :])
                    mm.then_inc(x_turned, 1)


def cross_attention(nc, ins, wq, wkt, wv, wo, cxt, ident, scratch):
    with ExitStack() as ctx:
        def sb(name, shape, dt=F32):
            return ctx.enter_context(nc.sbuf_tensor(name, shape, dt))

        def sem(name):
            return ctx.enter_context(nc.semaphore(name))

        def psum(name):
            return [ctx.enter_context(nc.psum_tensor(f"{name}{i}", [P, 512], F32)) for i in range(2)]

        xnt = sb("g_xnt", [P, 2, KC, GT], F32R)
        qt = sb("qt", [P, 2, 2, GT], F32R)
        qu = sb("qu", [P, 2, KC, GB, H, SQ], F32R)
        craw = sb("craw", [P, 2, KC, D])
        cs = sb("cs", [P, 2, 2, KC, D], F32R)
        ct = sb("ct", [P, 2, KC, LM + 2], F32R)
        prob = sb("prob", [P, 2, RT, LK])
        negmax = sb("negmax", [P, 2, RT])
        rowsum = sb("rowsum", [P, 2, RT])
        rinv = sb("rinv", [P, 2, RT])
        pxh = sb("pxh", [P, RT], F32R)
        px = sb("px", [P, NX])
        pt = sb("pt", [P, 2, KC, 512], F32R)
        xp = sb("xp", [NX, RT, P], F32R)
        cxg = sb("cxg", [NX, GB, D], F32R)
        mask = sb("row_mask", [NX, RT])
        heads = sb("heads", [P, 2, NP, GT], F32R)
        xg = sb("xg", [P, KC, D])

        s_bank, pt_bank, u_bank, m_bank = psum("s_bank"), psum("pt_bank"), psum("u_bank"), psum("m_bank")
        order = {"s": [], "pt": [], "u": [], "m": []}
        order["m"] += [("ct", 0)] + [("q", p) for p in range(NP)]
        for h in range(H):
            order["us"[h // 2 % 2]].append(("d", h))
        for b in range(GB):
            order["s"] += [("s", b, r) for r in range(RT)]
            order["pt"] += [("pt", b, c) for c in range(KC)]
            order["u"] += [("u", b, d) for d in range(KC)]
            order["m"] += [("px", b - 1)] * (b >= 1) + [("ct", b + 1)] * (b + 1 < GB)
        order["m"] += [("px", GB - 1), ("out", 0), ("out", 1)]
        for p in range(NP):
            order[("pt", "s")[p % 2]].append(("e", p))
        assert all(len(o) % 2 == 0 for o in order.values())
        banks = {"s": s_bank, "pt": pt_bank, "u": u_bank, "m": m_bank}
        ring = {what: (name, n) for name, o in order.items() for n, what in enumerate(o)}

        def bank_of(what):
            name, n = ring[what]
            return banks[name][n % 2]

        def held(what, like):
            v = bank_of(what)[:, 0:like.free_size()]
            if len(like.shape) == 3:
                v = v.rearrange("p (a b) -> p a b", a=like.shape[1])
            elif len(like.shape) == 4:
                v = v.rearrange("p (a b c) -> p a b c", a=like.shape[1], b=like.shape[2])
            return v

        fills = {name: sem(f"{name}_filled") for name in order}
        empties = {name: sem(f"{name}_emptied") for name in order}

        def filled(g, what, back=0):
            name, n = ring[what]
            return fills[name], (g + 1 - back) * len(order[name]) + n + 1

        def bank_free(g, what):
            name, n = ring[what]
            return empties[name], g * len(order[name]) + n + 1

        def emptied(g, what):
            name, n = ring[what]
            return empties[name], g * len(order[name]) + n + 3

        def fills_of(what):
            return fills[ring[what][0]]

        def empties_of(what):
            return empties[ring[what][0]]

        mask_in, cx_in, x_in, x_out, xnt_in = sem("mask_in"), sem("g_cx_in"), sem("g_x_in"), sem("g_x_out"), sem("g_xnt_in")
        c_in = [sem(f"c_in{i}") for i in range(2)]
        pad_set, passed, passed_sp = sem("pad_set"), sem("passed1"), sem("passed_sp")
        s_max, p_scaled, p_inv = sem("s_max"), sem("p_scaled"), sem("p_inv")
        ct_hi, q_hi, d_hi, pt_hi, u_hi, e_hi = (sem(f"{n}_hi") for n in ("ct", "q", "d", "pt", "u", "e"))
        c_hi, c_split, ct_last = sem("c_hi"), sem("c_split"), sem("ct_last")
        px_hi, px_done = sem("px_hi"), sem("px_done")
        block = ctx.enter_context(nc.Block())

        x_rows = ins["x"].rearrange("(g b) s d -> g (b s) d", g=G).rearrange("g (c p) d -> g p c d", p=P)
        x1_rows = scratch["x1"].rearrange("(g c p) d -> g p c d", c=KC, p=P)
        ctx_rows = ins["ctx"].rearrange("b k d -> b (k d)")
        started = (x_out,)

        def two_ago(b):
            return (b - 2) % GB, int(b < 2)

        @block.sync
        def _(sp):
            for counter in started:
                sp.sem_inc(counter, 1)
            sp.dma_start(mask[:, :], ins["mask"]).then_inc(mask_in, 16)
            with sp.Fori(0, G) as g:
                for b in range(GB):
                    sp.wait_ge(c_split, (g + 1) * GB + b - 1)
                    sp.sem_inc(passed_sp, 1)
                    sp.wait_ge(*filled(g, ("ct", two_ago(b)[0]), two_ago(b)[1]))
                    sp.sem_inc(passed_sp, 1)
                    sp.dma_start(craw[:, b % 2, :, :].rearrange("p c d -> p (c d)"),
                                 ctx_rows[bass.ds(g * GB + b, 1), 0:LM * D].rearrange("b (p n) -> (b p) n", p=P)
                                 ).then_inc(c_in[b % 2], 16)
                    if b == 1:
                        sp.wait_ge(*filled(g, ("q", NP - 1), 1))
                        sp.dma_start(fp(xnt[:, :, :, :]).rearrange("p a c t -> p (a c t)"),
                                     scratch["xnt"][bass.ds(g, 1)].rearrange("g p n -> (g p) n")).then_inc(xnt_in, 16)
                        sp.wait_ge(*filled(g, ("u", GB - 1, KC - 1), 1))
                        for t, part in enumerate((0, 0, 1)):
                            sp.dma_start(fp(cxg[t * RT:(t + 1) * RT, :, :]),
                                         scratch["cx"][part, bass.ds(g * GB, GB), :].partition_broadcast(RT)
                                         ).then_inc(cx_in, 16)
                        sp.wait_ge(x_out, 1 + g * 16)
                        sp.dma_start(xg[:, :, :], x_rows[bass.ds(g, 1)].rearrange("g p c d -> p (g c) d")).then_inc(x_in, 16)
            sp.wait_ge(x_out, 1 + G * 16)

        @block.gpsimd
        def _(pool):
            pool.memset(fp(ct[:, :, :, LM + 1:LM + 2]), 0.0).then_inc(pad_set, 1)
            pool.sem_inc(c_split, GB)
            with pool.Fori(0, G) as g:
                def split_c(b):
                    s = b % 2
                    pool.wait_ge(c_hi, g * GB + b + 1)
                    pool.tensor_tensor(cs[:, s, 1, :, :], craw[:, s, :, :], fp(cs[:, s, 0, :, :]), ALU.subtract).then_inc(c_split, 1)

                def last_row(b):
                    pool.wait_ge(*filled(g, ("s", (b - 1) % GB, RT - 1), int(b == 0)))
                    pool.sem_inc(passed, 1)
                    pool.tensor_copy(ct[:, :, :, LM], fp(cxt[:, :, :, bass.ds(g * GB + b, 1)]).rearrange("p a c b -> p a (c b)")).then_inc(ct_last, 1)

                def scale(b):
                    pool.wait_ge(p_inv, g * GB + b + 1)
                    pool.tensor_tensor(prob[:, b % 2], prob[:, b % 2], rinv[:, b % 2, :].unsqueeze(2).broadcast_to([P, RT, LK]),
                                       ALU.mult).then_inc(p_scaled, 1)

                def last_prob(b):
                    pool.wait_ge(p_scaled, g * GB + b + 1)
                    pool.wait_ge(*filled(g, ("px", (b - 1) % GB), int(b == 0)))
                    pool.sem_inc(passed, 1)
                    pool.tensor_copy(pxh[:, :], prob[:, b % 2, :, LM]).then_inc(px_hi, 1)
                    pool.wait_ge(px_hi, g * GB + b + 1)
                    pool.sem_inc(passed, 1)
                    pool.tensor_copy(px[:, 0:RT], fp(pxh[:, :]))
                    pool.tensor_copy(px[:, 2 * RT:3 * RT], fp(pxh[:, :]))
                    pool.tensor_tensor(px[:, RT:2 * RT], prob[:, b % 2, :, LM], fp(pxh[:, :]), ALU.subtract).then_inc(px_done, 1)

                split_c(0)
                last_row(0)
                for b in range(GB):
                    scale(b)
                    if b + 1 < GB:
                        last_row(b + 1)
                    last_prob(b)
                    if b + 1 < GB:
                        split_c(b + 1)

        @block.scalar
        def _(act):
            act.sem_inc(empties["m"], 2)
            with act.Fori(0, G) as g:
                def high(out, what, done):
                    act.wait_ge(*filled(g, what))
                    nc.scalar.activation(out, held(what, out), ACT.Copy).then_inc(done, 1)

                def c_high(b):
                    s = b % 2
                    act.wait_ge(c_in[s], (g * (GB // 2) + b // 2 + 1) * 16)
                    act.wait_ge(*filled(g, ("u", two_ago(b)[0], KC - 1), two_ago(b)[1]))
                    nc.scalar.activation(cs[:, s, 0, :, :], craw[:, s, :, :], ACT.Copy).then_inc(c_hi, 1)

                def exps(b, r):
                    act.wait_ge(s_max, g * GB * RT + RT * b + r + 1)
                    act.wait_ge(*filled(g, ("px", two_ago(b)[0]), two_ago(b)[1]))
                    nc.scalar.activation(prob[:, b % 2, r, :], bank_of(("s", b, r))[:, 0:LK], ACT.Exp, bias=negmax[:, b % 2, r:r + 1],
                                         accum_out=rowsum[:, b % 2, r:r + 1]).then_inc(empties["s"], 1)

                high(ct[:, 0, :, 0:LM], ("ct", 0), ct_hi)
                for p in range(NP):
                    high(qt[:, p % 2, 0, :], ("q", p), q_hi)
                    if p:
                        for h in (2 * p - 2, 2 * p - 1):
                            high(qu[:, 0, :, :, h, :], ("d", h), d_hi)
                c_high(0)
                for h in (H - 2, H - 1):
                    high(qu[:, 0, :, :, h, :], ("d", h), d_hi)
                for b in range(GB + 1):
                    if b < GB:
                        exps(b, 0)
                        exps(b, 1)
                    if b:
                        high(pt[:, 0, 0, :], ("pt", b - 1, 0), pt_hi)
                    if b < GB:
                        exps(b, 2)
                    if b:
                        high(pt[:, 0, 1, :], ("pt", b - 1, 1), pt_hi)
                    if b < GB:
                        exps(b, 3)
                    if b + 1 < GB:
                        high(ct[:, 0, :, 0:LM], ("ct", b + 1), ct_hi)
                        c_high(b + 1)
                    if b:
                        for d in range(KC):
                            high(qu[:, 0, d, b - 1, :, :].rearrange("p h q -> p (h q)"), ("u", b - 1, d), u_hi)
                for p in range(NP):
                    act.wait_ge(*filled(g, ("e", p)))
                    for s in range(2):
                        r = slice(s * DK, (s + 1) * DK)
                        op = nc.scalar.activation(heads[r, 0, p, :], bank_of(("e", p))[r, s * GT:(s + 1) * GT], ACT.Copy)
                    op.then_inc(e_hi, 1)
                act.wait_ge(*emptied(g, ("out", 1)))
                nc.scalar.dma_start(x1_rows[bass.ds(g, 1)].rearrange("g p c d -> p (g c) d"), xg[:, :, :]).then_inc(x_out, 16)

        @block.vector
        def _(dve):
            for name in ("s", "pt", "u"):
                dve.sem_inc(empties[name], 2)
            dve.wait_ge(mask_in, 16)
            with dve.Fori(0, G) as g:
                def low(out, hi, what, hi_sem, hi_count):
                    dve.wait_ge(hi_sem, hi_count)
                    dve.tensor_tensor(out, held(what, out), fp(hi), ALU.subtract).then_inc(empties_of(what), 1)

                def ct_low(b):
                    low(ct[:, 1, :, 0:LM], ct[:, 0, :, 0:LM], ("ct", b), ct_hi, g * GB + b + 1)

                def d_low(h):
                    low(qu[:, 1, :, :, h, :], qu[:, 0, :, :, h, :], ("d", h), d_hi, g * H + h + 1)

                def maxs(b, r):
                    dve.wait_ge(*filled(g, ("s", b, r)))
                    dve.tensor_reduce(negmax[:, b % 2, r:r + 1], bank_of(("s", b, r))[:, 0:LK], AX.X, ALU.max, negate=True).then_inc(s_max, 1)

                def invert(b):
                    dve.wait_ge(*emptied(g, ("s", b, RT - 1)))
                    dve.reciprocal(rinv[:, b % 2, :], rowsum[:, b % 2, :]).then_inc(p_inv, 1)

                def p_low(b, c):
                    low(pt[:, 1, c, :], pt[:, 0, c, :], ("pt", b, c), pt_hi, (g * GB + b) * KC + c + 1)

                def u_low(b, d):
                    hi, lo = (qu[:, i, d, b, :, :].rearrange("p h q -> p (h q)") for i in range(2))
                    low(lo, hi, ("u", b, d), u_hi, (g * GB + b) * KC + d + 1)

                def spread_px(b):
                    dve.wait_ge(*filled(g, ("px", b)))
                    dve.tensor_tensor(xp[:, :, :], bank_of(("px", b))[0:NX, 0:P].unsqueeze(1).broadcast_to([NX, RT, P]),
                                      mask[:, :].unsqueeze(2).broadcast_to([NX, RT, P]), ALU.mult).then_inc(empties["m"], 1)

                ct_low(0)
                for p in range(NP):
                    low(qt[:, p % 2, 1, :], qt[:, p % 2, 0, :], ("q", p), q_hi, g * NP + p + 1)
                    if p:
                        d_low(2 * p - 2)
                        d_low(2 * p - 1)
                d_low(H - 2)
                d_low(H - 1)
                for b in range(GB + 1):
                    if b < GB:
                        maxs(b, 0)
                        maxs(b, 1)
                        maxs(b, 2)
                    if b:
                        p_low(b - 1, 0)
                        spread_px(b - 1)
                    if b < GB:
                        maxs(b, 3)
                    if b:
                        p_low(b - 1, 1)
                    if b < GB:
                        invert(b)
                    if b + 1 < GB:
                        ct_low(b + 1)
                    if b:
                        u_low(b - 1, 0)
                        u_low(b - 1, 1)
                for p in range(NP):
                    dve.wait_ge(e_hi, g * NP + p + 1)
                    for s in range(2):
                        r = slice(s * DK, (s + 1) * DK)
                        op = dve.tensor_tensor(heads[r, 1, p, :], bank_of(("e", p))[r, s * GT:(s + 1) * GT],
                                               fp(heads[r, 0, p, :]), ALU.subtract)
                    op.then_inc(empties_of(("e", p)), 1)
                dve.wait_ge(x_in, (g + 1) * 16)
                for t in range(KC):
                    dve.wait_ge(*filled(g, ("out", t)))
                    dve.tensor_tensor(xg[:, t, :], bank_of(("out", t))[:, 0:D], xg[:, t, :], ALU.add).then_inc(empties["m"], 1)

        @block.tensor
        def _(pe):
            pe.wait_ge(pad_set, 1)
            for name, o in order.items():
                pe.sem_inc(fills[name], len(o))
            with pe.Fori(0, G) as g:
                def product(out, terms, first=True, last=True):
                    for i, (w, m) in enumerate(terms):
                        mm = pe.matmul(out, w, m, start=first and i == 0, stop=last and i == len(terms) - 1)
                    return mm

                def turn_c(b):
                    out = bank_of(("ct", b))
                    pe.wait_ge(c_in[b % 2], (g * (GB // 2) + b // 2 + 1) * 16)
                    pe.wait_ge(*bank_free(g, ("ct", b)))
                    for d in range(KC):
                        for c in range(KC):
                            mm = pe.transpose(out[:, d * LM + c * P:d * LM + (c + 1) * P],
                                              craw[:, b % 2, c, d * P:(d + 1) * P], ident[:, :])
                    mm.then_inc(fills["m"], 1)

                def project_q(p):
                    pe.wait_ge(*bank_free(g, ("q", p)))
                    if p == 0:
                        pe.wait_ge(xnt_in, (g + 1) * 16)
                    product(bank_of(("q", p))[:, 0:GT],
                            [(wq[:, i, c * H * DK + p * P:c * H * DK + (p + 1) * P], xnt[:, j, c, :])
                             for i, j in PASSES for c in range(KC)]).then_inc(fills["m"], 1)

                def q_to_context(p):
                    pe.wait_ge(*emptied(g, ("q", p)))
                    for s in range(2):
                        h, r = 2 * p + s, slice(s * DK, (s + 1) * DK)
                        pe.wait_ge(*bank_free(g, ("d", h)))
                        for c in range(KC):
                            mm = product(bank_of(("d", h))[:, c * GT:(c + 1) * GT],
                                         [(wkt[r, i, p, c * P:(c + 1) * P], qt[r, p % 2, j, :]) for i, j in PASSES])
                        mm.then_inc(fills_of(("d", h)), 1)

                def scores(b, r):
                    if r == 0:
                        pe.wait_ge(*emptied(g, ("ct", b)))
                        pe.wait_ge(ct_last, g * GB + b + 1)
                        if b == 0:
                            pe.wait_ge(*emptied(g, ("d", H - 3)))
                            pe.wait_ge(*emptied(g, ("d", H - 1)))
                    pe.wait_ge(*bank_free(g, ("s", b, r)))
                    product(bank_of(("s", b, r))[:, 0:LM + 2],
                            [(qu[:, i, c, b, HR * r:HR * (r + 1), :].rearrange("p h q -> p (h q)"), ct[:, j, c, :])
                             for i, j in PASSES for c in range(KC)]).then_inc(fills["s"], 1)

                def turn_p(b, c):
                    out = bank_of(("pt", b, c))
                    pe.wait_ge(p_scaled, g * GB + b + 1)
                    pe.wait_ge(*bank_free(g, ("pt", b, c)))
                    for r in range(RT):
                        mm = pe.transpose(out[:, r * P:(r + 1) * P], prob[:, b % 2, r, c * P:(c + 1) * P], ident[:, :])
                    mm.then_inc(fills["pt"], 1)

                def turn_px(b):
                    pe.wait_ge(px_done, g * GB + b + 1)
                    pe.wait_ge(*bank_free(g, ("px", b)))
                    pe.transpose(bank_of(("px", b))[0:NX, 0:P], px[:, :], ident[:, :]).then_inc(fills["m"], 1)

                def attend(b, d):
                    dd = slice(d * P, (d + 1) * P)
                    out = bank_of(("u", b, d))[:, :]
                    if d == 0:
                        pe.wait_ge(c_split, (g + 1) * GB + b + 1)
                        pe.wait_ge(pt_hi, (g * GB + b + 1) * KC)
                        if b == 0:
                            pe.wait_ge(cx_in, (g + 1) * 48)
                    pe.wait_ge(*bank_free(g, ("u", b, d)))
                    product(out, [(cs[:, b % 2, i, c, dd], pt[:, 0, c, :]) for i in range(2) for c in range(KC)], last=False)
                    if d == 0:
                        pe.wait_ge(*emptied(g, ("px", b)))
                        pe.wait_ge(*emptied(g, ("pt", b, KC - 1)))
                    product(out, [(cxg[:, b, dd], xp[:, :, :].rearrange("t r n -> t (r n)"))]
                            + [(cs[:, b % 2, 0, c, dd], pt[:, 1, c, :]) for c in range(KC)], first=False).then_inc(fills["u"], 1)

                turn_c(0)
                project_q(0)
                for p in range(NP):
                    if p + 1 < NP:
                        project_q(p + 1)
                    q_to_context(p)
                for b in range(GB + 1):
                    if b < GB:
                        scores(b, 0)
                        scores(b, 1)
                    if b:
                        turn_p(b - 1, 0)
                    if b < GB:
                        scores(b, 2)
                    if b:
                        turn_p(b - 1, 1)
                        turn_px(b - 1)
                    if b < GB:
                        scores(b, 3)
                    if b + 1 < GB:
                        turn_c(b + 1)
                    if b:
                        attend(b - 1, 0)
                        attend(b - 1, 1)
                for p in range(NP):
                    if p == 0:
                        pe.wait_ge(*emptied(g, ("u", GB - 1, KC - 1)))
                    pe.wait_ge(*bank_free(g, ("e", p)))
                    product(bank_of(("e", p))[:, :],
                            [(wv[:, i, c * H * DK + p * P:c * H * DK + (p + 1) * P],
                              qu[:, j, c, :, 2 * p:2 * p + 2, :].rearrange("p b h q -> p h b q"))
                             for i, j in PASSES for c in range(KC)]).then_inc(fills_of(("e", p)), 1)
                pe.wait_ge(*emptied(g, ("e", NP - 2)))
                pe.wait_ge(*emptied(g, ("e", NP - 1)))
                for t in range(KC):
                    pe.wait_ge(*bank_free(g, ("out", t)))
                    product(bank_of(("out", t))[:, 0:D],
                            [(heads[:, i, p, t * P:(t + 1) * P], wo[:, j, p * D:(p + 1) * D])
                             for i, j in PASSES for p in range(NP)]).then_inc(fills["m"], 1)


EXPERTS, CAP = 32, 160
HS, HD = 16, D // 16
HC = P // HD
SKIP = float(4 * EXPERTS * CAP)


def self_attention(nc, ins, scratch, gate, slot, ident):
    with ExitStack() as ctx:
        def sb(name, shape, dt=F32):
            return ctx.enter_context(nc.sbuf_tensor(name, shape, dt))

        def sem(name):
            return ctx.enter_context(nc.semaphore(name))

        w_self = sb("w_self", [P, 3, KC, D])
        w_f = sb("w_f", [P, KC, D])
        w_r = sb("w_r", [P, KC, EXPERTS])
        bq = sb("bq_col", [P, KC])
        bk = sb("bk_col", [P, KC])
        bv = sb("bv_col", [P, KC])
        bf = sb("bf_rows", [P, D])
        alibi = sb("alibi_tile", [P, RT, SQ])
        head_mask = sb("head_mask", [P, HC])
        upto = sb("upto", [P, P])
        ones = sb("ones", [P, P])
        rank = sb("rank", [P, EXPERTS])
        zero = sb("zero", [P, ZR * D])
        x1 = sb("x1_tile", [P, KC, D])
        x2 = sb("x2_tile", [P, KC, D])
        z = sb("z_tile", [P, KC, D])
        xn = sb("xn1", [P, KC, D])
        xn2 = sb("xn2", [P, KC, D])
        half = sb("minus_half", [P, KC, 1])
        stats = sb("stats1", [P, KC, 6])
        mv = sb("mean_var1", [P, KC, 2])
        rstd = sb("rstd1", [P, KC, 1])
        stats2 = sb("stats2", [P, KC, 6])
        mv2 = sb("mean_var2", [P, KC, 2])
        rstd2 = sb("rstd2", [P, KC, 1])
        xt = sb("xt", [P, KC, GT])
        xt2 = sb("xt2", [P, KC, GT])
        q_t = sb("q_t", [P, KC, GT])
        k_t = sb("k_t", [P, KC, GT])
        q_bd = sb("q_bd", [P, KC, GB, HC, SQ])
        v_bd = sb("v_bd", [P, KC, HR, KC, P])
        prob = sb("prob_self", [P, KC, HR * RT, SQ])
        negmax = sb("rowmax", [P, KC, HR * RT])
        rsum = sb("rsum", [P, KC, HR * RT])
        rinv = sb("rinv_self", [P, KC, HR * RT])
        p_t = sb("p_t", [P, KC, HR, P])
        o_t = sb("o_t", [P, KC, KC, HR, SQ])
        lmax = sb("lmax", [P, KC])
        nlmax = sb("nlmax", [P, KC])
        expl = sb("expl", [P, KC, EXPERTS])
        esum = sb("esum", [P, KC])
        cand = sb("cand", [P, KC, EXPERTS])
        best = sb("best", [P, KC])
        onehot = sb("onehot", [P, KC, EXPERTS])
        taken = sb("taken", [P, EXPERTS])
        place = sb("place", [P, KC, EXPERTS])
        pos = sb("pos", [P, KC])
        refused = sb("refused", [P, KC])
        slot_f = sb("slot_f", [P, KC])
        slot_s = sb("slot_s", [P, KC], I32)
        gate_r = sb("gate_r", [P, KC])
        kept = sb("kept", [P, KC])
        slot_g = sb("slot_g", [P, KC])

        bank = [ctx.enter_context(nc.psum_tensor(f"bank{i}", [P, 512], F32)) for i in range(8)]
        xt_b, q_b, k_b, v_b = bank[0:4]
        s_b, pt_b = bank[0:2], bank[4:6]
        o_b = (bank[6:8], bank[4:6])
        f_b, xt2_b, l_b, n_b = bank[6], bank[7], bank[4], bank[5]

        w_in, x_in = sem("w2_in"), sem("x1_in")
        z_out = sem("z_out")
        set_up, wq_scaled, zeroed = sem("set_up"), sem("wq_scaled"), sem("zeroed")
        aggr_ok, var_ok, rstd_ok, xn_ok = (sem(f"ln1_{n}") for n in ("aggr", "var", "rstd", "xn"))
        aggr2_ok, var2_ok, rstd2_ok, xn2_ok = (sem(f"ln2_{n}") for n in ("aggr", "var", "rstd", "xn"))
        xt_full, xt_ok = sem("xt_full"), sem("xt_ok")
        q_full, k_full, v_full = sem("q_full"), sem("k_full"), sem("v_full")
        q_ok, k_ok = sem("q_ok"), sem("k_ok")
        qbd_act, qbd_dve, qbd_pool, vbd_act, vbd_dve = sem("qbd_act"), sem("qbd_dve"), sem("qbd_pool"), sem("vbd_act"), sem("vbd_dve")
        sc_full, biased, max_ok, sub_ok, exp_ok, sum_ok, inv_ok, prob_ok = (
            sem(n) for n in ("sc_full", "biased", "max_ok", "sub_ok", "exp_ok", "sum_ok", "inv_ok", "prob_ok"))
        pt_full, pt_ok, o_full = sem("pt2_full"), sem("pt2_ok"), sem("o_full")
        ot_act, ot_dve = sem("ot_act"), sem("ot_dve")
        f_full, xb_ok, x2_ok, z_ok = sem("f_full"), sem("xb_ok"), sem("x2_ok"), sem("z_ok")
        xt2_full, xt2_ok, l_full = sem("xt2_full"), sem("xt2_ok"), sem("l_full")
        step, late, passed = sem("step"), sem("late"), sem("passed2")
        route = sem("route")
        lexp_ok, onehot_ok, n_full, slot_ok, sent, sent_ok = sem("lexp_ok"), sem("onehot_ok"), sem("n_full"), sem("slot_ok"), sem("sent"), sem("sent_ok")
        block = ctx.enter_context(nc.Block())

        def v_block(b, r):
            to = v_bd[r * SQ:(r + 1) * SQ, :, b, r // 2, :].rearrange("p t (h n) -> p t h n", h=HR)
            src = v_b[b * SQ:(b + 1) * SQ, :].rearrange("p (t r h n) -> p t r h n", t=KC, r=RT, h=HR)
            return to[:, :, :, (r % 2) * HD:(r % 2 + 1) * HD], src[:, :, r]

        x1_rows = scratch["x1"].rearrange("(g c p) d -> g p c d", c=KC, p=P)
        z_rows = scratch["z"].rearrange("(g c p) d -> g p c d", c=KC, p=P)
        HA = 5
        N_W = 7 + 6

        started = (x2_ok, xb_ok, z_ok, xn2_ok, sc_full, o_full, z_out, v_full, qbd_pool, qbd_dve, f_full, l_full, xt_full,
                   pt_full, sent_ok, xt2_full, lexp_ok, ot_dve, ot_act, xt2_ok, slot_ok)

        @block.sync
        def _(sp):
            for counter in started:
                sp.sem_inc(counter, 1)

            def load_x1(i):
                sp.wait_ge(xb_ok, 1 + i)
                sp.dma_start(x1[:, :, :], x1_rows[bass.ds(i, 1)].rearrange("g p c d -> p (g c) d")).then_inc(x_in, 16)

            def store_z(i):
                sp.wait_ge(z_ok, 1 + i + 1)
                sp.dma_start(z_rows[bass.ds(i, 1)].rearrange("g p c d -> p (g c) d"), z[:, :, :]).then_inc(z_out, 16)

            load_x1(0)
            for i, name in enumerate(("s_wq", "s_wk", "s_wv")):
                sp.dma_start(w_self[:, i], ins[name].rearrange("(c p) n -> p c n", p=P)).then_inc(w_in, 16)
            sp.dma_start(bq[:, :], ins["s_bq"]).then_inc(w_in, 16)
            sp.dma_start(bk[:, :], ins["s_bk"]).then_inc(w_in, 16)
            sp.dma_start(bv[:, :], ins["s_bv"]).then_inc(w_in, 16)
            sp.dma_start(bf[:, :], ins["s_bf"].partition_broadcast(P)).then_inc(w_in, 16)
            sp.wait_ge(set_up, 1)
            rows = scratch["buf"].rearrange("(a p j) d -> a p (j d)", p=P, j=ZR)
            for a in range(EXPERTS * CAP // (ZR * P)):
                sp.dma_start(rows[a], zero[:, :]).then_inc(zeroed, 16)
            with sp.Fori(0, G - 1) as i:
                load_x1(i + 1)
                store_z(i)
            store_z(G - 1)
            sp.wait_ge(z_out, 1 + 16 * G)

        @block.gpsimd
        def _(pool):
            def rstd_1(i):
                pool.wait_ge(var_ok, i + 1)
                pool.tensor_tensor(rstd[:, :, :], mv[:, :, 1:2], half[:, :, :], ALU.pow).then_inc(rstd_ok, 1)

            def spread_q(i):
                pool.wait_ge(q_ok, (i + 1) * KC)
                pool.wait_ge(sc_full, 1 + i * KC)
                to = [P, GB, HC - HA, SQ]
                pool.tensor_tensor(q_bd[:, 1, :, HA:HC, :], q_t[:, 1, :].rearrange("p (b q) -> p b q", b=GB).unsqueeze(2).broadcast_to(to),
                                   head_mask[:, HA:HC].unsqueeze(1).unsqueeze(3).broadcast_to(to), ALU.mult).then_inc(qbd_pool, 1)

            def add_bias(i):
                pool.wait_ge(x_in, (i + 1) * 16)
                pool.wait_ge(z_ok, 1 + i)
                pool.wait_ge(xn2_ok, 1 + i)
                pool.tensor_tensor(x2[:, :, :], x1[:, :, :], bf[:, :].unsqueeze(1).broadcast_to([P, KC, D]), ALU.add).then_inc(xb_ok, 1)

            def scale_prob(i, t):
                pool.wait_ge(inv_ok, i * KC + t + 1)
                pool.tensor_tensor(prob[:, t], prob[:, t], rinv[:, t, :].unsqueeze(2).broadcast_to([P, HR * RT, SQ]), ALU.mult).then_inc(prob_ok, 1)

            def rstd_2(i):
                pool.wait_ge(var2_ok, i + 1)
                pool.tensor_tensor(rstd2[:, :, :], mv2[:, :, 1:2], half[:, :, :], ALU.pow).then_inc(rstd2_ok, 1)

            def sum_z(i):
                pool.wait_ge(xn2_ok, 1 + i + 1)
                pool.wait_ge(z_out, 1 + i * 16)
                pool.tensor_tensor(z[:, :, :], x2[:, :, :], xn2[:, :, :], ALU.add).then_inc(z_ok, 1)

            def scatter(i):
                pool.wait_ge(slot_ok, 1 + i + 1)
                pool.sem_inc(passed, 1)
                for t in range(KC):
                    pool.indirect_dma_start(out=scratch["buf"], out_offset=bass.IndirectOffsetOnAxis(ap=slot_s[:, t:t + 1], axis=0),
                                            in_=xn2[:, t, :], in_offset=None, bounds_check=EXPERTS * CAP - 1, oob_is_err=False).then_inc(sent, 16)
                pool.wait_ge(sent, (i + 1) * 16 * KC)
                pool.sem_inc(sent_ok, 1)

            pool.memset(zero[:, :], 0.0).then_inc(set_up, 1)
            pool.memset(half[:, :, :], -0.5).then_inc(set_up, 1)
            pool.memset(ones[:, :], 1.0).then_inc(set_up, 1)
            pool.memset(taken[:, :], 0.0).then_inc(set_up, 1)
            pool.memset(v_bd[:, :, :, :, :], 0.0).then_inc(set_up, 1)
            pool.wait_ge(w_in, 16 * N_W)
            pool.wait_ge(set_up, 5)
            def round(i, more=True):
                spread_q(i + 1)
                rstd_2(i)
                sum_z(i)
                add_bias(i + 1)
                scale_prob(i + 1, 0)
                if more:
                    rstd_1(i + 2)
                scale_prob(i + 1, 1)
                scatter(i)

            rstd_1(0)
            spread_q(0)
            add_bias(0)
            rstd_1(1)
            for t in range(KC):
                scale_prob(0, t)
            pool.wait_ge(zeroed, 16 * (EXPERTS * CAP // (ZR * P)))
            with pool.Fori(0, G - 2) as i:
                round(i)
            round(G - 2, more=False)
            rstd_2(G - 1)
            sum_z(G - 1)
            scatter(G - 1)

        @block.scalar
        def _(act):
            def copy_xt(i):
                act.wait_ge(xt_full, 1 + i + 1)
                act.wait_ge(v_full, 1 + i)
                nc.scalar.activation(xt[:, :, :].rearrange("p c t -> p (c t)"), xt_b[:, :], ACT.Copy).then_inc(xt_ok, 1)

            def bias_q(i):
                act.wait_ge(q_full, i + 1)
                act.wait_ge(qbd_pool, 1 + i)
                act.wait_ge(qbd_dve, 1 + i)
                for c in range(KC):
                    nc.scalar.activation(q_t[:, c, :], q_b[:, c * GT:(c + 1) * GT], ACT.Identity, bias=bq[:, c:c + 1]).then_inc(q_ok, 1)

            def spread_q(i):
                act.wait_ge(q_ok, (i + 1) * KC)
                act.wait_ge(sc_full, 1 + i * KC)
                for h in range(HA):
                    op = nc.scalar.activation(q_bd[:, 1, :, h, :], q_t[:, 1, :].rearrange("p (b q) -> p b q", b=GB), ACT.Copy, scale=head_mask[:, h:h + 1])
                op.then_inc(qbd_act, 1)

            def bias_k(i):
                act.wait_ge(k_full, i + 1)
                act.wait_ge(sc_full, 1 + i * KC)
                for c in range(KC):
                    nc.scalar.activation(k_t[:, c, :], k_b[:, c * GT:(c + 1) * GT], ACT.Identity, bias=bk[:, c:c + 1]).then_inc(k_ok, 1)

            def spread_v(i):
                act.wait_ge(v_full, 1 + i + 1)
                act.wait_ge(o_full, 1 + i * KC)
                for b in (0, 1):
                    for r in range(RT):
                        op = nc.scalar.activation(*v_block(b, r), ACT.Copy)
                op.then_inc(vbd_act, 1)

            def exp_prob(i, t):
                act.wait_ge(sub_ok, i * KC + t + 1)
                nc.scalar.activation(prob[:, t], prob[:, t], ACT.Exp).then_inc(exp_ok, 1)

            def copy_pt(i, t):
                act.wait_ge(pt_full, 1 + i * KC + t + 1)
                act.wait_ge(o_full, 1 + i * KC)
                nc.scalar.activation(p_t[:, t].rearrange("p b n -> p (b n)"), pt_b[t][:, :], ACT.Copy).then_inc(pt_ok, 1)

            def take_o(i, t):
                act.wait_ge(o_full, 1 + i * KC + t + 1)
                act.wait_ge(f_full, 1 + i)
                for h in range(HR):
                    r = slice(h * SQ, (h + 1) * SQ)
                    op = nc.scalar.activation(o_t[r, 0, t], o_b[t][0][r, :].rearrange("p (b h q) -> p b h q", b=HR, h=HR)[:, :, h, :],
                                              ACT.Identity, bias=bv[r, 0:1])
                op.then_inc(ot_act, 1)

            def copy_xt2(i):
                act.wait_ge(xt2_full, 1 + i + 1)
                act.wait_ge(l_full, 1 + i)
                nc.scalar.activation(xt2[:, :, :].rearrange("p c t -> p (c t)"), xt2_b[:, :], ACT.Copy).then_inc(xt2_ok, 1)

            def exp_logits(i):
                act.wait_ge(route, i * 6 + 3)
                for t in range(KC):
                    op = nc.scalar.activation(expl[:, t, :], l_b[:, t * EXPERTS:(t + 1) * EXPERTS], ACT.Exp, bias=nlmax[:, t:t + 1], accum_out=esum[:, t:t + 1])
                op.then_inc(lexp_ok, 1)

            nc.scalar.dma_start(w_f[:, :, :], ins["s_wf"]).then_inc(w_in, 16)
            nc.scalar.dma_start(w_r[:, :, :], ins["w_router"].rearrange("(c p) n -> p c n", p=P)).then_inc(w_in, 16)
            for to, name in ((alibi[:, :, :], "alibi"), (head_mask[:, :], "head_mask"), (upto[:, :], "upto"), (rank[:, :], "rank")):
                nc.scalar.dma_start(to, ins[name]).then_inc(w_in, 16)
            act.wait_ge(w_in, 16 * N_W)
            nc.scalar.activation(w_self[:, 0], w_self[:, 0], ACT.Copy, scale=HD ** -0.5).then_inc(wq_scaled, 1)
            nc.scalar.activation(bq[:, :], bq[:, :], ACT.Copy, scale=HD ** -0.5).then_inc(wq_scaled, 1)
            act.wait_ge(wq_scaled, 2)
            copy_xt(0)
            bias_q(0)
            spread_q(0)
            bias_k(0)
            spread_v(0)
            for t in range(KC):
                exp_prob(0, t)
            with act.Fori(0, G - 1) as i:
                copy_xt(i + 1)
                copy_pt(i, 0)
                bias_q(i + 1)
                copy_pt(i, 1)
                spread_q(i + 1)
                take_o(i, 0)
                bias_k(i + 1)
                take_o(i, 1)
                spread_v(i + 1)
                copy_xt2(i)
                exp_prob(i + 1, 0)
                exp_prob(i + 1, 1)
                exp_logits(i)
            for t in range(KC):
                copy_pt(G - 1, t)
            for t in range(KC):
                take_o(G - 1, t)
            copy_xt2(G - 1)
            exp_logits(G - 1)

        @block.vector
        def _(dve):
            def stats_1(i):
                dve.wait_ge(x_in, (i + 1) * 16)
                for c in range(KC):
                    op = dve.bn_stats(stats[:, c, :], x1[:, c, :])
                dve.drain()
                for c in range(KC):
                    op = dve.bn_aggr(mv[:, c, :], stats[:, c, :])
                op.then_inc(aggr_ok, 1)
                dve.wait_ge(aggr_ok, i + 1)
                dve.tensor_scalar(mv[:, :, 1], mv[:, :, 1], EPS, None, ALU.add).then_inc(var_ok, 1)

            def norm_1(i):
                dve.wait_ge(rstd_ok, i + 1)
                dve.wait_ge(xt_full, 1 + i)
                for c in range(KC):
                    op = dve.tensor_scalar(xn[:, c, :], x1[:, c, :], mv[:, c, 0:1], rstd[:, c, :], ALU.subtract, ALU.mult)
                op.then_inc(xn_ok, 1)

            def spread_q(i):
                dve.wait_ge(q_ok, (i + 1) * KC)
                dve.wait_ge(sc_full, 1 + i * KC)
                for h in range(HC):
                    op = dve.tensor_scalar(q_bd[:, 0, :, h, :], q_t[:, 0, :].rearrange("p (b q) -> p b q", b=GB), head_mask[:, h:h + 1], None, ALU.mult)
                op.then_inc(qbd_dve, 1)

            def spread_v(i):
                dve.wait_ge(v_full, 1 + i + 1)
                dve.wait_ge(vbd_act, i + 1)
                dve.wait_ge(o_full, 1 + i * KC)
                for b in (2, 3):
                    for r in range(RT):
                        op = dve.tensor_copy(*v_block(b, r))
                op.then_inc(vbd_dve, 1)

            def shift_scores(i, t):
                dve.wait_ge(sc_full, 1 + i * KC + t + 1)
                dve.wait_ge(pt_full, 1 + i * KC)
                dve.tensor_tensor(prob[:, t].rearrange("p (b r) k -> p b (r k)", b=HR), s_b[t][:, :].rearrange("p (b n) -> p b n", b=HR),
                                  alibi[:, :, :].rearrange("p r k -> p (r k)").unsqueeze(1).broadcast_to([P, HR, RT * SQ]), ALU.add).then_inc(biased, 1)
                dve.wait_ge(biased, i * KC + t + 1)
                dve.tensor_reduce(negmax[:, t, :], prob[:, t], AX.X, ALU.max).then_inc(max_ok, 1)
                dve.wait_ge(max_ok, i * KC + t + 1)
                dve.tensor_tensor(prob[:, t], prob[:, t], negmax[:, t, :].unsqueeze(2).broadcast_to([P, HR * RT, SQ]), ALU.subtract).then_inc(sub_ok, 1)

            def sum_rows(i, t):
                dve.wait_ge(exp_ok, i * KC + t + 1)
                dve.tensor_reduce(rsum[:, t, :], prob[:, t], AX.X, ALU.add).then_inc(sum_ok, 1)
                dve.wait_ge(sum_ok, i * KC + t + 1)
                dve.reciprocal(rinv[:, t, :], rsum[:, t, :]).then_inc(inv_ok, 1)

            def take_o(i, t):
                dve.wait_ge(o_full, 1 + i * KC + t + 1)
                dve.wait_ge(f_full, 1 + i)
                for h in range(HR):
                    r = slice(h * SQ, (h + 1) * SQ)
                    op = dve.tensor_scalar(o_t[r, 1, t], o_b[t][1][r, :].rearrange("p (b h q) -> p b h q", b=HR, h=HR)[:, :, h, :],
                                           bv[r, 1:2], None, ALU.add)
                op.then_inc(ot_dve, 1)

            def stats_2(i):
                dve.wait_ge(f_full, 1 + i + 1)
                dve.wait_ge(xb_ok, 1 + i + 1)
                for t in range(KC):
                    dve.tensor_tensor(x2[:, t, :], f_b[:, t * D:(t + 1) * D], x2[:, t, :], ALU.add).then_inc(x2_ok, 1)
                dve.wait_ge(x2_ok, 1 + (i + 1) * KC)
                for c in range(KC):
                    op = dve.bn_stats(stats2[:, c, :], x2[:, c, :])
                dve.drain()
                for c in range(KC):
                    op = dve.bn_aggr(mv2[:, c, :], stats2[:, c, :])
                op.then_inc(aggr2_ok, 1)
                dve.wait_ge(aggr2_ok, i + 1)
                dve.tensor_scalar(mv2[:, :, 1], mv2[:, :, 1], EPS, None, ALU.add).then_inc(var2_ok, 1)

            def norm_2(i):
                dve.wait_ge(rstd2_ok, i + 1)
                dve.wait_ge(z_ok, 1 + i)
                dve.wait_ge(xt2_full, 1 + i)
                dve.wait_ge(sent_ok, 1 + i)
                for c in range(KC):
                    op = dve.tensor_scalar(xn2[:, c, :], x2[:, c, :], mv2[:, c, 0:1], rstd2[:, c, :], ALU.subtract, ALU.mult)
                op.then_inc(xn2_ok, 1)

            def choose(i):
                logits = l_b[:, 0:KC * EXPERTS].rearrange("p (t e) -> p t e", t=KC)
                dve.wait_ge(l_full, 1 + i + 1)
                dve.wait_ge(lexp_ok, 1 + i)
                dve.tensor_reduce(lmax[:, :], logits, AX.X, ALU.max).then_inc(route, 1)
                dve.tensor_reduce(nlmax[:, :], logits, AX.X, ALU.max, negate=True).then_inc(route, 1)
                dve.wait_ge(route, i * 6 + 2)
                for t in range(KC):
                    op = dve.scalar_tensor_tensor(out=cand[:, t, :], in0=logits[:, t, :], scalar=lmax[:, t:t + 1], in1=rank[:, :], op0=ALU.is_ge, op1=ALU.mult)
                op.then_inc(route, 1)
                dve.wait_ge(route, i * 6 + 3)
                dve.tensor_reduce(best[:, :], cand[:, :, :], AX.X, ALU.max).then_inc(route, 1)
                dve.wait_ge(route, i * 6 + 4)
                for t in range(KC):
                    op = dve.tensor_scalar(onehot[:, t, :], rank[:, :], best[:, t:t + 1], None, ALU.is_equal)
                op.then_inc(onehot_ok, 1)

            def give_slots(i):
                dve.wait_ge(n_full, i + 1)
                for t in range(KC):
                    dve.tensor_tensor(place[:, t, :], n_b[:, t * EXPERTS:(t + 1) * EXPERTS], taken[:, :], ALU.add).then_inc(step, 1)
                    dve.wait_ge(step, i * 4 + 2 * t + 1)
                    dve.tensor_tensor(taken[:, :], n_b[:, (KC + t) * EXPERTS:(KC + t + 1) * EXPERTS], taken[:, :], ALU.add).then_inc(step, 1)
                    dve.wait_ge(step, i * 4 + 2 * t + 2)
                dve.tensor_tensor(place[:, :, :], place[:, :, :], onehot[:, :, :], ALU.mult).then_inc(route, 1)
                dve.wait_ge(route, i * 6 + 5)
                dve.tensor_reduce(pos[:, :], place[:, :, :], AX.X, ALU.add).then_inc(route, 1)
                dve.wait_ge(route, i * 6 + 6)
                dve.tensor_scalar(refused[:, :], pos[:, :], float(CAP), SKIP, ALU.is_gt, ALU.mult).then_inc(late, 1)
                dve.tensor_scalar(kept[:, :], pos[:, :], float(CAP), None, ALU.is_le).then_inc(late, 1)
                dve.tensor_scalar(slot_f[:, :], best[:, :], -float(CAP), float(EXPERTS * CAP - 1), ALU.mult, ALU.add).then_inc(late, 1)
                dve.wait_ge(late, i * 8 + 3)
                dve.tensor_tensor(slot_f[:, :], slot_f[:, :], pos[:, :], ALU.add).then_inc(late, 1)
                dve.wait_ge(late, i * 8 + 4)
                dve.tensor_tensor(slot_f[:, :], slot_f[:, :], refused[:, :], ALU.add).then_inc(late, 1)
                dve.wait_ge(late, i * 8 + 5)
                dve.wait_ge(sent_ok, 1 + i)
                dve.tensor_copy(slot_s[:, :], slot_f[:, :]).then_inc(slot_ok, 1)
                dve.tensor_scalar(slot_g[:, :], slot_f[:, :], float(EXPERTS * CAP - 1), None, ALU.min).then_inc(late, 1)
                dve.wait_ge(lexp_ok, 1 + i + 1)
                dve.reciprocal(gate_r[:, :], esum[:, :]).then_inc(late, 1)
                dve.wait_ge(late, i * 8 + 7)
                dve.tensor_copy(slot[:, bass.ds(i * KC, KC)], slot_g[:, :])
                dve.tensor_tensor(gate[:, bass.ds(i * KC, KC)], gate_r[:, :], kept[:, :], ALU.mult).then_inc(late, 1)

            stats_1(0)
            norm_1(0)
            dve.wait_ge(w_in, 16 * N_W)
            dve.wait_ge(set_up, 5)
            spread_q(0)
            spread_v(0)
            for t in range(KC):
                shift_scores(0, t)
            stats_1(1)
            norm_1(1)
            for t in range(KC):
                sum_rows(0, t)

            def round(i, more=True):
                spread_q(i + 1)
                take_o(i, 0)
                take_o(i, 1)
                stats_2(i)
                norm_2(i)
                spread_v(i + 1)
                shift_scores(i + 1, 0)
                choose(i)
                shift_scores(i + 1, 1)
                sum_rows(i + 1, 0)
                if more:
                    stats_1(i + 2)
                sum_rows(i + 1, 1)
                if more:
                    norm_1(i + 2)
                give_slots(i)

            with dve.Fori(0, G - 2) as i:
                round(i)
            round(G - 2, more=False)
            for t in range(KC):
                take_o(G - 1, t)
            stats_2(G - 1)
            norm_2(G - 1)
            choose(G - 1)
            give_slots(G - 1)

        @block.tensor
        def _(pe):
            def turn(out, x):
                for c in range(KC):
                    for t in range(KC):
                        mm = pe.transpose(out[:, c * GT + t * P:c * GT + (t + 1) * P], x[:, t, c * P:(c + 1) * P], ident[:, :])
                return mm

            def turn_1(i):
                pe.wait_ge(xn_ok, i + 1)
                turn(xt_b, xn).then_inc(xt_full, 1)

            def project(i, w, out, done):
                pe.wait_ge(xt_ok, i + 1)
                for c in range(KC):
                    for kc in range(KC):
                        mm = pe.matmul(out[:, c * GT:(c + 1) * GT], w_self[:, w, kc, c * P:(c + 1) * P], xt[:, kc, :], start=(kc == 0), stop=(kc == KC - 1))
                mm.then_inc(done, 1)

            def values(i):
                for t in range(KC):
                    for kc in range(KC):
                        mm = pe.matmul(v_b[:, t * D:(t + 1) * D], xt[:, kc, t * P:(t + 1) * P], w_self[:, 2, kc, :], start=(kc == 0), stop=(kc == KC - 1))
                mm.then_inc(v_full, 1)

            def scores(i, t):
                pe.wait_ge(k_ok, (i + 1) * KC)
                pe.wait_ge(qbd_dve, 1 + i + 1)
                pe.wait_ge(qbd_act, i + 1)
                pe.wait_ge(qbd_pool, 1 + i + 1)
                for b in range(HR):
                    for r in range(RT):
                        at = (b * RT + r) * SQ
                        g = t * HR + b
                        mm = pe.matmul(s_b[t][:, at:at + SQ], q_bd[:, r // 2, g, HR * (r % 2):HR * (r % 2 + 1), :].rearrange("p h q -> p (h q)"),
                                       k_t[:, r // 2, g * SQ:(g + 1) * SQ], start=True, stop=True)
                mm.then_inc(sc_full, 1)

            def turn_prob(i, t):
                pe.wait_ge((lexp_ok, slot_ok)[t], 1 + i)
                pe.wait_ge(prob_ok, i * KC + t + 1)
                for b in range(HR):
                    mm = pe.transpose(pt_b[t][:, b * P:(b + 1) * P], prob[:, t, b * RT:(b + 1) * RT, :].rearrange("p r k -> p (r k)"), ident[:, :])
                mm.then_inc(pt_full, 1)

            def mix(i, t):
                pe.wait_ge(x2_ok, 1 + i * KC)
                pe.wait_ge(xt2_ok, 1 + i)
                pe.wait_ge(vbd_act, i + 1)
                pe.wait_ge(vbd_dve, i + 1)
                pe.wait_ge(pt_ok, i * KC + t + 1)
                for u in range(KC):
                    for b in range(HR):
                        mm = pe.matmul(o_b[t][u][:, b * P:(b + 1) * P], v_bd[:, t, b, u, :], p_t[:, t, b, :], start=True, stop=True)
                mm.then_inc(o_full, 1)

            def out_project(i):
                pe.wait_ge(ot_act, 1 + (i + 1) * KC)
                pe.wait_ge(ot_dve, 1 + (i + 1) * KC)
                for t in range(KC):
                    for u in range(KC):
                        mm = pe.matmul(f_b[:, t * D:(t + 1) * D], o_t[:, u, t].rearrange("p b q -> p (b q)"), w_f[:, u, :], start=(u == 0), stop=(u == KC - 1))
                mm.then_inc(f_full, 1)

            def turn_2(i):
                pe.wait_ge(xn2_ok, 1 + i + 1)
                turn(xt2_b, xn2).then_inc(xt2_full, 1)

            def router(i):
                pe.wait_ge(xt2_ok, 1 + i + 1)
                for t in range(KC):
                    for kc in range(KC):
                        mm = pe.matmul(l_b[:, t * EXPERTS:(t + 1) * EXPERTS], xt2[:, kc, t * P:(t + 1) * P], w_r[:, kc, :], start=(kc == 0), stop=(kc == KC - 1))
                mm.then_inc(l_full, 1)

            def count(i):
                pe.wait_ge(onehot_ok, i + 1)
                for j, w in enumerate((upto, ones)):
                    for t in range(KC):
                        at = (j * KC + t) * EXPERTS
                        mm = pe.matmul(n_b[:, at:at + EXPERTS], w[:, :], onehot[:, t, :], start=True, stop=True)
                mm.then_inc(n_full, 1)

            turn_1(0)
            pe.wait_ge(w_in, 16 * N_W)
            pe.wait_ge(set_up, 5)
            pe.wait_ge(wq_scaled, 2)
            project(0, 0, q_b, q_full)
            project(0, 1, k_b, k_full)
            values(0)
            for t in range(KC):
                scores(0, t)
            with pe.Fori(0, G - 1) as i:
                turn_1(i + 1)
                turn_prob(i, 0)
                project(i + 1, 0, q_b, q_full)
                turn_prob(i, 1)
                mix(i, 0)
                project(i + 1, 1, k_b, k_full)
                mix(i, 1)
                values(i + 1)
                out_project(i)
                scores(i + 1, 0)
                turn_2(i)
                scores(i + 1, 1)
                router(i)
                count(i)
            for t in range(KC):
                turn_prob(G - 1, t)
            for t in range(KC):
                mix(G - 1, t)
            out_project(G - 1)
            turn_2(G - 1)
            router(G - 1)
            count(G - 1)


def experts(nc, ins, scratch, gate, slot, ident, out):
    with ExitStack() as ctx:
        def sb(name, shape, dt=F32):
            return ctx.enter_context(nc.sbuf_tensor(name, shape, dt))

        def sem(name):
            return ctx.enter_context(nc.semaphore(name))

        NS = 2
        C2 = CAP - P
        w = [sb(f"w_expert{n}", [P, NS, KC, D]) for n in range(3)]
        rows = sb("rows", [P, NS, 2, D])
        bt = sb("bt", [P, NS, KC, CAP])
        ex = sb("ex", [P, NS, KC, CAP])
        act_t = sb("act_t", [P, NS, KC, CAP])
        y = sb("y", [P, NS, 2, D])
        z = sb("z_in", [P, NS, KC, D])
        yt = sb("y_rows", [P, NS, KC, D])
        o = sb("o_rows", [P, NS, KC, D])
        idx = sb("idx", [P, NS, KC], I32)
        gcol = sb("gcol", [P, NS, KC])
        idx_ok, gc_ok, passed = sem("idx_ok"), sem("gc_ok"), sem("passed3")
        bank = [ctx.enter_context(nc.psum_tensor(f"ebank{i}", [P, 512], F32)) for i in range(8)]
        bt_b, g_b, u_b, y_b = bank[0:2], bank[2:4], bank[4:6], bank[6:8]
        w_in = [sem(f"we_in{s}") for s in range(NS)]
        r_in = [sem(f"rows_in{s}") for s in range(NS)]
        y_out = [sem(f"y_out{s}") for s in range(NS)]
        z_in = [sem(f"z_in{s}") for s in range(NS)]
        y_in = [sem(f"yr_in{s}") for s in range(NS)]
        o_out = [sem(f"o_out{s}") for s in range(NS)]
        bt_full, bt_ok, gu_full, ex_ok, plus, inv, gate_ok, act_ok, y_full, y_ok, o_ok = (
            sem(n) for n in ("bt_full", "bt_ok", "gu_full", "ex_ok", "plus", "inv", "gated", "act_ok", "y_full", "y_ok", "o_ok"))
        block = ctx.enter_context(nc.Block())
        NE = EXPERTS // NS
        z_rows = scratch["z"].rearrange("(g c p) d -> g p c d", c=KC, p=P)
        o_rows = out.rearrange("(g b) s d -> g (b s) d", g=G).rearrange("g (c p) d -> g p c d", p=P)
        buf = scratch["buf"].rearrange("(e c) d -> e c d", c=CAP)
        yd = scratch["y"].rearrange("(e c) d -> e c d", c=CAP)

        started = (y_full, o_ok, *y_out, *o_out, y_ok)

        @block.sync
        def _(sp):
            for counter in started:
                sp.sem_inc(counter, 1)
            with sp.Fori(0, NE) as i:
                for s in range(NS):
                    e = i * NS + s
                    sp.wait_ge(y_full, 1 + i * NS)
                    for n, name in enumerate(("w_gate", "w_up", "w_down")):
                        sp.dma_start(w[n][:, s].rearrange("p c n -> p (c n)"),
                                     ins[name][bass.ds(e, 1)].rearrange("e (p c) n -> (e p) (c n)", c=KC)).then_inc(w_in[s], 16)
                    sp.dma_start(rows[:, s, 0, :], buf[bass.ds(e, 1), 0:P, :].rearrange("e c d -> (e c) d")).then_inc(r_in[s], 16)
                    sp.dma_start(rows[0:C2, s, 1, :], buf[bass.ds(e, 1), P:CAP, :].rearrange("e c d -> (e c) d")).then_inc(r_in[s], 16)
            for s in range(NS):
                sp.wait_ge(y_out[s], 1 + 32 * NE)
            with sp.Fori(0, G // NS) as i:
                for s in range(NS):
                    g = i * NS + s
                    sp.wait_ge(o_ok, 1 + i * NS)
                    sp.dma_start(z[:, s], z_rows[bass.ds(g, 1)].rearrange("g p c d -> p (g c) d")).then_inc(z_in[s], 16)
                for s in range(NS):
                    g = i * NS + s
                    sp.wait_ge(o_ok, 1 + g + 1)
                    sp.dma_start(o_rows[bass.ds(g, 1)].rearrange("g p c d -> p (g c) d"), o[:, s]).then_inc(o_out[s], 16)
            for s in range(NS):
                sp.wait_ge(o_out[s], 1 + 16 * (G // NS))

        @block.gpsimd
        def _(pool):
            for s in range(NS):
                pool.wait_ge(y_out[s], 1 + 32 * NE)
            with pool.Fori(0, G // NS) as i:
                for s in range(NS):
                    g = i * NS + s
                    pool.wait_ge(o_ok, 1 + i * NS)
                    for t in range(KC):
                        pool.tensor_copy(idx[:, s, t:t + 1], slot[:, bass.ds(g * KC + t, 1)]).then_inc(idx_ok, 1)
                        pool.wait_ge(idx_ok, g * KC + t + 1)
                        pool.sem_inc(passed, 1)
                        pool.indirect_dma_start(out=yt[:, s, t, :], out_offset=None, in_=scratch["y"],
                                                in_offset=bass.IndirectOffsetOnAxis(ap=idx[:, s, t:t + 1], axis=0),
                                                bounds_check=EXPERTS * CAP - 1, oob_is_err=False).then_inc(y_in[s], 16)

        @block.scalar
        def _(act):
            with act.Fori(0, NE) as i:
                for s in range(NS):
                    e = i * NS + s
                    act.wait_ge(bt_full, e + 1)
                    nc.scalar.activation(bt[:, s].rearrange("p c n -> p (c n)"), bt_b[s][:, 0:KC * CAP], ACT.Copy).then_inc(bt_ok, 1)
                for s in range(NS):
                    e = i * NS + s
                    act.wait_ge(gu_full, e + 1)
                    nc.scalar.activation(ex[:, s].rearrange("p c n -> p (c n)"), g_b[s][:, 0:KC * CAP], ACT.Exp, scale=-1.0).then_inc(ex_ok, 1)
                for s in range(NS):
                    e = i * NS + s
                    act.wait_ge(y_full, 1 + e + 1)
                    act.wait_ge(y_out[s], 1 + i * 32)
                    nc.scalar.activation(y[:, s, 0, :], y_b[s][:, 0:D], ACT.Copy)
                    nc.scalar.activation(y[0:C2, s, 1, :], y_b[s][0:C2, D:2 * D], ACT.Copy).then_inc(y_ok, 1)
                    act.wait_ge(y_ok, 1 + e + 1)
                    nc.scalar.dma_start(yd[bass.ds(e, 1), 0:P, :].rearrange("e c d -> (e c) d"), y[:, s, 0, :]).then_inc(y_out[s], 16)
                    nc.scalar.dma_start(yd[bass.ds(e, 1), P:CAP, :].rearrange("e c d -> (e c) d"), y[0:C2, s, 1, :]).then_inc(y_out[s], 16)

        @block.vector
        def _(dve):
            with dve.Fori(0, NE) as i:
                for s in range(NS):
                    e = i * NS + s
                    dve.wait_ge(ex_ok, e + 1)
                    dve.tensor_scalar(ex[:, s], ex[:, s], 1.0, None, ALU.add).then_inc(plus, 1)
                    dve.wait_ge(plus, e + 1)
                    dve.reciprocal(ex[:, s], ex[:, s]).then_inc(inv, 1)
                    dve.wait_ge(inv, e + 1)
                    dve.tensor_tensor(ex[:, s], g_b[s][:, 0:KC * CAP].rearrange("p (c n) -> p c n", c=KC), ex[:, s], ALU.mult).then_inc(gate_ok, 1)
                    dve.wait_ge(gate_ok, e + 1)
                    dve.tensor_tensor(act_t[:, s], u_b[s][:, 0:KC * CAP].rearrange("p (c n) -> p c n", c=KC), ex[:, s], ALU.mult).then_inc(act_ok, 1)
            with dve.Fori(0, G // NS) as i:
                for s in range(NS):
                    g = i * NS + s
                    dve.wait_ge(z_in[s], (i + 1) * 16)
                    dve.wait_ge(y_in[s], (i + 1) * 32)
                    dve.wait_ge(o_out[s], 1 + i * 16)
                    for t in range(KC):
                        dve.tensor_copy(gcol[:, s, t:t + 1], gate[:, bass.ds(g * KC + t, 1)]).then_inc(gc_ok, 1)
                    dve.wait_ge(gc_ok, (g + 1) * KC)
                    for t in range(KC):
                        op = dve.scalar_tensor_tensor(out=o[:, s, t, :], in0=yt[:, s, t, :], scalar=gcol[:, s, t:t + 1],
                                                      in1=z[:, s, t, :], op0=ALU.mult, op1=ALU.add)
                    op.then_inc(o_ok, 1)

        @block.tensor
        def _(pe):
            with pe.Fori(0, NE) as i:
                for s in range(NS):
                    e = i * NS + s
                    pe.wait_ge(r_in[s], (i + 1) * 32)
                    for c in range(KC):
                        pe.transpose(bt_b[s][:, c * CAP:c * CAP + P], rows[:, s, 0, c:D:KC], ident[:, :])
                        mm = pe.transpose(bt_b[s][:, c * CAP + P:(c + 1) * CAP], rows[0:C2, s, 1, c:D:KC], ident[0:C2, 0:C2])
                    mm.then_inc(bt_full, 1)
                for s in range(NS):
                    e = i * NS + s
                    pe.wait_ge(w_in[s], (i + 1) * 48)
                    pe.wait_ge(bt_ok, e + 1)
                    for n, b in ((0, g_b), (1, u_b)):
                        for f in range(KC):
                            for c in range(KC):
                                mm = pe.matmul(b[s][:, f * CAP:(f + 1) * CAP], w[n][:, s, c, f:D:KC], bt[:, s, c, :], start=(c == 0), stop=(c == KC - 1))
                    mm.then_inc(gu_full, 1)
                for s in range(NS):
                    e = i * NS + s
                    pe.wait_ge(act_ok, e + 1)
                    pe.wait_ge(y_ok, 1 + i * NS)
                    for f in range(KC):
                        pe.matmul(y_b[s][:, 0:D], act_t[:, s, f, 0:P], w[2][:, s, f, :], start=(f == 0), stop=(f == KC - 1))
                    for f in range(KC):
                        mm = pe.matmul(y_b[s][0:C2, D:2 * D], act_t[:, s, f, P:CAP], w[2][:, s, f, :], start=(f == 0), stop=(f == KC - 1))
                    mm.then_inc(y_full, 1)


def cross_weights(nc, ctx):
    def sb(name, shape, dt=F32R):
        return ctx.enter_context(nc.sbuf_tensor(name, shape, dt))

    return dict(wq=sb("w_q", [P, 2, KC * H * DK]), wkt=sb("w_kt", [P, 2, NP, D]), wv=sb("w_v", [P, 2, KC * H * DK]),
                wo=sb("w_o", [P, 2, NP * D]), cxt=sb("c_last_t", [P, 2, KC, NB]))


def constants():
    row = np.arange(NX)
    h4, q = np.divmod(np.arange(P), SQ)
    head = HR * np.arange(RT)[None, :] + h4[:, None]
    half = HS // 2
    base = np.float32(24.0 ** (1.0 / half))
    slopes = (np.float32(1.0) / base ** np.arange(1, half + 1, dtype=np.float32)).astype(np.float32)
    rel = (np.arange(SQ)[None, :] - q[:, None]).astype(np.float32)[:, None, :]
    slope = slopes[head % half][:, :, None]
    far = np.float32(-1e9)
    alibi = np.where((head < half)[:, :, None], np.where(rel <= 0, slope * rel, far), np.where(rel >= 0, -slope * rel, far))
    return {"ident": np.eye(P, dtype=np.float32),
            "mask": (row[:, None] % RT == np.arange(RT)[None, :]).astype(np.float32),
            "alibi": alibi.astype(np.float32),
            "head_mask": (np.arange(P)[:, None] // HD == np.arange(HC)[None, :]).astype(np.float32),
            "upto": np.triu(np.ones((P, P), np.float32)),
            "rank": np.tile(EXPERTS - np.arange(EXPERTS, dtype=np.float32), (P, 1))}


def perceiver(nc, ins, out):
    scratch = {"xnt": nc.dram_tensor("xnt_d", (G, P, 2 * KC * GT), F32, kind="Internal").ap(),
               "cx": nc.dram_tensor("cx_d", (2, NB, D), F32, kind="Internal").ap(),
               "x1": nc.dram_tensor("x1_d", (T, D), F32, kind="Internal").ap(),
               "z": nc.dram_tensor("z_d", (T, D), F32, kind="Internal").ap(),
               "buf": nc.dram_tensor("buf_d", (EXPERTS * CAP, D), F32, kind="Internal").ap(),
               "y": nc.dram_tensor("y_d", (EXPERTS * CAP, D), F32, kind="Internal").ap()}
    with ExitStack() as ctx:
        ident = ctx.enter_context(nc.sbuf_tensor("identity", [P, P], F32))
        gate = ctx.enter_context(nc.sbuf_tensor("gate", [P, T // P], F32))
        slot = ctx.enter_context(nc.sbuf_tensor("slot", [P, T // P], I32))
        with ExitStack() as first:
            weights = cross_weights(nc, first)
            prepare(nc, ins, scratch=scratch, ident=ident, **weights)
            cross_attention(nc, ins, scratch=scratch, ident=ident, **weights)
        self_attention(nc, ins, scratch, gate, slot, ident)
        experts(nc, ins, scratch, gate, slot, ident, out)


def order_small(arrays):
    out = dict(arrays)
    for name in ("s_bq", "s_bk"):
        out[name] = np.ascontiguousarray(arrays[name].reshape(KC, P).T)
    out["s_wf"] = np.ascontiguousarray(arrays["s_wf"].reshape(KC, 2, HR, HD, D).transpose(2, 1, 3, 0, 4).reshape(P, KC, D))
    out["s_bv"] = np.ascontiguousarray(arrays["s_bv"].reshape(KC, 2, HR, HD).transpose(2, 1, 3, 0).reshape(P, KC))
    return out


NAMES = {"x": "x", "ctx_1024": "ctx", "L0_xattn_W_Q": "wq", "L0_xattn_W_K": "wk", "L0_xattn_W_V": "wv", "L0_xattn_W_O": "wo",
         "L0_attn_Wq": "s_wq", "L0_attn_bq": "s_bq", "L0_attn_Wk": "s_wk", "L0_attn_bk": "s_bk", "L0_attn_Wv": "s_wv",
         "L0_attn_bv": "s_bv", "L0_attn_Wf": "s_wf", "L0_attn_bf": "s_bf", "L0_ffn_w_router": "w_router",
         "L0_ffn_w_gate": "w_gate", "L0_ffn_w_up": "w_up", "L0_ffn_w_down": "w_down"}


def kernel(**inputs):
    import concourse.bacc as bacc
    from concourse.bass_utils import run_bass_kernel_spmd

    nc = bacc.Bacc("TRN2", target_bir_lowering=False, num_devices=1)
    arrays = order_small({NAMES[name]: np.ascontiguousarray(inputs[name]) for name in NAMES})
    arrays.update(constants())
    ins = {name: nc.dram_tensor(f"in_{name}", a.shape, mybir.dt.from_np(a.dtype), kind="ExternalInput").ap()
           for name, a in arrays.items()}
    out = nc.dram_tensor("out", (NB, SQ, D), F32, kind="ExternalOutput").ap()
    perceiver(nc, ins, out)
    r = run_bass_kernel_spmd(nc, [{f"in_{name}": a for name, a in arrays.items()}], core_ids=[0])
    return r.results[0]["out"]
```

```python
from contextlib import ExitStack

import numpy as np

import concourse.bass as bass
from concourse import mybir

F32 = mybir.dt.float32
F32R = mybir.dt.float32r
I32 = mybir.dt.int32
U32 = mybir.dt.uint32
ALU = mybir.AluOpType
ACT = mybir.ActivationFunctionType
AX = mybir.AxisListType

P = 128
NB, SQ, D = 128, 32, 256
KC = D // P
T = NB * SQ
LK = 257
LM = LK - 1
H, DK = 16, 64
NP = H // 2
GB = 8
GT = GB * SQ
G = NB // GB
RT = H * SQ // P
HR = P // SQ
NX = 3 * RT
ZR = 8
EPS = 1e-5
PASSES = ((0, 0), (0, 1), (1, 0))


def fp(ap):
    return ap.bitcast(F32)


def prepare(nc, ins, wq, wkt, wv, wo, cxt, xnt, half, ident, scratch):
    with ExitStack() as ctx:
        def sb(name, shape, dt=F32):
            return ctx.enter_context(nc.sbuf_tensor(name, shape, dt))

        def sem(name):
            return ctx.enter_context(nc.semaphore(name))

        stage = sb("stage", [P, 4, KC * H * DK])
        x_in = sb("x_in", [P, KC, D])
        stats = sb("stats", [P, KC, 6])
        mean_var = sb("mean_var", [P, KC, 2])
        rstd = sb("rstd", [P, KC, 1])
        cx = sb("c_last", [P, D])
        cxs = sb("cxs", [P, 2, D], F32R)
        turn = [ctx.enter_context(nc.psum_tensor(f"turn{i}", [P, 512], F32)) for i in range(4)]
        wk_ps, x_ps, c_ps = turn[0:2], turn[2], turn[3]

        const_in, cx_in, x_ld = sem("const_in"), sem("cx_in"), sem("x_ld")
        w_in = [sem(f"w_in{i}") for i in range(4)]
        cx_out = sem("cx_out")
        w_hi = sem("w_hi")
        wk_turned, wk_hi, wk_lo = sem("wk_turned"), sem("wk_hi"), sem("wk_lo")
        cx_hi, cx_lo, cx_turned, cxt_hi = sem("cx_hi"), sem("cx_lo"), sem("cx_turned"), sem("cxt_hi")
        half_set, aggregated = sem("half_set"), sem("aggregated")
        moments, rstd_done = sem("moments"), sem("rstd_done")
        xn_done, x_turned, xnt_hi = sem("xn_done"), sem("x_turned"), sem("xnt_hi")
        block = ctx.enter_context(nc.Block())
        wview = stage[:, 1, :].rearrange("p (c h k) -> p c h k", c=KC, h=H)
        x_rows = ins["x"].rearrange("(g b) s d -> g (b s) d", g=G).rearrange("g (c p) d -> g p c d", p=P)

        @block.sync
        def _(sp):
            sp.dma_start(ident[:, :], ins["ident"]).then_inc(const_in, 16)
            sp.dma_start(stage[:, 1, :], ins["wk"]).then_inc(w_in[1], 16)
            sp.dma_start(stage[:, 0, :], ins["wq"]).then_inc(w_in[0], 16)
            sp.dma_start(stage[:, 2, :], ins["wv"]).then_inc(w_in[2], 16)
            sp.dma_start(stage[:, 3, :].rearrange("p (j n) -> p j n", n=D),
                         ins["wo"].rearrange("(j p) n -> p j n", p=P)).then_inc(w_in[3], 16)
            for half_no in range(2):
                sp.wait_ge(cx_hi if half_no == 0 else cx_lo, 1)
                sp.dma_start(scratch["cx"][half_no], fp(cxs[:, half_no, :])).then_inc(cx_out, 16)
            sp.wait_ge(cx_out, 32)

        @block.gpsimd
        def _(pool):
            pool.memset(half[:, :, :], -0.5).then_inc(half_set, 1)
            pool.wait_ge(half_set, 1)
            pool.wait_ge(moments, 1)
            pool.tensor_tensor(rstd[:, :, :], mean_var[:, :, 1:2], half[:, :, :], ALU.pow).then_inc(rstd_done, 1)

        @block.scalar
        def _(act):
            nc.scalar.dma_start(cx[:, :], ins["ctx"][:, LM, :]).then_inc(cx_in, 16)
            nc.scalar.dma_start(x_in[:, :, :], x_rows[0]).then_inc(x_ld, 16)
            act.wait_ge(cx_in, 16)
            nc.scalar.activation(cxs[:, 0, :], cx[:, :], ACT.Copy).then_inc(cx_hi, 1)
            act.wait_ge(cx_turned, 1)
            nc.scalar.activation(cxt[:, 0, :, :], c_ps[:, 0:KC * NB], ACT.Copy).then_inc(cxt_hi, 1)
            for p in range(NP):
                act.wait_ge(wk_turned, p + 1)
                nc.scalar.activation(wkt[:, 0, p, :], wk_ps[p % 2][:, 0:D], ACT.Copy).then_inc(wk_hi, 1)
            act.wait_ge(w_in[0], 16)
            nc.scalar.activation(wq[:, 0, :], stage[:, 0, :], ACT.Copy, scale=DK ** -0.5).then_inc(w_hi, 1)
            act.wait_ge(x_turned, 1)
            nc.scalar.activation(xnt[:, 0], x_ps[:, :], ACT.Copy).then_inc(xnt_hi, 1)
            act.wait_ge(w_in[2], 16)
            nc.scalar.activation(wv[:, 0, :], stage[:, 2, :], ACT.Copy).then_inc(w_hi, 1)
            act.wait_ge(w_in[3], 16)
            nc.scalar.activation(wo[:, 0, :], stage[:, 3, :], ACT.Copy).then_inc(w_hi, 1)

        @block.vector
        def _(dve):
            dve.wait_ge(cx_hi, 1)
            dve.tensor_tensor(cxs[:, 1, :], cx[:, :], fp(cxs[:, 0, :]), ALU.subtract).then_inc(cx_lo, 1)
            dve.wait_ge(cxt_hi, 1)
            dve.tensor_tensor(cxt[:, 1, :, :].rearrange("p c b -> p (c b)"), c_ps[:, 0:KC * NB],
                              fp(cxt[:, 0, :, :]).rearrange("p c b -> p (c b)"), ALU.subtract).then_inc(cx_lo, 1)
            dve.wait_ge(x_ld, 16)
            for c in range(KC):
                dve.bn_stats(stats[:, c, :], x_in[:, c, :])
            dve.drain()
            for c in range(KC):
                op = dve.bn_aggr(mean_var[:, c, :], stats[:, c, :])
            op.then_inc(aggregated, 1)
            dve.wait_ge(aggregated, 1)
            dve.tensor_scalar(mean_var[:, :, 1], mean_var[:, :, 1], EPS, None, ALU.add).then_inc(moments, 1)
            dve.wait_ge(rstd_done, 1)
            for c in range(KC):
                op = dve.tensor_scalar(x_in[:, c, :], x_in[:, c, :], mean_var[:, c, 0:1], rstd[:, c, :], ALU.subtract, ALU.mult)
            op.then_inc(xn_done, 1)
            for p in range(NP):
                dve.wait_ge(wk_hi, p + 1)
                dve.tensor_tensor(wkt[:, 1, p, :], wk_ps[p % 2][:, 0:D], fp(wkt[:, 0, p, :]), ALU.subtract).then_inc(wk_lo, 1)
            for n, (w, i, k) in enumerate(((wq, 0, DK ** -0.5), (wv, 2, 1.0), (wo, 3, 1.0))):
                dve.wait_ge(w_hi, n + 1)
                dve.scalar_tensor_tensor(out=w[:, 1, :], in0=stage[:, i, :], scalar=k, in1=fp(w[:, 0, :]),
                                         op0=ALU.mult, op1=ALU.subtract)
                if n == 0:
                    dve.wait_ge(xnt_hi, 1)
                    dve.tensor_tensor(xnt[:, 1].rearrange("p c t -> p (c t)"), x_ps[:, :],
                                      fp(xnt[:, 0]).rearrange("p c t -> p (c t)"), ALU.subtract)

        @block.tensor
        def _(pe):
            pe.wait_ge(const_in, 16)
            pe.wait_ge(cx_in, 16)
            for c in range(KC):
                mm = pe.transpose(c_ps[:, c * NB:(c + 1) * NB], cx[:, c * P:(c + 1) * P], ident[:, :])
            mm.then_inc(cx_turned, 1)
            pe.wait_ge(w_in[1], 16)
            for p in range(NP):
                if p >= 2:
                    pe.wait_ge(wk_lo, p - 1)
                for c in range(KC):
                    mm = pe.transpose(wk_ps[p % 2][:, c * P:(c + 1) * P], wview[:, c, 2 * p:2 * p + 2, :], ident[:, :])
                mm.then_inc(wk_turned, 1)
            pe.wait_ge(xn_done, 1)
            for c in range(KC):
                for t in range(KC):
                    mm = pe.transpose(x_ps[:, c * GT + t * P:c * GT + (t + 1) * P], x_in[:, t, c * P:(c + 1) * P], ident[:, :])
            mm.then_inc(x_turned, 1)


def cross_attention(nc, ins, wq, wkt, wv, wo, cxt, xnt, half, ident, scratch):
    with ExitStack() as ctx:
        def sb(name, shape, dt=F32):
            return ctx.enter_context(nc.sbuf_tensor(name, shape, dt))

        def sem(name):
            return ctx.enter_context(nc.semaphore(name))

        def psum(name):
            return [ctx.enter_context(nc.psum_tensor(f"{name}{i}", [P, 512], F32)) for i in range(2)]

        xn = sb("x_next", [P, KC, D])
        stats = sb("next_stats", [P, KC, 6])
        mean_var = sb("next_mean_var", [P, KC, 2])
        rstd = sb("next_rstd", [P, KC, 1])
        qt = sb("qt", [P, 2, 2, GT], F32R)
        qu = sb("qu", [P, 2, KC, GB, H, SQ], F32R)
        craw = sb("craw", [P, 2, KC, D])
        cs = sb("cs", [P, 2, 2, KC, D], F32R)
        ct = sb("ct", [P, 2, 2, KC, LM + 2], F32R)
        prob = sb("prob", [P, 2, RT, LK])
        negmax = sb("negmax", [P, 2, RT])
        rowsum = sb("rowsum", [P, 2, RT])
        rinv = sb("rinv", [P, 2, RT])
        pxh = sb("pxh", [P, RT], F32R)
        px = sb("px", [P, NX])
        pt = sb("pt", [P, 2, KC, 512], F32R)
        xp = sb("xp", [NX, RT, P], F32R)
        cxg = sb("cxg", [NX, GB, D], F32R)
        mask = sb("row_mask", [NX, RT])
        heads = sb("heads", [P, 2, NP, GT], F32R)
        xg = sb("xg", [P, KC, D])

        s_bank, pt_bank, u_bank, m_bank = psum("s_bank"), psum("pt_bank"), psum("u_bank"), psum("m_bank")
        order = {"s": [], "pt": [], "u": [], "m": []}
        ahead = [("ct", 0), ("q", 0), ("q", 1), ("d", 0), ("d", 1)]
        LB = 5
        early = {7: 0, 11: 1, H - 1: 2}
        order["m"] += [("q", p) for p in range(2, NP)]
        for h in range(2, H):
            order["su"[h // 2 % 2]].append(("d", h))
            if h in early:
                order["s"].append(("s", 0, early[h]))
        for b in range(GB):
            order["s"] += [("s", b, r) for r in range(RT) if (b, r) not in [(0, r) for r in early.values()]]
            order["pt"] += [("pt", b, c) for c in range(KC)]
            order["u"] += [("u", b, d) for d in range(KC)]
            order["m"] += [("px", b - 1)] * (b >= 1) + [("ct", b + 1)] * (b + 1 < GB) + [("xt", 0), ("xt", 1)] * (b == LB)
        order["m"] += [("px", GB - 1)] + ahead[0:3] + [("out", 0), ("out", 1)]
        for p in range(NP):
            order[("s", "pt")[p % 2]].append(("e", p))
        order["s"] += ahead[3:5]
        assert all(len(o) % 2 == 0 for o in order.values())
        banks = {"s": s_bank, "pt": pt_bank, "u": u_bank, "m": m_bank}
        ring = {what: (name, n) for name, o in order.items() for n, what in enumerate(o)}

        def bank_of(what):
            name, n = ring[what]
            return banks[name][n % 2]

        def held(what, like):
            v = bank_of(what)[:, 0:like.free_size()]
            if len(like.shape) == 3:
                v = v.rearrange("p (a b) -> p a b", a=like.shape[1])
            elif len(like.shape) == 4:
                v = v.rearrange("p (a b c) -> p a b c", a=like.shape[1], b=like.shape[2])
            return v

        fills = {name: sem(f"{name}_filled") for name in order}
        empties = {name: sem(f"{name}_emptied") for name in order}

        first_fills = {"s": len(order["s"]) - 2, "pt": len(order["pt"]), "u": len(order["u"]), "m": len(order["m"]) - 5}

        def filled(g, what, back=0):
            name, n = ring[what]
            return fills[name], (g + 1 - back - (what in ahead)) * len(order[name]) + n + 1

        def bank_free(g, what):
            name, n = ring[what]
            return empties[name], (g + 1 - (what in ahead)) * len(order[name]) + n + 1

        def emptied(g, what):
            name, n = ring[what]
            return empties[name], (g + 1 - (what in ahead)) * len(order[name]) + n + 3

        def fills_of(what):
            return fills[ring[what][0]]

        def empties_of(what):
            return empties[ring[what][0]]

        mask_in, cx_in, x_in, x_out, xn_in = sem("mask_in"), sem("g_cx_in"), sem("g_x_in"), sem("g_x_out"), sem("xn_in")
        aggregated, moments, rstd_done, xn_done, xt_hi = sem("aggregated1"), sem("moments1"), sem("rstd_done1"), sem("xn_done1"), sem("xt_hi")
        c_in = [sem(f"c_in{i}") for i in range(2)]
        pad_set, passed, passed_sp = sem("pad_set"), sem("passed1"), sem("passed_sp")
        s_max, p_scaled, p_inv = sem("s_max"), sem("p_scaled"), sem("p_inv")
        ct_hi, q_hi, d_hi, pt_hi, u_hi, e_hi = (sem(f"{n}_hi") for n in ("ct", "q", "d", "pt", "u", "e"))
        c_hi, c_split, ct_last = sem("c_hi"), sem("c_split"), sem("ct_last")
        px_hi, px_done = sem("px_hi"), sem("px_done")
        block = ctx.enter_context(nc.Block())

        x_rows = ins["x"].rearrange("(g b) s d -> g (b s) d", g=G).rearrange("g (c p) d -> g p c d", p=P)
        x1_rows = scratch["x1"].rearrange("(g c p) d -> g p c d", c=KC, p=P)
        ctx_rows = ins["ctx"].rearrange("b k d -> b (k d)")
        def two_ago(b):
            return (b - 2) % GB, int(b < 2)

        @block.sync
        def _(sp):
            def store_x1(g):
                sp.wait_ge(*emptied(g, ("out", 1)))
                sp.sem_inc(passed_sp, 1)
                sp.dma_start(x1_rows[bass.ds(g, 1)].rearrange("g p c d -> p (g c) d"), xg[:, :, :]).then_inc(x_out, 16)

            def group(g, first=False, last=False):
                for b in range(GB):
                    sp.wait_ge(c_split, (g + 1) * GB + b - 1)
                    sp.sem_inc(passed_sp, 1)
                    if not (first and b < 2):
                        sp.wait_ge(*filled(g, ("ct", two_ago(b)[0]), two_ago(b)[1]))
                        sp.sem_inc(passed_sp, 1)
                    sp.dma_start(craw[:, b % 2, :, :].rearrange("p c d -> p (c d)"),
                                 ctx_rows[bass.ds(g * GB + b, 1), 0:LM * D].rearrange("b (p n) -> (b p) n", p=P)
                                 ).then_inc(c_in[b % 2], 16)
                    if b == 1:
                        if not first:
                            sp.wait_ge(*filled(g, ("xt", 1), 1))
                            sp.sem_inc(passed_sp, 1)
                        sp.dma_start(xn[:, :, :], x_rows[bass.ds(g if last else g + 1, 1)].rearrange("g p c d -> p (g c) d")).then_inc(xn_in, 16)
                        if not first:
                            sp.wait_ge(*filled(g, ("u", GB - 1, KC - 1), 1))
                        for t, part in enumerate((0, 0, 1)):
                            sp.dma_start(fp(cxg[t * RT:(t + 1) * RT, :, :]),
                                         scratch["cx"][part, bass.ds(g * GB, GB), :].partition_broadcast(RT)
                                         ).then_inc(cx_in, 16)
                    if b == 2 and not first:
                        store_x1(g - 1)
                    if b == 3:
                        if not first:
                            sp.wait_ge(x_out, g * 16)
                        sp.dma_start(xg[:, :, :], x_rows[bass.ds(g, 1)].rearrange("g p c d -> p (g c) d")).then_inc(x_in, 16)

            sp.dma_start(mask[:, :], ins["mask"]).then_inc(mask_in, 16)
            group(0, first=True)
            with sp.Fori(1, G - 1) as g:
                group(g)
            group(G - 1, last=True)
            store_x1(G - 1)
            sp.wait_ge(x_out, G * 16)

        @block.gpsimd
        def _(pool):
            pool.memset(fp(ct[:, :, :, :, LM + 1:LM + 2]), 0.0).then_inc(pad_set, 1)
            pool.sem_inc(c_split, GB)
            with pool.Fori(0, G) as g:
                def split_c(b):
                    s = b % 2
                    pool.wait_ge(c_hi, g * GB + b + 1)
                    pool.tensor_tensor(cs[:, s, 1, :, :], craw[:, s, :, :], fp(cs[:, s, 0, :, :]), ALU.subtract).then_inc(c_split, 1)

                def last_row(b):
                    pool.wait_ge(*filled(g, ("s", two_ago(b)[0], RT - 1), two_ago(b)[1]))
                    pool.sem_inc(passed, 1)
                    pool.tensor_copy(ct[:, b % 2, :, :, LM], fp(cxt[:, :, :, bass.ds(g * GB + b, 1)]).rearrange("p a c b -> p a (c b)")).then_inc(ct_last, 1)

                def scale(b):
                    pool.wait_ge(p_inv, g * GB + b + 1)
                    pool.tensor_tensor(prob[:, b % 2], prob[:, b % 2], rinv[:, b % 2, :].unsqueeze(2).broadcast_to([P, RT, LK]),
                                       ALU.mult).then_inc(p_scaled, 1)

                def last_prob(b):
                    pool.wait_ge(p_scaled, g * GB + b + 1)
                    pool.wait_ge(*filled(g, ("px", (b - 1) % GB), int(b == 0)))
                    pool.sem_inc(passed, 1)
                    pool.tensor_copy(pxh[:, :], prob[:, b % 2, :, LM]).then_inc(px_hi, 1)
                    pool.wait_ge(px_hi, g * GB + b + 1)
                    pool.sem_inc(passed, 1)
                    pool.tensor_copy(px[:, 0:RT], fp(pxh[:, :]))
                    pool.tensor_copy(px[:, 2 * RT:3 * RT], fp(pxh[:, :]))
                    pool.tensor_tensor(px[:, RT:2 * RT], prob[:, b % 2, :, LM], fp(pxh[:, :]), ALU.subtract).then_inc(px_done, 1)

                def rstd_next():
                    pool.wait_ge(moments, g + 1)
                    pool.tensor_tensor(rstd[:, :, :], mean_var[:, :, 1:2], half[:, :, :], ALU.pow).then_inc(rstd_done, 1)

                last_row(0)
                last_row(1)
                split_c(0)
                for b in range(GB):
                    if 0 < b < GB - 1:
                        scale(b)
                    if b + 2 < GB:
                        last_row(b + 2)
                    last_prob(b)
                    if b + 1 < GB:
                        split_c(b + 1)
                    if b == LB - 2:
                        rstd_next()

        @block.scalar
        def _(act):
            act.sem_inc(empties["m"], first_fills["m"] + 2)

            def high(g, out, what, done):
                act.wait_ge(*filled(g, what))
                nc.scalar.activation(out, held(what, out), ACT.Copy).then_inc(done, 1)

            def q_high(g, p):
                high(g, qt[:, p % 2, 0, :], ("q", p), q_hi)

            def d_high(g, h):
                high(g, qu[:, 0, :, :, h, :], ("d", h), d_hi)

            def ct_high(g, b):
                high(g, ct[:, b % 2, 0, :, 0:LM], ("ct", b), ct_hi)

            def group(g, last=False):
                def c_high(b):
                    s = b % 2
                    act.wait_ge(c_in[s], (g * (GB // 2) + b // 2 + 1) * 16)
                    act.wait_ge(*filled(g, ("u", two_ago(b)[0], KC - 1), two_ago(b)[1]))
                    nc.scalar.activation(cs[:, s, 0, :, :], craw[:, s, :, :], ACT.Copy).then_inc(c_hi, 1)

                def exps(b, r):
                    act.wait_ge(s_max, g * GB * RT + RT * b + r + 1)
                    act.wait_ge(*filled(g, ("px", two_ago(b)[0]), two_ago(b)[1]))
                    nc.scalar.activation(prob[:, b % 2, r, :], bank_of(("s", b, r))[:, 0:LK], ACT.Exp, bias=negmax[:, b % 2, r:r + 1],
                                         accum_out=rowsum[:, b % 2, r:r + 1]).then_inc(empties["s"], 1)

                c_high(0)
                for p in range(2, NP):
                    q_high(g, p)
                    if 2 * p - 3 in early:
                        exps(0, early[2 * p - 3])
                    d_high(g, 2 * p - 2)
                    d_high(g, 2 * p - 1)
                ct_high(g, 1)
                d_high(g, H - 2)
                d_high(g, H - 1)
                exps(0, early[H - 1])
                for b in range(GB + 1):
                    if 0 < b < GB:
                        exps(b, 0)
                        c_high(b)
                        exps(b, 1)
                    if b == LB + 1:
                        for c in range(KC):
                            high(g, xnt[:, 0, c, :], ("xt", c), xt_hi)
                    if b:
                        high(g, pt[:, 0, 0, :], ("pt", b - 1, 0), pt_hi)
                        high(g, pt[:, 0, 1, :], ("pt", b - 1, 1), pt_hi)
                    if 0 < b < GB:
                        exps(b, 2)
                    if b < GB:
                        exps(b, 3)
                    if 0 < b < GB - 1:
                        ct_high(g, b + 1)
                    if b == GB and not last:
                        ct_high(g + 1, 0)
                    if b:
                        for d in range(KC):
                            high(g, qu[:, 0, d, b - 1, :, :].rearrange("p h q -> p (h q)"), ("u", b - 1, d), u_hi)
                if not last:
                    q_high(g + 1, 0)
                    q_high(g + 1, 1)
                for p in range(NP):
                    act.wait_ge(*filled(g, ("e", p)))
                    for s in range(2):
                        r = slice(s * DK, (s + 1) * DK)
                        op = nc.scalar.activation(heads[r, 0, p, :], bank_of(("e", p))[r, s * GT:(s + 1) * GT], ACT.Copy)
                    op.then_inc(e_hi, 1)
                if not last:
                    d_high(g + 1, 0)
                    d_high(g + 1, 1)

            ct_high(0, 0)
            q_high(0, 0)
            q_high(0, 1)
            d_high(0, 0)
            d_high(0, 1)
            with act.Fori(0, G - 1) as g:
                group(g)
            group(G - 1, last=True)

        @block.vector
        def _(dve):
            for name in ("s", "pt", "u"):
                dve.sem_inc(empties[name], first_fills[name] + 2)
            dve.wait_ge(mask_in, 16)

            def low(out, hi, what, hi_sem, hi_count):
                dve.wait_ge(hi_sem, hi_count)
                dve.tensor_tensor(out, held(what, out), fp(hi), ALU.subtract).then_inc(empties_of(what), 1)

            def ct_low(g, b):
                low(ct[:, b % 2, 1, :, 0:LM], ct[:, b % 2, 0, :, 0:LM], ("ct", b), ct_hi, g * GB + b + 1)

            def q_low(g, p):
                low(qt[:, p % 2, 1, :], qt[:, p % 2, 0, :], ("q", p), q_hi, g * NP + p + 1)

            def d_low(g, h):
                low(qu[:, 1, :, :, h, :], qu[:, 0, :, :, h, :], ("d", h), d_hi, g * H + h + 1)

            def group(g, last=False):
                def maxs(b, r):
                    dve.wait_ge(*filled(g, ("s", b, r)))
                    dve.tensor_reduce(negmax[:, b % 2, r:r + 1], bank_of(("s", b, r))[:, 0:LK], AX.X, ALU.max, negate=True).then_inc(s_max, 1)

                def invert(b):
                    dve.wait_ge(*emptied(g, ("s", b, RT - 1)))
                    dve.reciprocal(rinv[:, b % 2, :], rowsum[:, b % 2, :]).then_inc(p_inv, 1)

                def p_low(b, c):
                    low(pt[:, 1, c, :], pt[:, 0, c, :], ("pt", b, c), pt_hi, (g * GB + b) * KC + c + 1)

                def u_low(b, d):
                    hi, lo = (qu[:, i, d, b, :, :].rearrange("p h q -> p (h q)") for i in range(2))
                    low(lo, hi, ("u", b, d), u_hi, (g * GB + b) * KC + d + 1)

                def spread_px(b):
                    dve.wait_ge(*filled(g, ("px", b)))
                    dve.tensor_tensor(xp[:, :, :], bank_of(("px", b))[0:NX, 0:P].unsqueeze(1).broadcast_to([NX, RT, P]),
                                      mask[:, :].unsqueeze(2).broadcast_to([NX, RT, P]), ALU.mult).then_inc(empties["m"], 1)

                for p in range(2, NP):
                    if 2 * p - 3 in early:
                        maxs(0, early[2 * p - 3])
                    q_low(g, p)
                    d_low(g, 2 * p - 2)
                    d_low(g, 2 * p - 1)
                ct_low(g, 1)
                d_low(g, H - 2)
                d_low(g, H - 1)
                maxs(0, early[H - 1])
                for b in range(GB + 1):
                    if 0 < b < GB:
                        maxs(b, 0)
                        maxs(b, 1)
                    if b > 1:
                        u_low(b - 2, 1)
                    if b == LB + 1:
                        for c in range(KC):
                            low(xnt[:, 1, c, :], xnt[:, 0, c, :], ("xt", c), xt_hi, g * KC + c + 1)
                    if 0 < b < GB:
                        maxs(b, 2)
                    if b:
                        p_low(b - 1, 0)
                    if b < GB:
                        maxs(b, 3)
                    if b:
                        spread_px(b - 1)
                    if b:
                        p_low(b - 1, 1)
                    if b < GB:
                        invert(b)
                    if b in (0, GB - 1):
                        dve.wait_ge(p_inv, g * GB + b + 1)
                        for r in range(RT):
                            op = dve.tensor_scalar(prob[:, b % 2, r, :], prob[:, b % 2, r, :], rinv[:, b % 2, r:r + 1], None, ALU.mult)
                        op.then_inc(p_scaled, 1)
                    if 0 < b < GB - 1:
                        ct_low(g, b + 1)
                    if b == GB and not last:
                        ct_low(g + 1, 0)
                    if b == LB - 2:
                        dve.wait_ge(xn_in, (g + 1) * 16)
                        for c in range(KC):
                            dve.bn_stats(stats[:, c, :], xn[:, c, :])
                        dve.drain()
                        for c in range(KC):
                            op = dve.bn_aggr(mean_var[:, c, :], stats[:, c, :])
                        op.then_inc(aggregated, 1)
                        dve.wait_ge(aggregated, g + 1)
                        dve.tensor_scalar(mean_var[:, :, 1], mean_var[:, :, 1], EPS, None, ALU.add).then_inc(moments, 1)
                    if b == LB - 1:
                        dve.wait_ge(rstd_done, g + 1)
                        for c in range(KC):
                            op = dve.tensor_scalar(xn[:, c, :], xn[:, c, :], mean_var[:, c, 0:1], rstd[:, c, :], ALU.subtract, ALU.mult)
                        op.then_inc(xn_done, 1)
                    if b:
                        u_low(b - 1, 0)
                u_low(GB - 1, 1)
                if not last:
                    q_low(g + 1, 0)
                    q_low(g + 1, 1)
                for p in range(NP):
                    dve.wait_ge(e_hi, g * NP + p + 1)
                    for s in range(2):
                        r = slice(s * DK, (s + 1) * DK)
                        op = dve.tensor_tensor(heads[r, 1, p, :], bank_of(("e", p))[r, s * GT:(s + 1) * GT],
                                               fp(heads[r, 0, p, :]), ALU.subtract)
                    op.then_inc(empties_of(("e", p)), 1)
                if not last:
                    d_low(g + 1, 0)
                    d_low(g + 1, 1)
                dve.wait_ge(x_in, (g + 1) * 16)
                for t in range(KC):
                    dve.wait_ge(*filled(g, ("out", t)))
                    dve.tensor_tensor(xg[:, t, :], bank_of(("out", t))[:, 0:D], xg[:, t, :], ALU.add).then_inc(empties["m"], 1)

            ct_low(0, 0)
            q_low(0, 0)
            q_low(0, 1)
            d_low(0, 0)
            d_low(0, 1)
            with dve.Fori(0, G - 1) as g:
                group(g)
            group(G - 1, last=True)

        @block.tensor
        def _(pe):
            pe.wait_ge(pad_set, 1)
            for name in order:
                pe.sem_inc(fills[name], first_fills[name])
            def product(out, terms, first=True, last=True):
                for i, (w, m) in enumerate(terms):
                    mm = pe.matmul(out, w, m, start=first and i == 0, stop=last and i == len(terms) - 1)
                return mm

            def turn_c(g, b):
                out = bank_of(("ct", b))
                pe.wait_ge(c_in[b % 2], (g * (GB // 2) + b // 2 + 1) * 16)
                pe.wait_ge(*bank_free(g, ("ct", b)))
                for d in range(KC):
                    for c in range(KC):
                        mm = pe.transpose(out[:, d * LM + c * P:d * LM + (c + 1) * P],
                                          craw[:, b % 2, c, d * P:(d + 1) * P], ident[:, :])
                mm.then_inc(fills["m"], 1)

            def project_q(g, p):
                pe.wait_ge(*bank_free(g, ("q", p)))
                product(bank_of(("q", p))[:, 0:GT],
                        [(wq[:, i, c * H * DK + p * P:c * H * DK + (p + 1) * P], xnt[:, j, c, :])
                         for i, j in PASSES for c in range(KC)]).then_inc(fills["m"], 1)

            def q_to_context(g, p):
                pe.wait_ge(*emptied(g, ("q", p)))
                for s in range(2):
                    h, r = 2 * p + s, slice(s * DK, (s + 1) * DK)
                    pe.wait_ge(*bank_free(g, ("d", h)))
                    for c in range(KC):
                        mm = product(bank_of(("d", h))[:, c * GT:(c + 1) * GT],
                                     [(wkt[r, i, p, c * P:(c + 1) * P], qt[r, p % 2, j, :]) for i, j in PASSES])
                    mm.then_inc(fills_of(("d", h)), 1)

            def group(g, last=False):
                def scores(b, r):
                    if r == 0:
                        pe.wait_ge(*emptied(g, ("ct", b)))
                        pe.wait_ge(ct_last, g * GB + b + 1)
                    if b == 0:
                        pe.wait_ge(*emptied(g, ("d", HR * r + 1)))
                        pe.wait_ge(*emptied(g, ("d", HR * r + 3)))
                    pe.wait_ge(*bank_free(g, ("s", b, r)))
                    product(bank_of(("s", b, r))[:, 0:LM + 2],
                            [(qu[:, i, c, b, HR * r:HR * (r + 1), :].rearrange("p h q -> p (h q)"), ct[:, b % 2, j, c, :])
                             for i, j in PASSES for c in range(KC)]).then_inc(fills["s"], 1)

                def turn_p(b, c):
                    out = bank_of(("pt", b, c))
                    pe.wait_ge(p_scaled, g * GB + b + 1)
                    pe.wait_ge(*bank_free(g, ("pt", b, c)))
                    for r in range(RT):
                        mm = pe.transpose(out[:, r * P:(r + 1) * P], prob[:, b % 2, r, c * P:(c + 1) * P], ident[:, :])
                    mm.then_inc(fills["pt"], 1)

                def turn_px(b):
                    pe.wait_ge(px_done, g * GB + b + 1)
                    pe.wait_ge(*bank_free(g, ("px", b)))
                    pe.transpose(bank_of(("px", b))[0:NX, 0:P], px[:, :], ident[:, :]).then_inc(fills["m"], 1)

                def attend(b):
                    outs = [bank_of(("u", b, d))[:, :] for d in range(KC)]
                    for c in range(KC):
                        pe.wait_ge(pt_hi, (g * GB + b) * KC + c + 1)
                        for d, out in enumerate(outs):
                            if c == 0 and d == 0:
                                pe.wait_ge(c_split, (g + 1) * GB + b + 1)
                                if b == 0:
                                    pe.wait_ge(cx_in, (g + 1) * 48)
                            if c == 0:
                                pe.wait_ge(*bank_free(g, ("u", b, d)))
                            product(out, [(cs[:, b % 2, i, c, d * P:(d + 1) * P], pt[:, 0, c, :]) for i in range(2)], first=(c == 0), last=False)
                    pe.wait_ge(*emptied(g, ("px", b)))
                    pe.wait_ge(*emptied(g, ("pt", b, KC - 1)))
                    for d, out in enumerate(outs):
                        dd = slice(d * P, (d + 1) * P)
                        product(out, [(cxg[:, b, dd], xp[:, :, :].rearrange("t r n -> t (r n)"))]
                                + [(cs[:, b % 2, 0, c, dd], pt[:, 1, c, :]) for c in range(KC)], first=False).then_inc(fills["u"], 1)

                for p in range(1, NP):
                    if p + 1 < NP:
                        project_q(g, p + 1)
                    q_to_context(g, p)
                    if p == NP - 2:
                        turn_c(g, 1)
                    if 2 * p + 1 in early:
                        scores(0, early[2 * p + 1])
                for b in range(GB + 1):
                    if 0 < b < GB:
                        scores(b, 0)
                        scores(b, 1)
                    if b:
                        turn_p(b - 1, 0)
                        turn_p(b - 1, 1)
                    if 0 < b < GB:
                        scores(b, 2)
                    if b < GB:
                        scores(b, 3)
                    if b:
                        turn_px(b - 1)
                    if 0 < b < GB - 1:
                        turn_c(g, b + 1)
                    if b == GB and not last:
                        turn_c(g + 1, 0)
                    if b:
                        attend(b - 1)
                    if b == LB:
                        pe.wait_ge(xn_done, g + 1)
                        for c in range(KC):
                            pe.wait_ge(*bank_free(g, ("xt", c)))
                            for t in range(KC):
                                mm = pe.transpose(bank_of(("xt", c))[:, t * P:(t + 1) * P], xn[:, t, c * P:(c + 1) * P], ident[:, :])
                            mm.then_inc(fills["m"], 1)
                if not last:
                    pe.wait_ge(*emptied(g, ("xt", 1)))
                    project_q(g + 1, 0)
                    project_q(g + 1, 1)
                else:
                    pe.sem_inc(fills["m"], 3)
                    pe.sem_inc(empties["m"], 3)
                for p in range(NP):
                    if p == 0:
                        pe.wait_ge(*emptied(g, ("u", GB - 1, KC - 1)))
                    pe.wait_ge(*bank_free(g, ("e", p)))
                    product(bank_of(("e", p))[:, :],
                            [(wv[:, i, c * H * DK + p * P:c * H * DK + (p + 1) * P],
                              qu[:, j, c, :, 2 * p:2 * p + 2, :].rearrange("p b h q -> p h b q"))
                             for i, j in PASSES for c in range(KC)]).then_inc(fills_of(("e", p)), 1)
                if not last:
                    q_to_context(g + 1, 0)
                pe.wait_ge(*emptied(g, ("e", NP - 2)))
                pe.wait_ge(*emptied(g, ("e", NP - 1)))
                for t in range(KC):
                    pe.wait_ge(*bank_free(g, ("out", t)))
                    product(bank_of(("out", t))[:, 0:D],
                            [(heads[:, i, p, t * P:(t + 1) * P], wo[:, j, p * D:(p + 1) * D])
                             for i, j in PASSES for p in range(NP)]).then_inc(fills["m"], 1)

            turn_c(0, 0)
            project_q(0, 0)
            project_q(0, 1)
            q_to_context(0, 0)
            pe.wait_ge(*emptied(0, ("q", 1)))
            pe.sem_inc(fills["m"], 2)
            pe.sem_inc(empties["m"], 2)
            with pe.Fori(0, G - 1) as g:
                group(g)
            group(G - 1, last=True)


EXPERTS, CAP = 32, 160
HS, HD = 16, D // 16
HC = P // HD
SKIP = float(4 * EXPERTS * CAP)


def self_attention(nc, ins, scratch, gate, slot, z, ident):
    with ExitStack() as ctx:
        def sb(name, shape, dt=F32):
            return ctx.enter_context(nc.sbuf_tensor(name, shape, dt))

        def sem(name):
            return ctx.enter_context(nc.semaphore(name))

        w_self = sb("w_self", [P, 3, KC, D])
        w_f = sb("w_f", [P, KC, D])
        w_r = sb("w_r", [P, KC, EXPERTS])
        bq = sb("bq_col", [P, KC])
        bk = sb("bk_col", [P, KC])
        bv = sb("bv_col", [P, KC])
        bf = sb("bf_rows", [P, D])
        alibi = sb("alibi_tile", [P, RT, SQ])
        head_mask = sb("head_mask", [P, HC])
        upto = sb("upto", [P, P])
        ones = sb("ones", [P, P])
        rank = sb("rank", [P, EXPERTS])
        zero = sb("zero", [P, ZR * D])
        x1 = sb("x1_tile", [P, KC, D])
        x2 = sb("x2_tile", [P, KC, D])
        xb = sb("x1_plus_bias", [P, KC, D])
        xn = sb("xn1", [P, KC, D])
        xn2 = sb("xn2", [P, KC, D])
        half = sb("minus_half2", [P, KC, 1])
        stats = sb("stats1", [P, KC, 6])
        mv = sb("mean_var1", [P, KC, 2])
        rstd = sb("rstd1", [P, KC, 1])
        stats2 = sb("stats2", [P, KC, 6])
        mv2 = sb("mean_var2", [P, KC, 2])
        rstd2 = sb("rstd2", [P, KC, 1])
        xt = sb("xt", [P, KC, GT])
        xt2 = sb("xt2", [P, KC, GT])
        q_t = sb("q_t", [P, KC, GT])
        k_t = sb("k_t", [P, KC, GT])
        q_bd = sb("q_bd", [P, KC, GB, HC, SQ])
        v_bd = sb("v_bd", [P, KC, HR, KC, P])
        prob = sb("prob_self", [P, KC, HR * RT, SQ])
        negmax = sb("rowmax", [P, KC, HR * RT])
        rsum = sb("rsum", [P, KC, HR * RT])
        rinv = sb("rinv_self", [P, KC, HR * RT])
        p_t = sb("p_t", [P, KC, HR, P])
        o_t = sb("o_t", [P, KC, KC, HR, SQ])
        lmax = sb("lmax", [P, KC])
        nlmax = sb("nlmax", [P, KC])
        expl = sb("expl", [P, KC, EXPERTS])
        esum = sb("esum", [P, KC])
        cand = sb("cand", [P, KC, EXPERTS])
        best = sb("best", [P, KC])
        onehot = sb("onehot", [P, KC, EXPERTS])
        taken = sb("taken", [P, EXPERTS])
        place = sb("place", [P, KC, EXPERTS])
        pos = sb("pos", [P, KC])
        refused = sb("refused", [P, KC])
        slot_f = sb("slot_f", [P, KC])
        slot_s = sb("slot_s", [P, KC], I32)
        gate_r = sb("gate_r", [P, KC])
        kept = sb("kept", [P, KC])
        slot_g = sb("slot_g", [P, KC])

        bank = [ctx.enter_context(nc.psum_tensor(f"bank{i}", [P, 512], F32)) for i in range(8)]
        xt_b, q_b, k_b, v_b = bank[0:4]
        s_b, pt_b = bank[0:2], bank[4:6]
        o_b = (bank[6:8], bank[4:6])
        f_b, xt2_b, l_b, n_b = bank[6], bank[7], bank[7], bank[3]

        w_in, x_in, xb_in = sem("w2_in"), sem("x1_in"), sem("xb_in")
        set_up, wq_scaled, zeroed = sem("set_up"), sem("wq_scaled"), sem("zeroed")
        aggr_ok, var_ok, rstd_ok, xn_ok = (sem(f"ln1_{n}") for n in ("aggr", "var", "rstd", "xn"))
        aggr2_ok, var2_ok, rstd2_ok, xn2_ok = (sem(f"ln2_{n}") for n in ("aggr", "var", "rstd", "xn"))
        xt_full, xt_ok = sem("xt_full"), sem("xt_ok")
        q_full, k_full, v_full = sem("q_full"), sem("k_full"), sem("v_full")
        q_ok, k_ok = sem("q_ok"), sem("k_ok")
        qbd_act, qbd_dve, qbd_pool, vbd_act, vbd_dve = sem("qbd_act"), sem("qbd_dve"), sem("qbd_pool"), sem("vbd_act"), sem("vbd_dve")
        sc_full, biased, max_ok, sub_ok, exp_ok, sum_ok, inv_ok, prob_ok = (
            sem(n) for n in ("sc_full", "biased", "max_ok", "sub_ok", "exp_ok", "sum_ok", "inv_ok", "prob_ok"))
        pt_full, pt_ok, o_full = sem("pt2_full"), sem("pt2_ok"), sem("o_full")
        ot_act, ot_dve = sem("ot_act"), sem("ot_dve")
        f_full, xb_ok, x2_ok, z_ok = sem("f_full"), sem("xb_ok"), sem("x2_ok"), sem("z_ok")
        xt2_full, xt2_ok, l_full = sem("xt2_full"), sem("xt2_ok"), sem("l_full")
        step, late, passed = sem("step"), sem("late"), sem("passed2")
        route = sem("route")
        lexp_ok, onehot_ok, n_full, slot_ok, sent, sent_ok = sem("lexp_ok"), sem("onehot_ok"), sem("n_full"), sem("slot_ok"), sem("sent"), sem("sent_ok")
        block = ctx.enter_context(nc.Block())

        def v_block(b, r):
            to = v_bd[r * SQ:(r + 1) * SQ, :, b, r // 2, :].rearrange("p t (h n) -> p t h n", h=HR)
            src = v_b[b * SQ:(b + 1) * SQ, :].rearrange("p (t r h n) -> p t r h n", t=KC, r=RT, h=HR)
            return to[:, :, :, (r % 2) * HD:(r % 2 + 1) * HD], src[:, :, r]

        x1_rows = scratch["x1"].rearrange("(g c p) d -> g p c d", c=KC, p=P)
        HA = 5
        N_W = 7 + 6

        started = (x2_ok, xn_ok, z_ok, xn2_ok, sc_full, o_full, v_full, qbd_pool, qbd_dve, f_full, l_full, xt_full,
                   pt_full, sent_ok, xt2_full, lexp_ok, ot_dve, ot_act, xt2_ok, slot_ok)

        @block.sync
        def _(sp):
            for counter in started:
                sp.sem_inc(counter, 1)

            def load_x1(i):
                sp.wait_ge(xn_ok, 1 + i)
                sp.dma_start(x1[:, :, :], x1_rows[bass.ds(i, 1)].rearrange("g p c d -> p (g c) d")).then_inc(x_in, 16)

            def load_xb(i):
                sp.wait_ge(x2_ok, 1 + i * KC)
                sp.dma_start(xb[:, :, :], x1_rows[bass.ds(i, 1)].rearrange("g p c d -> p (g c) d")).then_inc(xb_in, 16)

            load_x1(0)
            load_xb(0)
            for i, name in enumerate(("s_wq", "s_wk", "s_wv")):
                sp.dma_start(w_self[:, i], ins[name].rearrange("(c p) n -> p c n", p=P)).then_inc(w_in, 16)
            sp.dma_start(bq[:, :], ins["s_bq"]).then_inc(w_in, 16)
            sp.dma_start(bk[:, :], ins["s_bk"]).then_inc(w_in, 16)
            sp.dma_start(bv[:, :], ins["s_bv"]).then_inc(w_in, 16)
            sp.dma_start(bf[:, :], ins["s_bf"].partition_broadcast(P)).then_inc(w_in, 16)
            load_x1(1)
            sp.wait_ge(set_up, 2)
            rows = scratch["buf"].rearrange("(a p j) d -> a p (j d)", p=P, j=ZR)
            for a in range(EXPERTS * CAP // (ZR * P)):
                sp.dma_start(rows[a], zero[:, :]).then_inc(zeroed, 16)
            with sp.Fori(0, G - 2) as i:
                load_x1(i + 2)
                load_xb(i + 1)
            load_xb(G - 1)

        @block.gpsimd
        def _(pool):
            def rstd_1(i):
                pool.wait_ge(var_ok, i + 1)
                pool.tensor_tensor(rstd[:, :, :], mv[:, :, 1:2], half[:, :, :], ALU.pow).then_inc(rstd_ok, 1)

            def spread_q(i):
                pool.wait_ge(q_ok, (i + 1) * KC)
                pool.wait_ge(sc_full, 1 + i * KC)
                to = [P, GB, HC - HA, SQ]
                pool.tensor_tensor(q_bd[:, 1, :, HA:HC, :], q_t[:, 1, :].rearrange("p (b q) -> p b q", b=GB).unsqueeze(2).broadcast_to(to),
                                   head_mask[:, HA:HC].unsqueeze(1).unsqueeze(3).broadcast_to(to), ALU.mult).then_inc(qbd_pool, 1)

            def add_bias(i):
                pool.wait_ge(xb_in, (i + 1) * 16)
                pool.tensor_tensor(xb[:, :, :], xb[:, :, :], bf[:, :].unsqueeze(1).broadcast_to([P, KC, D]), ALU.add).then_inc(xb_ok, 1)

            def scale_prob(i, t):
                pool.wait_ge(inv_ok, i * KC + t + 1)
                pool.tensor_tensor(prob[:, t], prob[:, t], rinv[:, t, :].unsqueeze(2).broadcast_to([P, HR * RT, SQ]), ALU.mult).then_inc(prob_ok, 1)

            def rstd_2(i):
                pool.wait_ge(var2_ok, i + 1)
                pool.tensor_tensor(rstd2[:, :, :], mv2[:, :, 1:2], half[:, :, :], ALU.pow).then_inc(rstd2_ok, 1)

            def sum_z(i):
                pool.wait_ge(xn2_ok, 1 + i + 1)
                pool.tensor_tensor(z[:, bass.ds(i * KC, KC), :], x2[:, :, :], xn2[:, :, :], ALU.add).then_inc(z_ok, 1)

            def scatter(i):
                pool.wait_ge(slot_ok, 1 + i + 1)
                pool.sem_inc(passed, 1)
                for t in range(KC):
                    pool.indirect_dma_start(out=scratch["buf"], out_offset=bass.IndirectOffsetOnAxis(ap=slot_s[:, t:t + 1], axis=0),
                                            in_=xn2[:, t, :], in_offset=None, bounds_check=EXPERTS * CAP - 1, oob_is_err=False).then_inc(sent, 16)
                pool.wait_ge(sent, (i + 1) * 16 * KC)
                pool.sem_inc(sent_ok, 1)

            pool.memset(half[:, :, :], -0.5).then_inc(set_up, 1)
            pool.memset(zero[:, :], 0.0).then_inc(set_up, 1)
            pool.wait_ge(set_up, 1)
            rstd_1(0)
            pool.memset(ones[:, :], 1.0).then_inc(set_up, 1)
            pool.memset(taken[:, :], 0.0).then_inc(set_up, 1)
            pool.memset(v_bd[:, :, :, :, :], 0.0).then_inc(set_up, 1)
            pool.wait_ge(w_in, 16 * N_W)
            pool.wait_ge(set_up, 5)
            def round(i, behind=True, ahead=2):
                if ahead > 0:
                    spread_q(i + 1)
                if behind:
                    scatter(i - 1)
                if ahead > 1:
                    rstd_1(i + 2)
                rstd_2(i)
                if ahead > 0:
                    scale_prob(i + 1, 0)
                sum_z(i)
                if ahead > 0:
                    add_bias(i + 1)
                    scale_prob(i + 1, 1)

            spread_q(0)
            rstd_1(1)
            add_bias(0)
            for t in range(KC):
                scale_prob(0, t)
            pool.wait_ge(zeroed, 16 * (EXPERTS * CAP // (ZR * P)))
            round(0, behind=False)
            with pool.Fori(1, G - 2) as i:
                round(i)
            round(G - 2, ahead=1)
            round(G - 1, ahead=0)
            scatter(G - 1)

        @block.scalar
        def _(act):
            def copy_xt(i):
                act.wait_ge(xt_full, 1 + i + 1)
                act.wait_ge(v_full, 1 + i)
                nc.scalar.activation(xt[:, :, :].rearrange("p c t -> p (c t)"), xt_b[:, :], ACT.Copy).then_inc(xt_ok, 1)

            def bias_q(i):
                act.wait_ge(q_full, i + 1)
                act.wait_ge(qbd_pool, 1 + i)
                act.wait_ge(qbd_dve, 1 + i)
                for c in range(KC):
                    nc.scalar.activation(q_t[:, c, :], q_b[:, c * GT:(c + 1) * GT], ACT.Identity, bias=bq[:, c:c + 1]).then_inc(q_ok, 1)

            def spread_q(i):
                act.wait_ge(q_ok, (i + 1) * KC)
                act.wait_ge(sc_full, 1 + i * KC)
                for h in range(HA):
                    op = nc.scalar.activation(q_bd[:, 1, :, h, :], q_t[:, 1, :].rearrange("p (b q) -> p b q", b=GB), ACT.Copy, scale=head_mask[:, h:h + 1])
                op.then_inc(qbd_act, 1)

            def bias_k(i):
                act.wait_ge(k_full, i + 1)
                act.wait_ge(sc_full, 1 + i * KC)
                for c in range(KC):
                    nc.scalar.activation(k_t[:, c, :], k_b[:, c * GT:(c + 1) * GT], ACT.Identity, bias=bk[:, c:c + 1]).then_inc(k_ok, 1)

            def spread_v(i):
                act.wait_ge(v_full, 1 + i + 1)
                act.wait_ge(o_full, 1 + i * KC)
                for b in (0, 1):
                    for r in range(RT):
                        op = nc.scalar.activation(*v_block(b, r), ACT.Copy)
                op.then_inc(vbd_act, 1)

            def exp_prob(i, t):
                act.wait_ge(sub_ok, i * KC + t + 1)
                nc.scalar.activation(prob[:, t], prob[:, t], ACT.Exp).then_inc(exp_ok, 1)

            def copy_pt(i, t):
                act.wait_ge(pt_full, 1 + i * KC + t + 1)
                act.wait_ge(o_full, 1 + i * KC)
                nc.scalar.activation(p_t[:, t].rearrange("p b n -> p (b n)"), pt_b[t][:, :], ACT.Copy).then_inc(pt_ok, 1)

            def take_o(i, t):
                act.wait_ge(o_full, 1 + i * KC + t + 1)
                act.wait_ge(f_full, 1 + i)
                for h in range(HR):
                    r = slice(h * SQ, (h + 1) * SQ)
                    op = nc.scalar.activation(o_t[r, 0, t], o_b[t][0][r, :].rearrange("p (b h q) -> p b h q", b=HR, h=HR)[:, :, h, :],
                                              ACT.Identity, bias=bv[r, 0:1])
                op.then_inc(ot_act, 1)

            def copy_xt2(i):
                act.wait_ge(xt2_full, 1 + i + 1)
                act.wait_ge(l_full, 1 + i)
                nc.scalar.activation(xt2[:, :, :].rearrange("p c t -> p (c t)"), xt2_b[:, :], ACT.Copy).then_inc(xt2_ok, 1)

            def exp_logits(i):
                act.wait_ge(route, i * 6 + 3)
                for t in range(KC):
                    op = nc.scalar.activation(expl[:, t, :], l_b[:, t * EXPERTS:(t + 1) * EXPERTS], ACT.Exp, bias=nlmax[:, t:t + 1], accum_out=esum[:, t:t + 1])
                op.then_inc(lexp_ok, 1)

            nc.scalar.dma_start(w_f[:, :, :], ins["s_wf"]).then_inc(w_in, 16)
            nc.scalar.dma_start(w_r[:, :, :], ins["w_router"].rearrange("(c p) n -> p c n", p=P)).then_inc(w_in, 16)
            for to, name in ((alibi[:, :, :], "alibi"), (head_mask[:, :], "head_mask"), (upto[:, :], "upto"), (rank[:, :], "rank")):
                nc.scalar.dma_start(to, ins[name]).then_inc(w_in, 16)
            act.wait_ge(w_in, 16 * N_W)
            nc.scalar.activation(w_self[:, 0], w_self[:, 0], ACT.Copy, scale=HD ** -0.5).then_inc(wq_scaled, 1)
            nc.scalar.activation(bq[:, :], bq[:, :], ACT.Copy, scale=HD ** -0.5).then_inc(wq_scaled, 1)
            act.wait_ge(wq_scaled, 2)
            copy_xt(0)
            bias_q(0)
            spread_q(0)
            bias_k(0)
            exp_prob(0, 0)
            spread_v(0)
            exp_prob(0, 1)
            copy_xt(1)

            def round(i, behind=True, ahead=2):
                copy_pt(i, 0)
                if ahead > 0:
                    bias_q(i + 1)
                if behind:
                    exp_logits(i - 1)
                if ahead > 0:
                    bias_k(i + 1)
                copy_pt(i, 1)
                if ahead > 0:
                    spread_q(i + 1)
                take_o(i, 0)
                take_o(i, 1)
                if ahead > 0:
                    exp_prob(i + 1, 0)
                    spread_v(i + 1)
                copy_xt2(i)
                if ahead > 1:
                    copy_xt(i + 2)
                if ahead > 0:
                    exp_prob(i + 1, 1)

            round(0, behind=False)
            with act.Fori(1, G - 2) as i:
                round(i)
            round(G - 2, ahead=1)
            round(G - 1, ahead=0)
            exp_logits(G - 1)

        @block.vector
        def _(dve):
            def stats_1(i):
                dve.wait_ge(x_in, (i + 1) * 16)
                for c in range(KC):
                    op = dve.bn_stats(stats[:, c, :], x1[:, c, :])
                dve.drain()
                for c in range(KC):
                    op = dve.bn_aggr(mv[:, c, :], stats[:, c, :])
                op.then_inc(aggr_ok, 1)
                dve.wait_ge(aggr_ok, i + 1)
                dve.tensor_scalar(mv[:, :, 1], mv[:, :, 1], EPS, None, ALU.add).then_inc(var_ok, 1)

            def norm_1(i):
                dve.wait_ge(rstd_ok, i + 1)
                dve.wait_ge(xt_full, 1 + i)
                for c in range(KC):
                    op = dve.tensor_scalar(xn[:, c, :], x1[:, c, :], mv[:, c, 0:1], rstd[:, c, :], ALU.subtract, ALU.mult)
                op.then_inc(xn_ok, 1)

            def spread_q(i):
                dve.wait_ge(q_ok, (i + 1) * KC)
                dve.wait_ge(sc_full, 1 + i * KC)
                for h in range(HC):
                    op = dve.tensor_scalar(q_bd[:, 0, :, h, :], q_t[:, 0, :].rearrange("p (b q) -> p b q", b=GB), head_mask[:, h:h + 1], None, ALU.mult)
                op.then_inc(qbd_dve, 1)

            def spread_v(i):
                dve.wait_ge(v_full, 1 + i + 1)
                dve.wait_ge(vbd_act, i + 1)
                dve.wait_ge(o_full, 1 + i * KC)
                for b in (2, 3):
                    for r in range(RT):
                        op = dve.tensor_copy(*v_block(b, r))
                op.then_inc(vbd_dve, 1)

            def shift_scores(i, t):
                dve.wait_ge(sc_full, 1 + i * KC + t + 1)
                dve.wait_ge(pt_full, 1 + i * KC)
                dve.tensor_tensor(prob[:, t].rearrange("p (b r) k -> p b (r k)", b=HR), s_b[t][:, :].rearrange("p (b n) -> p b n", b=HR),
                                  alibi[:, :, :].rearrange("p r k -> p (r k)").unsqueeze(1).broadcast_to([P, HR, RT * SQ]), ALU.add).then_inc(biased, 1)
                dve.wait_ge(biased, i * KC + t + 1)
                dve.tensor_reduce(negmax[:, t, :], prob[:, t], AX.X, ALU.max).then_inc(max_ok, 1)
                dve.wait_ge(max_ok, i * KC + t + 1)
                dve.tensor_tensor(prob[:, t], prob[:, t], negmax[:, t, :].unsqueeze(2).broadcast_to([P, HR * RT, SQ]), ALU.subtract).then_inc(sub_ok, 1)

            def sum_rows(i, t):
                dve.wait_ge(exp_ok, i * KC + t + 1)
                dve.tensor_reduce(rsum[:, t, :], prob[:, t], AX.X, ALU.add).then_inc(sum_ok, 1)
                dve.wait_ge(sum_ok, i * KC + t + 1)
                dve.reciprocal(rinv[:, t, :], rsum[:, t, :]).then_inc(inv_ok, 1)

            def take_o(i, t):
                dve.wait_ge(o_full, 1 + i * KC + t + 1)
                dve.wait_ge(f_full, 1 + i)
                for h in range(HR):
                    r = slice(h * SQ, (h + 1) * SQ)
                    op = dve.tensor_scalar(o_t[r, 1, t], o_b[t][1][r, :].rearrange("p (b h q) -> p b h q", b=HR, h=HR)[:, :, h, :],
                                           bv[r, 1:2], None, ALU.add)
                op.then_inc(ot_dve, 1)

            def stats_2(i):
                dve.wait_ge(f_full, 1 + i + 1)
                dve.wait_ge(xb_ok, i + 1)
                dve.wait_ge(z_ok, 1 + i)
                for t in range(KC):
                    dve.tensor_tensor(x2[:, t, :], f_b[:, t * D:(t + 1) * D], xb[:, t, :], ALU.add).then_inc(x2_ok, 1)
                dve.wait_ge(x2_ok, 1 + (i + 1) * KC)
                for c in range(KC):
                    op = dve.bn_stats(stats2[:, c, :], x2[:, c, :])
                dve.drain()
                for c in range(KC):
                    op = dve.bn_aggr(mv2[:, c, :], stats2[:, c, :])
                op.then_inc(aggr2_ok, 1)
                dve.wait_ge(aggr2_ok, i + 1)
                dve.tensor_scalar(mv2[:, :, 1], mv2[:, :, 1], EPS, None, ALU.add).then_inc(var2_ok, 1)

            def norm_2(i):
                dve.wait_ge(rstd2_ok, i + 1)
                dve.wait_ge(z_ok, 1 + i)
                dve.wait_ge(xt2_full, 1 + i)
                dve.wait_ge(sent_ok, 1 + i)
                for c in range(KC):
                    op = dve.tensor_scalar(xn2[:, c, :], x2[:, c, :], mv2[:, c, 0:1], rstd2[:, c, :], ALU.subtract, ALU.mult)
                op.then_inc(xn2_ok, 1)

            def choose(i):
                logits = l_b[:, 0:KC * EXPERTS].rearrange("p (t e) -> p t e", t=KC)
                dve.wait_ge(l_full, 1 + i + 1)
                dve.wait_ge(lexp_ok, 1 + i)
                dve.tensor_reduce(lmax[:, :], logits, AX.X, ALU.max).then_inc(route, 1)
                dve.tensor_reduce(nlmax[:, :], logits, AX.X, ALU.max, negate=True).then_inc(route, 1)
                dve.wait_ge(route, i * 6 + 2)
                for t in range(KC):
                    op = dve.scalar_tensor_tensor(out=cand[:, t, :], in0=logits[:, t, :], scalar=lmax[:, t:t + 1], in1=rank[:, :], op0=ALU.is_ge, op1=ALU.mult)
                op.then_inc(route, 1)
                dve.wait_ge(route, i * 6 + 3)
                dve.tensor_reduce(best[:, :], cand[:, :, :], AX.X, ALU.max).then_inc(route, 1)
                dve.wait_ge(route, i * 6 + 4)
                for t in range(KC):
                    op = dve.tensor_scalar(onehot[:, t, :], rank[:, :], best[:, t:t + 1], None, ALU.is_equal)
                op.then_inc(onehot_ok, 1)

            def give_slots(i):
                dve.wait_ge(n_full, i + 1)
                for t in range(KC):
                    dve.tensor_tensor(place[:, t, :], n_b[:, t * EXPERTS:(t + 1) * EXPERTS], taken[:, :], ALU.add).then_inc(step, 1)
                    dve.wait_ge(step, i * 4 + 2 * t + 1)
                    dve.tensor_tensor(taken[:, :], n_b[:, (KC + t) * EXPERTS:(KC + t + 1) * EXPERTS], taken[:, :], ALU.add).then_inc(step, 1)
                    dve.wait_ge(step, i * 4 + 2 * t + 2)
                dve.tensor_tensor(place[:, :, :], place[:, :, :], onehot[:, :, :], ALU.mult).then_inc(route, 1)
                dve.wait_ge(route, i * 6 + 5)
                dve.tensor_reduce(pos[:, :], place[:, :, :], AX.X, ALU.add).then_inc(route, 1)
                dve.wait_ge(route, i * 6 + 6)
                dve.tensor_scalar(refused[:, :], pos[:, :], float(CAP), SKIP, ALU.is_gt, ALU.mult).then_inc(late, 1)
                dve.tensor_scalar(kept[:, :], pos[:, :], float(CAP), None, ALU.is_le).then_inc(late, 1)
                dve.tensor_scalar(slot_f[:, :], best[:, :], -float(CAP), float(EXPERTS * CAP - 1), ALU.mult, ALU.add).then_inc(late, 1)
                dve.wait_ge(late, i * 8 + 3)
                dve.tensor_tensor(slot_f[:, :], slot_f[:, :], pos[:, :], ALU.add).then_inc(late, 1)
                dve.wait_ge(late, i * 8 + 4)
                dve.tensor_tensor(slot_f[:, :], slot_f[:, :], refused[:, :], ALU.add).then_inc(late, 1)
                dve.wait_ge(late, i * 8 + 5)
                dve.wait_ge(sent_ok, 1 + i)
                dve.tensor_copy(slot_s[:, :], slot_f[:, :]).then_inc(slot_ok, 1)
                dve.tensor_scalar(slot_g[:, :], slot_f[:, :], float(EXPERTS * CAP - 1), None, ALU.min).then_inc(late, 1)
                dve.wait_ge(lexp_ok, 1 + i + 1)
                dve.reciprocal(gate_r[:, :], esum[:, :]).then_inc(late, 1)
                dve.wait_ge(late, i * 8 + 7)
                dve.tensor_copy(slot[:, bass.ds(i * KC, KC)], slot_g[:, :])
                dve.tensor_tensor(gate[:, bass.ds(i * KC, KC)], gate_r[:, :], kept[:, :], ALU.mult).then_inc(late, 1)

            stats_1(0)
            norm_1(0)
            dve.wait_ge(w_in, 16 * N_W)
            dve.wait_ge(set_up, 5)
            spread_q(0)
            stats_1(1)
            norm_1(1)
            shift_scores(0, 0)
            spread_v(0)
            shift_scores(0, 1)
            for t in range(KC):
                sum_rows(0, t)

            def round(i, behind=True, ahead=2):
                if ahead > 0:
                    spread_q(i + 1)
                if behind:
                    give_slots(i - 1)
                take_o(i, 0)
                take_o(i, 1)
                if ahead > 1:
                    stats_1(i + 2)
                if ahead > 0:
                    shift_scores(i + 1, 0)
                if ahead > 1:
                    norm_1(i + 2)
                stats_2(i)
                if ahead > 0:
                    sum_rows(i + 1, 0)
                norm_2(i)
                if ahead > 0:
                    shift_scores(i + 1, 1)
                    spread_v(i + 1)
                    sum_rows(i + 1, 1)
                choose(i)

            round(0, behind=False)
            with dve.Fori(1, G - 2) as i:
                round(i)
            round(G - 2, ahead=1)
            round(G - 1, ahead=0)
            give_slots(G - 1)

        @block.tensor
        def _(pe):
            def turn(out, x):
                for c in range(KC):
                    for t in range(KC):
                        mm = pe.transpose(out[:, c * GT + t * P:c * GT + (t + 1) * P], x[:, t, c * P:(c + 1) * P], ident[:, :])
                return mm

            def turn_1(i):
                pe.wait_ge(xn_ok, 1 + i + 1)
                turn(xt_b, xn).then_inc(xt_full, 1)

            def project(i, w, out, done):
                pe.wait_ge(xt_ok, i + 1)
                for c in range(KC):
                    for kc in range(KC):
                        mm = pe.matmul(out[:, c * GT:(c + 1) * GT], w_self[:, w, kc, c * P:(c + 1) * P], xt[:, kc, :], start=(kc == 0), stop=(kc == KC - 1))
                mm.then_inc(done, 1)

            def values(i, t):
                for kc in range(KC):
                    mm = pe.matmul(v_b[:, t * D:(t + 1) * D], xt[:, kc, t * P:(t + 1) * P], w_self[:, 2, kc, :], start=(kc == 0), stop=(kc == KC - 1))
                if t == KC - 1:
                    mm.then_inc(v_full, 1)

            def scores(i, t, batches):
                pe.wait_ge(k_ok, (i + 1) * KC)
                pe.wait_ge(qbd_dve, 1 + i + 1)
                pe.wait_ge(qbd_act, i + 1)
                pe.wait_ge(qbd_pool, 1 + i + 1)
                for b in batches:
                    for r in range(RT):
                        at = (b * RT + r) * SQ
                        g = t * HR + b
                        mm = pe.matmul(s_b[t][:, at:at + SQ], q_bd[:, r // 2, g, HR * (r % 2):HR * (r % 2 + 1), :].rearrange("p h q -> p (h q)"),
                                       k_t[:, r // 2, g * SQ:(g + 1) * SQ], start=True, stop=True)
                if b == HR - 1:
                    mm.then_inc(sc_full, 1)

            def turn_prob(i, t):
                pe.wait_ge(prob_ok, i * KC + t + 1)
                for b in range(HR):
                    mm = pe.transpose(pt_b[t][:, b * P:(b + 1) * P], prob[:, t, b * RT:(b + 1) * RT, :].rearrange("p r k -> p (r k)"), ident[:, :])
                mm.then_inc(pt_full, 1)

            def mix(i, t):
                pe.wait_ge(x2_ok, 1 + i * KC)
                pe.wait_ge(lexp_ok, 1 + i)
                pe.wait_ge(vbd_act, i + 1)
                pe.wait_ge(vbd_dve, i + 1)
                pe.wait_ge(pt_ok, i * KC + t + 1)
                for u in range(KC):
                    for b in range(HR):
                        mm = pe.matmul(o_b[t][u][:, b * P:(b + 1) * P], v_bd[:, t, b, u, :], p_t[:, t, b, :], start=True, stop=True)
                mm.then_inc(o_full, 1)

            def out_project(i):
                pe.wait_ge(ot_act, 1 + (i + 1) * KC)
                pe.wait_ge(ot_dve, 1 + (i + 1) * KC)
                for t in range(KC):
                    for u in range(KC):
                        mm = pe.matmul(f_b[:, t * D:(t + 1) * D], o_t[:, u, t].rearrange("p b q -> p (b q)"), w_f[:, u, :], start=(u == 0), stop=(u == KC - 1))
                mm.then_inc(f_full, 1)

            def turn_2(i):
                pe.wait_ge(xn2_ok, 1 + i + 1)
                turn(xt2_b, xn2).then_inc(xt2_full, 1)

            def router(i):
                pe.wait_ge(xt2_ok, 1 + i + 1)
                for t in range(KC):
                    for kc in range(KC):
                        mm = pe.matmul(l_b[:, t * EXPERTS:(t + 1) * EXPERTS], xt2[:, kc, t * P:(t + 1) * P], w_r[:, kc, :], start=(kc == 0), stop=(kc == KC - 1))
                mm.then_inc(l_full, 1)

            def count(i):
                pe.wait_ge(onehot_ok, i + 1)
                pe.wait_ge(vbd_dve, i + 1)
                pe.wait_ge(vbd_act, i + 1)
                for j, w in enumerate((upto, ones)):
                    for t in range(KC):
                        at = (j * KC + t) * EXPERTS
                        mm = pe.matmul(n_b[:, at:at + EXPERTS], w[:, :], onehot[:, t, :], start=True, stop=True)
                mm.then_inc(n_full, 1)

            turn_1(0)
            pe.wait_ge(w_in, 16 * N_W)
            pe.wait_ge(set_up, 5)
            pe.wait_ge(wq_scaled, 2)
            project(0, 0, q_b, q_full)
            project(0, 1, k_b, k_full)
            scores(0, 0, (0, 1))
            values(0, 0)
            scores(0, 0, (2, 3))
            values(0, 1)
            scores(0, 1, range(HR))

            def round(i, behind=True, ahead=2):
                turn_prob(i, 0)
                if ahead:
                    pe.wait_ge(biased, (i + 1) * KC)
                    project(i + 1, 0, q_b, q_full)
                if ahead:
                    project(i + 1, 1, k_b, k_full)
                turn_prob(i, 1)
                if behind:
                    count(i - 1)
                mix(i, 0)
                mix(i, 1)
                if ahead:
                    scores(i + 1, 0, (0, 1))
                    pe.wait_ge(slot_ok, 1 + i)
                    values(i + 1, 0)
                    scores(i + 1, 0, (2, 3))
                out_project(i)
                if ahead:
                    scores(i + 1, 1, (0, 1))
                    values(i + 1, 1)
                    scores(i + 1, 1, (2, 3))
                turn_2(i)
                if ahead > 1:
                    turn_1(i + 2)
                router(i)

            pe.wait_ge(biased, 1)
            turn_1(1)
            round(0, behind=False)
            with pe.Fori(1, G - 2) as i:
                round(i)
            round(G - 2, ahead=1)
            round(G - 1, ahead=0)
            count(G - 1)


def experts(nc, ins, scratch, gate, slot, z, ident, out):
    with ExitStack() as ctx:
        def sb(name, shape, dt=F32):
            return ctx.enter_context(nc.sbuf_tensor(name, shape, dt))

        def sem(name):
            return ctx.enter_context(nc.semaphore(name))

        NS = 4
        JR = 2
        PR = CAP // JR
        w = [sb(f"w_expert{n}", [P, NS, KC, D]) for n in range(3)]
        rows = sb("rows", [PR, NS, JR, D])
        bt = sb("bt", [P, NS, KC, CAP])
        ex = sb("ex", [P, NS, KC, CAP])
        act_t = sb("act_t", [P, NS, KC, CAP])
        y = sb("y", [PR, NS, JR, D])
        NG = 4
        TG = 4
        yt = sb("y_rows", [P, NG, TG, D])
        idx = sb("idx", [P, NG, TG], I32)
        gcol = sb("gcol", [P, NG, TG])
        idx_ok, gc_ok, passed = sem("idx_ok"), sem("gc_ok"), sem("passed3")
        bank = [ctx.enter_context(nc.psum_tensor(f"ebank{i}", [P, 512], F32)) for i in range(8)]
        bt_b, g_b, u_b, y_b = bank[0:2], bank[2:4], bank[4:6], bank[6:8]
        w_in = [sem(f"we_in{s}") for s in range(NS)]
        r_in = [sem(f"rows_in{s}") for s in range(NS)]
        y_out = [sem(f"y_out{s}") for s in range(NS)]
        y_in = [sem(f"yr_in{s}") for s in range(NG)]
        o_out = sem("o_out")
        bt_full, bt_ok, gu_full, ex_ok, plus, inv, gate_ok, act_ok, y_full, y_ok, o_ok = (
            sem(n) for n in ("bt_full", "bt_ok", "gu_full", "ex_ok", "plus", "inv", "gated", "act_ok", "y_full", "y_ok", "o_ok"))
        block = ctx.enter_context(nc.Block())
        NR = EXPERTS // NS
        NT = T // P // TG
        o_tiles = out.rearrange("(g b) s d -> g (b s) d", g=G).rearrange("(n k) (c p) d -> n p k c d", p=P, k=TG // KC)
        buf = scratch["buf"].rearrange("(e p j) d -> e p (j d)", p=PR, j=JR)
        yd = scratch["y"].rearrange("(e p j) d -> e p (j d)", p=PR, j=JR)

        started = y_out

        @block.sync
        def _(sp):
            for counter in started:
                sp.sem_inc(counter, 1)
            sp.sem_inc(y_full, NS)
            sp.sem_inc(y_ok, 2)
            sp.sem_inc(o_ok, NG)
            with sp.Fori(0, NR) as i:
                for s in range(NS):
                    e = i * NS + s
                    sp.wait_ge(y_full, e + 1)
                    sp.dma_start(rows[:, s].rearrange("p j d -> p (j d)"), buf[bass.ds(e, 1)].rearrange("e p n -> (e p) n")).then_inc(r_in[s], 16)
                    for n, name in enumerate(("w_gate", "w_up", "w_down")):
                        sp.dma_start(w[n][:, s].rearrange("p c n -> p (c n)"),
                                     ins[name][bass.ds(e, 1)].rearrange("e (p c) n -> (e p) (c n)", c=KC)).then_inc(w_in[s], 16)
            with sp.Fori(0, NT) as n:
                sp.wait_ge(o_ok, NG + n + 1)
                sp.dma_start(o_tiles[bass.ds(n, 1)].rearrange("n p k c d -> p (n k c) d"), z[:, bass.ds(n * TG, TG), :]).then_inc(o_out, 16)
            sp.wait_ge(o_out, 16 * NT)

        @block.gpsimd
        def _(pool):
            for s in range(NS):
                pool.wait_ge(y_out[s], 1 + 16 * NR)
            with pool.Fori(0, NT // NG) as i:
                for s in range(NG):
                    n = i * NG + s
                    pool.wait_ge(o_ok, n + 1)
                    pool.tensor_copy(idx[:, s, :], slot[:, bass.ds(n * TG, TG)]).then_inc(idx_ok, 1)
                    pool.wait_ge(idx_ok, n + 1)
                    pool.sem_inc(passed, 1)
                    for t in range(TG):
                        pool.indirect_dma_start(out=yt[:, s, t, :], out_offset=None, in_=scratch["y"],
                                                in_offset=bass.IndirectOffsetOnAxis(ap=idx[:, s, t:t + 1], axis=0),
                                                bounds_check=EXPERTS * CAP - 1, oob_is_err=False).then_inc(y_in[s], 16)

        @block.scalar
        def _(act):
            def copy_rows(e, s):
                act.wait_ge(bt_full, e + 1)
                nc.scalar.activation(bt[:, s].rearrange("p c n -> p (c n)"), bt_b[s % 2][:, 0:KC * CAP], ACT.Copy).then_inc(bt_ok, 1)

            def exp_gate(e, s):
                act.wait_ge(gu_full, e + 1)
                nc.scalar.activation(ex[:, s].rearrange("p c n -> p (c n)"), g_b[s % 2][:, 0:KC * CAP], ACT.Exp, scale=-1.0).then_inc(ex_ok, 1)

            def store_y(e, s, round):
                act.wait_ge(y_full, NS + e + 1)
                act.wait_ge(y_out[s], 1 + round * 16)
                nc.scalar.activation(y[:, s].rearrange("p j d -> p (j d)"), y_b[s % 2][0:PR, :], ACT.Copy).then_inc(y_ok, 1)
                act.wait_ge(y_ok, 2 + e + 1)
                nc.scalar.dma_start(yd[bass.ds(e, 1)].rearrange("e p n -> (e p) n"), y[:, s].rearrange("p j d -> p (j d)")).then_inc(y_out[s], 16)

            copy_rows(0, 0)
            copy_rows(1, 1)
            exp_gate(0, 0)
            copy_rows(2, 2)
            exp_gate(1, 1)
            with act.Fori(0, NR - 1) as i:
                for s in range(NS):
                    e = i * NS + s
                    store_y(e, s, i)
                    copy_rows(e + 3, (s + 3) % NS)
                    exp_gate(e + 2, (s + 2) % NS)
            for s in range(NS):
                e = EXPERTS - NS + s
                store_y(e, s, NR - 1)
                if e + 3 < EXPERTS:
                    copy_rows(e + 3, (s + 3) % NS)
                if e + 2 < EXPERTS:
                    exp_gate(e + 2, (s + 2) % NS)

        @block.vector
        def _(dve):
            with dve.Fori(0, NR) as i:
                for s in range(NS):
                    e = i * NS + s
                    dve.wait_ge(ex_ok, e + 1)
                    dve.tensor_scalar(ex[:, s], ex[:, s], 1.0, None, ALU.add).then_inc(plus, 1)
                    dve.wait_ge(plus, e + 1)
                    dve.reciprocal(ex[:, s], ex[:, s]).then_inc(inv, 1)
                    dve.wait_ge(inv, e + 1)
                    dve.tensor_tensor(ex[:, s], g_b[s % 2][:, 0:KC * CAP].rearrange("p (c n) -> p c n", c=KC), ex[:, s], ALU.mult).then_inc(gate_ok, 1)
                    dve.wait_ge(gate_ok, e + 1)
                    dve.wait_ge(y_full, e + 1)
                    dve.tensor_tensor(act_t[:, s], u_b[s % 2][:, 0:KC * CAP].rearrange("p (c n) -> p c n", c=KC), ex[:, s], ALU.mult).then_inc(act_ok, 1)
            with dve.Fori(0, NT // NG) as i:
                for s in range(NG):
                    n = i * NG + s
                    dve.tensor_copy(gcol[:, s, :], gate[:, bass.ds(n * TG, TG)]).then_inc(gc_ok, 1)
                    dve.wait_ge(gc_ok, n + 1)
                    dve.wait_ge(y_in[s], (i + 1) * 16 * TG)
                    for t in range(TG):
                        at = bass.ds(n * TG + t, 1)
                        op = dve.scalar_tensor_tensor(out=z[:, at, :].rearrange("p t d -> p (t d)"), in0=yt[:, s, t, :], scalar=gcol[:, s, t:t + 1],
                                                      in1=z[:, at, :].rearrange("p t d -> p (t d)"), op0=ALU.mult, op1=ALU.add)
                    op.then_inc(o_ok, 1)

        @block.tensor
        def _(pe):
            def turn(e, s, round):
                pe.wait_ge(r_in[s], round * 16)
                for c in range(KC):
                    for j in range(JR):
                        at = c * CAP + j * PR
                        mm = pe.transpose(bt_b[s % 2][:, at:at + PR], rows[:, s, j, c:D:KC], ident[0:PR, 0:PR])
                mm.then_inc(bt_full, 1)

            def gate_up(e, s, round):
                pe.wait_ge(w_in[s], round * 48)
                pe.wait_ge(bt_ok, e + 1)
                for n, b in ((0, g_b), (1, u_b)):
                    for f in range(KC):
                        for c in range(KC):
                            mm = pe.matmul(b[s % 2][:, f * CAP:(f + 1) * CAP], w[n][:, s, c, f:D:KC], bt[:, s, c, :], start=(c == 0), stop=(c == KC - 1))
                mm.then_inc(gu_full, 1)

            def down(e, s):
                pe.wait_ge(act_ok, e + 1)
                pe.wait_ge(y_ok, e + 1)
                for j in range(JR):
                    for f in range(KC):
                        mm = pe.matmul(y_b[s % 2][0:PR, j * D:(j + 1) * D], act_t[:, s, f, j * PR:(j + 1) * PR], w[2][:, s, f, :], start=(f == 0), stop=(f == KC - 1))
                mm.then_inc(y_full, 1)

            turn(0, 0, 1)
            turn(1, 1, 1)
            gate_up(0, 0, 1)
            turn(2, 2, 1)
            gate_up(1, 1, 1)
            with pe.Fori(0, NR - 1) as i:
                for s in range(NS):
                    e = i * NS + s
                    down(e, s)
                    turn(e + 3, (s + 3) % NS, i + 1 + (s + 3) // NS)
                    gate_up(e + 2, (s + 2) % NS, i + 1 + (s + 2) // NS)
            for s in range(NS):
                e = EXPERTS - NS + s
                down(e, s)
                if e + 3 < EXPERTS:
                    turn(e + 3, (s + 3) % NS, NR)
                if e + 2 < EXPERTS:
                    gate_up(e + 2, (s + 2) % NS, NR)


def cross_weights(nc, ctx):
    def sb(name, shape, dt=F32R):
        return ctx.enter_context(nc.sbuf_tensor(name, shape, dt))

    return dict(wq=sb("w_q", [P, 2, KC * H * DK]), wkt=sb("w_kt", [P, 2, NP, D]), wv=sb("w_v", [P, 2, KC * H * DK]),
                wo=sb("w_o", [P, 2, NP * D]), cxt=sb("c_last_t", [P, 2, KC, NB]),
                xnt=sb("x_norm_t", [P, 2, KC, GT]),
                half=sb("minus_half", [P, KC, 1], F32))


def constants():
    row = np.arange(NX)
    h4, q = np.divmod(np.arange(P), SQ)
    head = HR * np.arange(RT)[None, :] + h4[:, None]
    half = HS // 2
    base = np.float32(24.0 ** (1.0 / half))
    slopes = (np.float32(1.0) / base ** np.arange(1, half + 1, dtype=np.float32)).astype(np.float32)
    rel = (np.arange(SQ)[None, :] - q[:, None]).astype(np.float32)[:, None, :]
    slope = slopes[head % half][:, :, None]
    far = np.float32(-1e9)
    alibi = np.where((head < half)[:, :, None], np.where(rel <= 0, slope * rel, far), np.where(rel >= 0, -slope * rel, far))
    return {"ident": np.eye(P, dtype=np.float32),
            "mask": (row[:, None] % RT == np.arange(RT)[None, :]).astype(np.float32),
            "alibi": alibi.astype(np.float32),
            "head_mask": (np.arange(P)[:, None] // HD == np.arange(HC)[None, :]).astype(np.float32),
            "upto": np.triu(np.ones((P, P), np.float32)),
            "rank": np.tile(EXPERTS - np.arange(EXPERTS, dtype=np.float32), (P, 1))}


def perceiver(nc, ins, out):
    scratch = {"cx": nc.dram_tensor("cx_d", (2, NB, D), F32, kind="Internal").ap(),
               "x1": nc.dram_tensor("x1_d", (T, D), F32, kind="Internal").ap(),
               "buf": nc.dram_tensor("buf_d", (EXPERTS * CAP, D), F32, kind="Internal").ap(),
               "y": nc.dram_tensor("y_d", (EXPERTS * CAP, D), F32, kind="Internal").ap()}
    with ExitStack() as ctx:
        ident = ctx.enter_context(nc.sbuf_tensor("identity", [P, P], F32))
        gate = ctx.enter_context(nc.sbuf_tensor("gate", [P, T // P], F32))
        slot = ctx.enter_context(nc.sbuf_tensor("slot", [P, T // P], I32))
        with ExitStack() as first:
            weights = cross_weights(nc, first)
            prepare(nc, ins, scratch=scratch, ident=ident, **weights)
            cross_attention(nc, ins, scratch=scratch, ident=ident, **weights)
        z = ctx.enter_context(nc.sbuf_tensor("z_tiles", [P, T // P, D], F32))
        self_attention(nc, ins, scratch, gate, slot, z, ident)
        experts(nc, ins, scratch, gate, slot, z, ident, out)


def order_weights(arrays):
    out = dict(arrays)
    for name in ("wq", "wk", "wv"):
        out[name] = np.ascontiguousarray(arrays[name].reshape(H, KC, P, DK).transpose(2, 1, 0, 3).reshape(P, KC * H * DK))
    for name in ("s_bq", "s_bk"):
        out[name] = np.ascontiguousarray(arrays[name].reshape(KC, P).T)
    out["s_wf"] = np.ascontiguousarray(arrays["s_wf"].reshape(KC, 2, HR, HD, D).transpose(2, 1, 3, 0, 4).reshape(P, KC, D))
    out["s_bv"] = np.ascontiguousarray(arrays["s_bv"].reshape(KC, 2, HR, HD).transpose(2, 1, 3, 0).reshape(P, KC))
    return out


NAMES = {"x": "x", "ctx_1024": "ctx", "L0_xattn_W_Q": "wq", "L0_xattn_W_K": "wk", "L0_xattn_W_V": "wv", "L0_xattn_W_O": "wo",
         "L0_attn_Wq": "s_wq", "L0_attn_bq": "s_bq", "L0_attn_Wk": "s_wk", "L0_attn_bk": "s_bk", "L0_attn_Wv": "s_wv",
         "L0_attn_bv": "s_bv", "L0_attn_Wf": "s_wf", "L0_attn_bf": "s_bf", "L0_ffn_w_router": "w_router",
         "L0_ffn_w_gate": "w_gate", "L0_ffn_w_up": "w_up", "L0_ffn_w_down": "w_down"}


def kernel(**inputs):
    import concourse.bacc as bacc
    from concourse.bass_utils import run_bass_kernel_spmd

    nc = bacc.Bacc("TRN2", target_bir_lowering=False, num_devices=1)
    arrays = order_weights({NAMES[name]: np.ascontiguousarray(inputs[name]) for name in NAMES})
    arrays.update(constants())
    ins = {name: nc.dram_tensor(f"in_{name}", a.shape, mybir.dt.from_np(a.dtype), kind="ExternalInput").ap()
           for name, a in arrays.items()}
    out = nc.dram_tensor("out", (NB, SQ, D), F32, kind="ExternalOutput").ap()
    perceiver(nc, ins, out)
    r = run_bass_kernel_spmd(nc, [{f"in_{name}": a for name, a in arrays.items()}], core_ids=[0])
    return r.results[0]["out"]
```
